# Optimizing a Trainium2 kernel written in Bass

```python
import numpy as np
import jax
import jax.numpy as jnp

def _softmax(x, axis=-1):
    return jax.nn.softmax(x, axis=axis)

def _gelu(x):
    return jax.nn.gelu(x, approximate=True)

def _silu(x):
    return jax.nn.silu(x)

def _sigmoid(x):
    return jax.nn.sigmoid(x)

def _layernorm(x, axis=-1, eps=1e-05):
    m = jnp.mean(x, axis=axis, keepdims=True)
    v = jnp.var(x, axis=axis, keepdims=True)
    return (x - m) / jnp.sqrt(v + eps)

def _scatter_add(tgt, idx, src, axis=0):
    return tgt.at[idx].add(src)

def _segment_sum(src, seg, n):
    return jax.ops.segment_sum(src, seg, n)
kernel_name = 'mk_xattn_ffn_d2_seqx_r4_52b75c'

def setup_inputs(seed: int=0):
    np.random.seed(seed)
    _w = jnp.asarray

    def _rec_inputs():
        import jax
        import jax.numpy as jnp
        _rk = jax.random.key(seed)
        x = 7.22e-05 + 1 * jax.random.normal(jax.random.fold_in(_rk, 1), (4, 1024, 256), jnp.float32)
        _lenS = 1024 - jax.random.randint(jax.random.fold_in(_rk, 7), (4,), 0, max(1, 1024 // 4) + 1, jnp.int32)
        _lenS2 = 77 - jax.random.randint(jax.random.fold_in(_rk, 8), (4,), 0, max(1, 77 // 4) + 1, jnp.int32)
        _ctx_1024P = jax.random.normal(jax.random.fold_in(_rk, 11), (4, 16, 256), jnp.float32)
        _ctx_1024c = jax.random.dirichlet(jax.random.fold_in(_rk, 511), 0.3 * jnp.ones((16,), jnp.float32), (4, 77))
        _ctx_1024t = jnp.einsum('bsk,bkd->bsd', _ctx_1024c, _ctx_1024P)
        _ctx_1024t = _ctx_1024t * jax.lax.rsqrt(jnp.mean(jnp.square(_ctx_1024t)) + 1e-12) * 0.953939
        ctx_1024 = 4.13588e-05 + 0.999923 * (_ctx_1024t + 0.3 * jax.random.normal(jax.random.fold_in(_rk, 611), (4, 77, 256), jnp.float32))
        _validS = jnp.arange(1024)[None, :] < _lenS[:, None]
        _validS2 = jnp.arange(77)[None, :] < _lenS2[:, None]
        _causal = jnp.tril(jnp.ones((1024, 1024), dtype=bool))
        mask_Bx1xSxS2_ik0 = jnp.where(jnp.broadcast_to(_validS2[:, None, None, :], (4, 1, 1024, 77)), 0, 1).astype(jnp.int32)
        return (x, ctx_1024, mask_Bx1xSxS2_ik0)
    x, ctx_1024, mask_Bx1xSxS2_ik0 = _rec_inputs()

    def _L0_xattn_setup():
        import jax, jax.numpy as jnp
        import numpy as np
        D_MODEL = 256
        NUM_HEADS = 16
        D_K = D_MODEL // NUM_HEADS

        def _split_heads(x):
            B, S, _ = x.shape
            return x.reshape(B, S, NUM_HEADS, D_K).transpose(0, 2, 1, 3)
        key = jax.random.key(seed)
        k1, k2, k3, kq, kk, kv, ko = jax.random.split(key, 7)
        B, S = (4, 512)
        scale = 1.0 / np.sqrt(D_MODEL)
        return {'Q_in': jax.random.normal(k1, (B, S, D_MODEL), dtype=jnp.float32), 'K_in': jax.random.normal(k2, (B, S, D_MODEL), dtype=jnp.float32), 'V_in': jax.random.normal(k3, (B, S, D_MODEL), dtype=jnp.float32), 'W_q': jax.random.normal(kq, (D_MODEL, D_MODEL), dtype=jnp.float32) * scale, 'W_k': jax.random.normal(kk, (D_MODEL, D_MODEL), dtype=jnp.float32) * scale, 'W_v': jax.random.normal(kv, (D_MODEL, D_MODEL), dtype=jnp.float32) * scale, 'W_o': jax.random.normal(ko, (D_MODEL, D_MODEL), dtype=jnp.float32) * scale}
    _L0_xattn_all = _L0_xattn_setup()
    _L0_xattn_in = {k: v for k, v in _L0_xattn_all.items() if k in ('W_q', 'W_k', 'W_v', 'W_o')}
    del _L0_xattn_all

    def _L0_ffn_setup():
        import jax, jax.numpy as jnp
        import numpy as np
        B, T, D = (2, 256, 256)
        H, DK, K = (8, 128, 8)
        NKEYS = 64
        NEXP = NKEYS * NKEYS

        def _rmsnorm(x, w, eps=1e-06):
            inv = jax.lax.rsqrt(jnp.mean(x * x, axis=-1, keepdims=True) + eps)
            return x * inv * w
        key = jax.random.key(seed)
        ks = jax.random.split(key, 5)
        return {'x': jax.random.normal(ks[0], (B, T, D), jnp.float32), 'w_q': jax.random.normal(ks[1], (H * 2 * DK, D), jnp.float32) * 0.02, 'keys': jax.random.normal(ks[2], (H, NKEYS, 2, DK), jnp.float32) * 0.02, 'expert_down': jax.random.normal(ks[3], (NEXP, D), jnp.float32) * 0.02, 'expert_up': jax.random.normal(ks[4], (NEXP, D), jnp.float32) * 0.02, 'norm_w': jnp.ones((D,), jnp.float32)}
    _L0_ffn_all = _L0_ffn_setup()
    _L0_ffn_in = {k: v for k, v in _L0_ffn_all.items() if k in ('w_q', 'keys', 'expert_down', 'expert_up', 'norm_w')}
    del _L0_ffn_all

    def _L1_xattn_setup():
        import jax, jax.numpy as jnp
        import numpy as np
        D_MODEL = 256
        N_HEADS = 16
        D_K = D_MODEL // N_HEADS
        B, S = (2, 512)

        def _rope_emb(seq_len, d_k):
            inv_freq = 1.0 / 10000.0 ** (jnp.arange(0, d_k, 2, dtype=jnp.float32) / d_k)
            t = jnp.arange(seq_len, dtype=jnp.float32)
            freqs = jnp.outer(t, inv_freq)
            return jnp.concatenate([freqs, freqs], axis=-1)

        def _rotate_half(x):
            x1, x2 = jnp.split(x, 2, axis=-1)
            return jnp.concatenate([-x2, x1], axis=-1)

        def _apply_rope(x, emb):
            return x * jnp.cos(emb)[None, None] + _rotate_half(x) * jnp.sin(emb)[None, None]
        key = jax.random.key(seed)
        ks = jax.random.split(key, 7)
        scale = 1.0 / np.sqrt(D_MODEL)
        q = jax.random.normal(ks[0], (B, S, D_MODEL), dtype=jnp.float32)
        k = jax.random.normal(ks[1], (B, S, D_MODEL), dtype=jnp.float32)
        v = jax.random.normal(ks[2], (B, S, D_MODEL), dtype=jnp.float32)
        W_q = jax.random.normal(ks[3], (D_MODEL, D_MODEL), dtype=jnp.float32) * scale
        W_k = jax.random.normal(ks[4], (D_MODEL, D_MODEL), dtype=jnp.float32) * scale
        W_v = jax.random.normal(ks[5], (D_MODEL, D_MODEL), dtype=jnp.float32) * scale
        W_o = jax.random.normal(ks[6], (D_MODEL, D_MODEL), dtype=jnp.float32) * scale
        mask = jnp.tril(jnp.ones((S, S), dtype=jnp.int32))[None, None]
        mask = jnp.broadcast_to(mask, (B, 1, S, S))
        return {'query': q, 'key': k, 'value': v, 'mask': mask, 'W_q': W_q, 'W_k': W_k, 'W_v': W_v, 'W_o': W_o}
    _L1_xattn_all = _L1_xattn_setup()
    _L1_xattn_in = {k: v for k, v in _L1_xattn_all.items() if k in ('W_q', 'W_k', 'W_v', 'W_o')}
    del _L1_xattn_all

    def _L1_ffn_setup():
        import jax, jax.numpy as jnp
        import numpy as np
        key = jax.random.key(seed)
        ks = jax.random.split(key, 5)
        B, T, D, E = (4, 512, 256, 8)
        inputs = jax.random.normal(ks[0], (B, T, D), dtype=jnp.float32)
        Wr = jax.random.normal(ks[1], (D, E), dtype=jnp.float32) * 0.02
        br = jnp.zeros((E,), dtype=jnp.float32)
        W1 = jax.random.normal(ks[2], (E, D, D), dtype=jnp.float32) * 0.02
        b1 = jnp.zeros((E, D), dtype=jnp.float32)
        W2 = jax.random.normal(ks[3], (E, D, D), dtype=jnp.float32) * 0.02
        b2 = jnp.zeros((E, D), dtype=jnp.float32)
        return {'inputs': inputs, 'Wr': Wr, 'br': br, 'W1': W1, 'b1': b1, 'W2': W2, 'b2': b2}
    _L1_ffn_all = _L1_ffn_setup()
    _L1_ffn_in = {k: v for k, v in _L1_ffn_all.items() if k in ('Wr', 'br', 'W1', 'b1', 'W2', 'b2')}
    del _L1_ffn_all
    return {'x': x, 'ctx_1024': ctx_1024, 'mask_Bx1xSxS2_ik0': mask_Bx1xSxS2_ik0, 'L0_xattn_W_q': _L0_xattn_in['W_q'], 'L0_xattn_W_k': _L0_xattn_in['W_k'], 'L0_xattn_W_v': _L0_xattn_in['W_v'], 'L0_xattn_W_o': _L0_xattn_in['W_o'], 'L0_ffn_w_q': _L0_ffn_in['w_q'], 'L0_ffn_keys': _L0_ffn_in['keys'], 'L0_ffn_expert_down': _L0_ffn_in['expert_down'], 'L0_ffn_expert_up': _L0_ffn_in['expert_up'], 'L0_ffn_norm_w': _L0_ffn_in['norm_w'], 'L1_xattn_W_q': _L1_xattn_in['W_q'], 'L1_xattn_W_k': _L1_xattn_in['W_k'], 'L1_xattn_W_v': _L1_xattn_in['W_v'], 'L1_xattn_W_o': _L1_xattn_in['W_o'], 'L1_ffn_Wr': _L1_ffn_in['Wr'], 'L1_ffn_br': _L1_ffn_in['br'], 'L1_ffn_W1': _L1_ffn_in['W1'], 'L1_ffn_b1': _L1_ffn_in['b1'], 'L1_ffn_W2': _L1_ffn_in['W2'], 'L1_ffn_b2': _L1_ffn_in['b2']}

def reference(x, ctx_1024, mask_Bx1xSxS2_ik0, L0_xattn_W_q, L0_xattn_W_k, L0_xattn_W_v, L0_xattn_W_o, L0_ffn_w_q, L0_ffn_keys, L0_ffn_expert_down, L0_ffn_expert_up, L0_ffn_norm_w, L1_xattn_W_q, L1_xattn_W_k, L1_xattn_W_v, L1_xattn_W_o, L1_ffn_Wr, L1_ffn_br, L1_ffn_W1, L1_ffn_b1, L1_ffn_W2, L1_ffn_b2):
    import jax
    import jax.numpy as jnp

    def _L0_xattn_ref(Q_in, K_in, V_in, W_q, W_k, W_v, W_o):
        import jax, jax.numpy as jnp
        import numpy as np
        D_MODEL = 256
        NUM_HEADS = 16
        D_K = D_MODEL // NUM_HEADS

        def _split_heads(x):
            B, S, _ = x.shape
            return x.reshape(B, S, NUM_HEADS, D_K).transpose(0, 2, 1, 3)
        Q = _split_heads(Q_in @ W_q.T)
        K = _split_heads(K_in @ W_k.T)
        V = _split_heads(V_in @ W_v.T)
        scores = jnp.einsum('bhqd,bhkd->bhqk', Q, K) / jnp.sqrt(jnp.float32(D_K))
        attn = jax.nn.softmax(scores, axis=-1)
        out = jnp.einsum('bhqk,bhkd->bhqd', attn, V)
        B, H, S, dk = out.shape
        concat = out.transpose(0, 2, 1, 3).reshape(B, S, H * dk)
        return concat @ W_o.T

    def _L0_ffn_ref(x, w_q, keys, expert_down, expert_up, norm_w):
        import jax, jax.numpy as jnp
        import numpy as np
        B, T, D = (2, 256, 256)
        H, DK, K = (8, 128, 8)
        NKEYS = 64
        NEXP = NKEYS * NKEYS

        def _rmsnorm(x, w, eps=1e-06):
            inv = jax.lax.rsqrt(jnp.mean(x * x, axis=-1, keepdims=True) + eps)
            return x * inv * w
        b, t, d = x.shape
        xn = _rmsnorm(x, norm_w)
        q = (xn @ w_q.T).reshape(b, t, H, 2, DK)
        sim1 = jnp.einsum('bthd,hkd->bthk', q[..., 0, :], keys[:, :, 0, :])
        sim2 = jnp.einsum('bthd,hkd->bthk', q[..., 1, :], keys[:, :, 1, :])
        s1, i1 = jax.lax.top_k(sim1, K)
        s2, i2 = jax.lax.top_k(sim2, K)
        all_idx = (i1[..., :, None] * NKEYS + i2[..., None, :]).reshape(b, t, H, K * K)
        all_sc = (s1[..., :, None] + s2[..., None, :]).reshape(b, t, H, K * K)
        fs, pk = jax.lax.top_k(all_sc, K)
        fi = jnp.take_along_axis(all_idx, pk, axis=-1)
        wd = expert_down[fi]
        wu = expert_up[fi]
        hidden = jax.nn.gelu(jnp.einsum('btd,bthkd->bthk', xn, wd), approximate=False)
        hidden = hidden * jax.nn.relu(fs)
        return jnp.einsum('bthk,bthkd->btd', hidden, wu)

    def _L1_xattn_ref(query, key, value, mask, W_q, W_k, W_v, W_o):
        import jax, jax.numpy as jnp
        import numpy as np
        D_MODEL = 256
        N_HEADS = 16
        D_K = D_MODEL // N_HEADS
        B, S = (2, 512)

        def _rope_emb(seq_len, d_k):
            inv_freq = 1.0 / 10000.0 ** (jnp.arange(0, d_k, 2, dtype=jnp.float32) / d_k)
            t = jnp.arange(seq_len, dtype=jnp.float32)
            freqs = jnp.outer(t, inv_freq)
            return jnp.concatenate([freqs, freqs], axis=-1)

        def _rotate_half(x):
            x1, x2 = jnp.split(x, 2, axis=-1)
            return jnp.concatenate([-x2, x1], axis=-1)

        def _apply_rope(x, emb):
            return x * jnp.cos(emb)[None, None] + _rotate_half(x) * jnp.sin(emb)[None, None]
        b = query.shape[0]

        def proj(x, W):
            y = jnp.einsum('bsd,ed->bse', x, W)
            return y.reshape(b, -1, N_HEADS, D_K).transpose(0, 2, 1, 3)
        Q = proj(query, W_q)
        K = proj(key, W_k)
        V = proj(value, W_v)
        emb_q = _rope_emb(Q.shape[2], D_K)
        emb_k = _rope_emb(K.shape[2], D_K)
        Q = _apply_rope(Q, emb_q)
        K = _apply_rope(K, emb_k)
        scores = jnp.einsum('bhqd,bhkd->bhqk', Q, K) / jnp.sqrt(jnp.float32(D_K))
        scores = jnp.where(mask == 0, jnp.float32(-jnp.inf), scores)
        attn = jax.nn.softmax(scores, axis=-1)
        ctx = jnp.einsum('bhqk,bhkd->bhqd', attn, V)
        ctx = ctx.transpose(0, 2, 1, 3).reshape(b, -1, D_MODEL)
        return jnp.einsum('bsd,ed->bse', ctx, W_o)

    def _L1_ffn_ref(inputs, Wr, br, W1, b1, W2, b2):
        import jax, jax.numpy as jnp
        import numpy as np
        B, T, D = inputs.shape
        E = Wr.shape[1]
        x = inputs.reshape(B * T, D)
        N = x.shape[0]
        C = N // E
        logits = x @ Wr + br
        probs = jax.nn.softmax(logits, axis=-1)
        gate = jnp.max(probs, axis=-1, keepdims=True)
        idx = jnp.argmax(probs, axis=-1)
        mask = jax.nn.one_hot(idx, E, dtype=jnp.float32)
        pos = (jnp.cumsum(mask, axis=0) * mask).astype(jnp.int32)
        mask = mask * (pos < C).astype(jnp.float32)
        mask_flat = jnp.sum(mask, axis=-1, keepdims=True)
        gate = gate * mask_flat
        combine = (gate * mask_flat * jax.nn.one_hot(idx, E, dtype=jnp.float32))[..., None] * jax.nn.one_hot(pos, C, dtype=jnp.float32)
        dispatch = combine
        expert_in = jnp.einsum('nd,nec->ecd', x, dispatch)
        h = jax.nn.relu(jnp.einsum('ecd,edf->ecf', expert_in, W1) + b1[:, None, :])
        eo = jnp.einsum('ecf,efd->ecd', h, W2) + b2[:, None, :]
        out = jnp.einsum('ecd,nec->nd', eo, combine)
        return out.reshape(B, T, D)
    x = x + _L0_xattn_ref(_layernorm(x, axis=-1), ctx_1024, ctx_1024, L0_xattn_W_q, L0_xattn_W_k, L0_xattn_W_v, L0_xattn_W_o)
    x = x + _L0_ffn_ref(_layernorm(x, axis=-1), L0_ffn_w_q, L0_ffn_keys, L0_ffn_expert_down, L0_ffn_expert_up, L0_ffn_norm_w)
    x = x + _L1_xattn_ref(_layernorm(x, axis=-1), ctx_1024, ctx_1024, mask_Bx1xSxS2_ik0, L1_xattn_W_q, L1_xattn_W_k, L1_xattn_W_v, L1_xattn_W_o)
    x = x + _L1_ffn_ref(_layernorm(x, axis=-1), L1_ffn_Wr, L1_ffn_br, L1_ffn_W1, L1_ffn_b1, L1_ffn_W2, L1_ffn_b2)
    return x

_drawn_inputs = setup_inputs


def setup_inputs(seed=0):
    import zlib

    import numpy as np

    out = dict(_drawn_inputs(seed))
    spreads = {'L0_ffn_norm_w': (1.0, 0.6),
     'L1_ffn_br': (0.0, 2.0),
     'L1_ffn_b1': (0.0, 2.0),
     'L1_ffn_b2': (0.0, 2.0)}
    factors = {'L0_ffn_w_q': 8.0,
     'L0_ffn_keys': 8.0,
     'L0_ffn_expert_down': 8.0,
     'L0_ffn_expert_up': 8.0,
     'L1_ffn_Wr': 18.57,
     'L1_ffn_W1': 35.579,
     'L1_ffn_W2': 27.098,
     'L1_xattn_W_q': 8.0,
     'L1_xattn_W_k': 8.0,
     'L1_xattn_W_v': 8.0,
     'L1_xattn_W_o': 8.0}
    for name, (base, spread) in spreads.items():
        noise = np.random.default_rng([zlib.crc32(name.encode()), seed]).standard_normal(out[name].shape)
        drawn = base * np.exp(spread * noise) if base else spread * noise
        out[name] = jnp.asarray(drawn.astype(out[name].dtype))
    for name, factor in factors.items():
        out[name] = (out[name] * factor).astype(out[name].dtype)
    return out
```

```python
from contextlib import ExitStack

import concourse.bass as bass
from concourse import mybir

F32 = mybir.dt.float32
BF16 = mybir.dt.bfloat16
I32 = mybir.dt.int32
U32 = mybir.dt.uint32
ALU = mybir.AluOpType
ACT = mybir.ActivationFunctionType
AX = mybir.AxisListType

P = 128
D = 256
DC = D // P
B, S, SK = 4, 1024, 77
N = B * S
TILES = N // P
TPB = S // P
H, DK = 16, 16
HU = H // 2
GRP = 4
BANK = 512
LN_EPS = 1e-5
RMS_EPS = 1e-6
PH, NKEYS, TOPK = 8, 64, 8
E8, CAP = 8, N // 8


def row_scale(nc, ctx, block, mv, scale, rms, name):
    var = mv[:, :, 1]
    a = ctx.enter_context(nc.sbuf_tensor(name + "_a", [P, TILES], F32))
    root = ctx.enter_context(nc.sbuf_tensor(name + "_root", [P, TILES], F32))
    r = ctx.enter_context(nc.sbuf_tensor(name + "_r", [P, TILES], F32))
    t = ctx.enter_context(nc.sbuf_tensor(name + "_t", [P, TILES], F32))
    a_ready = ctx.enter_context(nc.semaphore(name + "_a_ready"))
    root_ready = ctx.enter_context(nc.semaphore(name + "_root_ready"))
    step = ctx.enter_context(nc.semaphore(name + "_step"))
    rounds = 2 if rms else 1

    def on_vector(dve):
        n = 0
        for k in range(rounds):
            if k == 0:
                dve.tensor_scalar(a[:], var, LN_EPS, None, ALU.add).then_inc(a_ready, 1)
            else:
                dve.tensor_tensor(t[:], scale[:], scale[:], ALU.mult).then_inc(step, 1)
                n += 1
                dve.wait_ge(step, n)
                dve.tensor_tensor(t[:], t[:], var, ALU.mult).then_inc(step, 1)
                n += 1
                dve.wait_ge(step, n)
                dve.tensor_scalar(a[:], t[:], RMS_EPS, None, ALU.add).then_inc(a_ready, 1)
            dve.wait_ge(root_ready, k + 1)
            dve.reciprocal(r[:], root[:]).then_inc(step, 1)
            n += 1
            dve.wait_ge(step, n)
            dve.tensor_tensor(t[:], r[:], r[:], ALU.mult).then_inc(step, 1)
            n += 1
            dve.wait_ge(step, n)
            dve.wait_ge(a_ready, k + 1)
            dve.tensor_tensor(t[:], t[:], a[:], ALU.mult).then_inc(step, 1)
            n += 1
            dve.wait_ge(step, n)
            dve.tensor_scalar(t[:], t[:], -0.5, 1.5, ALU.mult, ALU.add).then_inc(step, 1)
            n += 1
            dve.wait_ge(step, n)
            if k == 0:
                dve.tensor_tensor(scale[:], r[:], t[:], ALU.mult).then_inc(step, 1)
            else:
                dve.tensor_tensor(r[:], r[:], t[:], ALU.mult).then_inc(step, 1)
                n += 1
                dve.wait_ge(step, n)
                dve.tensor_tensor(scale[:], scale[:], r[:], ALU.mult).then_inc(step, 1)
            n += 1
            dve.wait_ge(step, n)

    def on_scalar(act):
        for k in range(rounds):
            act.wait_ge(a_ready, k + 1)
            act.activation(root[:], a[:], ACT.Sqrt).then_inc(root_ready, 1)

    return on_vector, on_scalar


def first_stats(nc, x_in, mv):
    with ExitStack() as ctx:
        x = ctx.enter_context(nc.sbuf_tensor("fs_x", [P, TILES, D], F32))
        st = ctx.enter_context(nc.sbuf_tensor("fs_st", [P, TILES, 6], F32))
        loaded = [ctx.enter_context(nc.semaphore(f"fs_loaded{g}")) for g in range(4)]
        sums_ready = ctx.enter_context(nc.semaphore("fs_sums_ready"))
        block = ctx.enter_context(nc.Block())
        G = TILES // 4

        @block.sync
        def _(sp):
            for g in range(4):
                sp.dma_start(x[:, g * G:(g + 1) * G, :],
                             x_in[g * G:(g + 1) * G].rearrange("t p d -> p t d")).then_inc(loaded[g], 16)

        @block.vector
        def _(dve):
            for t in range(TILES):
                if t % G == 0:
                    dve.wait_ge(loaded[t // G], 16)
                dve.bn_stats(st[:, t, :], x[:, t, :]).then_inc(sums_ready, 1)
            for t in range(TILES):
                dve.wait_ge(sums_ready, t + 1)
                dve.bn_aggr(mv[:, t, :], st[:, t, :])


def attention(nc, tag, x_in, x_out, mv, ctxT, wqT, wkT, wvT, woT, bmask, ident_d, rope=None, mask=None):
    with ExitStack() as ctx:
        def sb(name, shape, dt=F32):
            return ctx.enter_context(nc.sbuf_tensor(f"{tag}_{name}", shape, dt))

        def sem(name):
            return ctx.enter_context(nc.semaphore(f"{tag}_{name}"))

        ident = sb("ident", [P, P])
        bm = sb("bm", [P, HU])
        cT = sb("cT", [P, DC, B * SK])
        wq, wk, wv, wo = (sb(n, [P, DC, D]) for n in ("wq", "wk", "wv", "wo"))
        keys_bd = sb("keys_bd", [P, DC, B, HU, SK])
        vals = sb("vals", [SK, B, H, DK + 1])
        scale = sb("scale", [P, TILES])
        xa = sb("xa", [P, 2, D])
        xr = sb("xr", [P, 2, D])
        xo = sb("xo", [P, 2, D])
        y = sb("y", [P, 2, D])
        yT = sb("yT", [P, DC, P])
        qT = sb("qT", [P, 2, DC, P])
        pr = sb("pr", [P, 2, 2, HU, SK])
        mx = sb("mx", [P, 2, 2, HU])
        pT = sb("pT", [SK, 2, HU, P])
        rs = sb("rs", [P, H])
        o = sb("o", [P, D])
        oT = sb("oT", [P, DC, P])
        st = sb("st", [P, 6])
        ag = sb("ag", [P, 2])
        if rope:
            wqr, wkr = sb("wqr", [P, DC, D]), sb("wkr", [P, DC, D])
            cos, sin = sb("cos", [P, S]), sb("sin", [P, S])
            rk = sb("rk", [P, B, SK])
            rt = sb("rt", [P, 2, DC, P])
        if mask is not None:
            mi = sb("mi", [P, 2, SK], I32)
            mb = sb("mb", [P, 2, SK])
            ms = sb("ms", [P, 2, HU, SK])

        def ps(name, shape):
            return ctx.enter_context(nc.psum_tensor(f"{tag}_{name}", shape, F32))

        ps_s = ps("ps_s", [P, 2, 2, BANK])
        ps_t = ps("ps_t", [P, HU, P])
        ps_m = ps("ps_m", [P, BANK])
        ps_o = ps("ps_o", [P, BANK])

        consts = sem("consts")
        proj_ready, proj_used, dve_setup, setup_done = (sem(n) for n in (
            "proj_ready", "proj_used", "dve_setup", "setup_done"))
        xa_loaded = [sem(f"xa_loaded{p}") for p in range(2)]
        xr_loaded = [sem(f"xr_loaded{p}") for p in range(2)]
        m_loaded = [sem(f"m_loaded{p}") for p in range(2)]
        stored = [sem(f"stored{p}") for p in range(2)]
        y_ready, yT_ready, yT_copied, q_ready, q_copied = (sem(n) for n in (
            "y_ready", "yT_ready", "yT_copied", "q_ready", "q_copied"))
        s_ready, sub_ready, p_ready, pT_ready, pT_copied = (sem(n) for n in (
            "s_ready", "sub_ready", "p_ready", "pT_ready", "pT_copied"))
        av_ready, o_ready, oT_ready, oT_copied, out_ready, res_done = (sem(n) for n in (
            "av_ready", "o_ready", "oT_ready", "oT_copied", "out_ready", "res_done"))
        dve_a, dve_b, bias_ready = sem("dve_a"), sem("dve_b"), sem("bias_ready")

        scale_dve, scale_act = row_scale(nc, ctx, None, mv, scale, False, tag + "_ln")
        NCONST = 7 + (4 if rope else 0)
        block = ctx.enter_context(nc.Block())

        @block.sync
        def _(sp):
            sp.dma_start(cT[:], ctxT).then_inc(consts, 16)
            sp.dma_start(wk[:], wkT).then_inc(consts, 16)
            sp.dma_start(wv[:], wvT).then_inc(consts, 16)
            sp.dma_start(wq[:], wqT).then_inc(consts, 16)
            sp.dma_start(wo[:], woT).then_inc(consts, 16)
            sp.dma_start(bm[:], bmask).then_inc(consts, 16)
            sp.dma_start(ident[:], ident_d).then_inc(consts, 16)
            if rope:
                sp.dma_start(wqr[:], rope[0]).then_inc(consts, 16)
                sp.dma_start(wkr[:], rope[1]).then_inc(consts, 16)
                sp.dma_start(cos[:], rope[2]).then_inc(consts, 16)
                sp.dma_start(sin[:], rope[3]).then_inc(consts, 16)

            def load_a(i, p):
                sp.dma_start(xa[:, p, :], x_in[i]).then_inc(xa_loaded[p], 16)
                if mask is not None:
                    sp.dma_start(mi[:, p, :], mask[i]).then_inc(m_loaded[p], 16)

            def store(i, p):
                sp.wait_ge(res_done, i + 2)
                sp.dma_start(x_out[i], xo[:, p, :]).then_inc(stored[p], 16)

            for p in range(2):
                sp.sem_inc(stored[p], 16)
                load_a(p, p)
                sp.dma_start(xr[:, p, :], x_in[p]).then_inc(xr_loaded[p], 16)
            with sp.Fori(0, TILES // 2 - 1) as t:
                for p in range(2):
                    i = t * 2 + p
                    sp.wait_ge(y_ready, i + 1)
                    load_a(i + 2, p)
                    store(i, p)
                    sp.dma_start(xr[:, p, :], x_in[i + 2]).then_inc(xr_loaded[p], 16)
            for p in range(2):
                store(TILES - 2 + p, p)
            for p in range(2):
                sp.wait_ge(stored[p], 16 * (TILES // 2 + 1))

        @block.tensor
        def _(pe):
            pe.wait_ge(consts, 16 * NCONST)
            n = 0
            for c in range(DC):
                for w in ((wk, wkr) if rope else (wk,)):
                    if n >= 2:
                        pe.wait_ge(proj_used, n - 1)
                    for k in range(DC):
                        last = pe.matmul(ps_s[:, 0, n % 2, 0:B * SK], w[:, k, c * P:(c + 1) * P], cT[:, k, :],
                                         start=(k == 0), stop=(k == DC - 1))
                    last.then_inc(proj_ready, 1)
                    n += 1
            for b in range(B):
                if n >= 2:
                    pe.wait_ge(proj_used, n - 1)
                for k in range(DC):
                    last = pe.matmul(ps_s[0:SK, 0, n % 2, 0:D], cT[:, k, b * SK:(b + 1) * SK], wv[:, k, :],
                                     start=(k == 0), stop=(k == DC - 1))
                last.then_inc(proj_ready, 1)
                n += 1
            pe.wait_ge(setup_done, 1)

            def ahead(i, p, first=False):
                pe.wait_ge(y_ready, i + 1)
                for k in range(DC):
                    last = pe.transpose(ps_m[:, k * P:(k + 1) * P], y[:, p, k * P:(k + 1) * P], ident[:])
                last.then_inc(yT_ready, 1)
                pe.wait_ge(yT_copied, i + 1)
                for r, w in enumerate((wq, wqr) if rope else (wq,)):
                    for c in range(DC):
                        for k in range(DC):
                            last = pe.matmul(ps_m[:, (r * DC + c) * P:(r * DC + c + 1) * P],
                                             w[:, k, c * P:(c + 1) * P], yT[:, k, :],
                                             start=(k == 0), stop=(k == DC - 1))
                last.then_inc(q_ready, 1)
                pe.wait_ge(q_copied, i + 1)
                for u in range(2):
                    if not first:
                        pe.wait_ge(sub_ready, i * 2 + u - 1)
                    for g in range(2):
                        last = pe.matmul(ps_s[:, u, g, 0:GRP * SK], qT[:, p, u, :],
                                         keys_bd[:, u, i // TPB, g * GRP:(g + 1) * GRP, :],
                                         start=True, stop=True)
                    last.then_inc(s_ready, 1)

            def behind(i, p):
                for u in range(2):
                    pe.wait_ge(p_ready, i * 2 + u + 1)
                    pe.wait_ge(pT_copied, i * 2 + u + 1)
                    for h in range(HU):
                        last = pe.transpose(ps_t[0:SK, h, :], pr[:, p, u, h, :], ident[:])
                    last.then_inc(pT_ready, 1)
                    pe.wait_ge(pT_copied, i * 2 + u + 2)
                    if u == 0:
                        pe.wait_ge(res_done, i + 1)
                    for h in range(HU):
                        g = u * HU + h
                        last = pe.matmul(ps_o[:, g * (DK + 1):(g + 1) * (DK + 1)], pT[:, u, h, :],
                                         vals[:, i // TPB, g, :], start=True, stop=True)
                last.then_inc(av_ready, 1)
                pe.wait_ge(o_ready, i + 1)
                for k in range(DC):
                    last = pe.transpose(ps_m[:, k * P:(k + 1) * P], o[:, k * P:(k + 1) * P], ident[:])
                last.then_inc(oT_ready, 1)
                pe.wait_ge(oT_copied, i + 1)
                for k in range(DC):
                    last = pe.matmul(ps_o[:, 0:D], oT[:, k, :], wo[:, k, :], start=(k == 0), stop=(k == DC - 1))
                last.then_inc(out_ready, 1)

            ahead(0, 0, first=True)
            with pe.Fori(0, TILES // 2 - 1) as t:
                ahead(t * 2 + 1, 1)
                behind(t * 2, 0)
                ahead(t * 2 + 2, 0)
                behind(t * 2 + 1, 1)
            ahead(TILES - 1, 1)
            behind(TILES - 2, 0)
            behind(TILES - 1, 1)

        @block.scalar
        def _(act):
            scale_act(act)
            act.sem_inc(pT_copied, 1)

            def ahead(i, p):
                act.wait_ge(yT_ready, i + 1)
                act.activation(yT[:], ps_m[:, 0:D].rearrange("p (c t) -> p c t", c=DC), ACT.Copy).then_inc(yT_copied, 1)
                if not rope:
                    act.wait_ge(q_ready, i + 1)
                    act.activation(qT[:, p], ps_m[:, 0:D].rearrange("p (c t) -> p c t", c=DC),
                                   ACT.Copy).then_inc(q_copied, 1)
                for u in range(2):
                    act.wait_ge(sub_ready, i * 2 + u + 1)
                    act.activation(pr[:, p, u], pr[:, p, u], ACT.Exp, scale=float(DK) ** -0.5).then_inc(p_ready, 1)

            def behind(i, p):
                for u in range(2):
                    act.wait_ge(pT_ready, i * 2 + u + 1)
                    act.activation(pT[:, u], ps_t[0:SK], ACT.Copy).then_inc(pT_copied, 1)
                act.wait_ge(oT_ready, i + 1)
                act.activation(oT[:], ps_m[:, 0:D].rearrange("p (c t) -> p c t", c=DC), ACT.Copy).then_inc(oT_copied, 1)

            ahead(0, 0)
            with act.Fori(0, TILES // 2 - 1) as t:
                ahead(t * 2 + 1, 1)
                behind(t * 2, 0)
                ahead(t * 2 + 2, 0)
                behind(t * 2 + 1, 1)
            ahead(TILES - 1, 1)
            behind(TILES - 2, 0)
            behind(TILES - 1, 1)

        @block.vector
        def _(dve):
            scale_dve(dve)
            dve.wait_ge(consts, 16 * NCONST)
            n, m = 0, 0
            for c in range(DC):
                mask_bc = bm[:].unsqueeze(1).unsqueeze(3).broadcast_to([P, B, HU, SK])
                if rope:
                    dve.wait_ge(proj_ready, n + 1)
                    if c:
                        dve.wait_ge(dve_setup, m)
                    cos_b = cos[:, 0:SK].unsqueeze(1).broadcast_to([P, B, SK])
                    sin_b = sin[:, 0:SK].unsqueeze(1).broadcast_to([P, B, SK])
                    k0 = ps_s[:, 0, n % 2, 0:B * SK].rearrange("p (b k) -> p b k", b=B)
                    k1 = ps_s[:, 0, (n + 1) % 2, 0:B * SK].rearrange("p (b k) -> p b k", b=B)
                    dve.tensor_tensor(rk[:], k0, cos_b, ALU.mult).then_inc(proj_used, 1)
                    dve.wait_ge(proj_ready, n + 2)
                    tmp = pr[:].rearrange("p a u h k -> p (a u h k)")[:, 0:B * SK].rearrange("p (b k) -> p b k", b=B)
                    dve.tensor_tensor(tmp, k1, sin_b, ALU.mult).then_inc(proj_used, 1)
                    dve.wait_ge(proj_used, n + 2)
                    dve.tensor_tensor(rk[:], rk[:], tmp, ALU.add).then_inc(dve_setup, 1)
                    m += 1
                    dve.wait_ge(dve_setup, m)
                    n += 2
                    for b in range(B):
                        last = dve.tensor_tensor(keys_bd[:, c, b], rk[:, b].unsqueeze(1).broadcast_to([P, HU, SK]),
                                                 bm[:].unsqueeze(2).broadcast_to([P, HU, SK]), ALU.mult)
                    last.then_inc(dve_setup, 1)
                    m += 1
                else:
                    dve.wait_ge(proj_ready, n + 1)
                    for b in range(B):
                        last = dve.tensor_tensor(
                            keys_bd[:, c, b],
                            ps_s[:, 0, n % 2, b * SK:(b + 1) * SK].unsqueeze(1).broadcast_to([P, HU, SK]),
                            bm[:].unsqueeze(2).broadcast_to([P, HU, SK]), ALU.mult)
                    last.then_inc(proj_used, 1)
                    n += 1
            dve.memset(vals[:, :, :, DK:DK + 1], 1.0)
            for b in range(B):
                dve.wait_ge(proj_ready, n + 1)
                last = dve.tensor_copy(vals[:, b, :, 0:DK], ps_s[0:SK, 0, n % 2, 0:D].rearrange("p (h d) -> p h d", h=H))
                last.then_inc(proj_used, 1)
                n += 1
            dve.wait_ge(proj_used, n)
            dve.sem_inc(setup_done, 1)
            dve.sem_inc(res_done, 1)

            def ahead(i, p, t):
                dve.wait_ge(xa_loaded[p], (t + 1) * 16)
                if mask is not None:
                    dve.wait_ge(m_loaded[p], (t + 1) * 16)
                    dve.tensor_scalar(mb[:, p, :], mi[:, p, :], 0.0, -3e38, ALU.is_equal, ALU.mult).then_inc(bias_ready, 1)
                dve.tensor_scalar(y[:, p, :], xa[:, p, :], mv[:, bass.ds(i, 1), 0], scale[:, bass.ds(i, 1)],
                                  ALU.subtract, ALU.mult).then_inc(y_ready, 1)
                if rope:
                    tok = slice(0, P)
                    off = (i % TPB) * P
                    dve.wait_ge(q_ready, i + 1)
                    for r, tab in ((0, cos), (1, sin)):
                        last = dve.tensor_tensor(rt[:, r],
                                                 ps_m[:, r * D:(r + 1) * D].rearrange("p (c t) -> p c t", c=DC),
                                                 tab[:, bass.ds(off, P)].unsqueeze(1).broadcast_to([P, DC, P]), ALU.mult)
                    last.then_inc(dve_a, 1)
                    dve.wait_ge(dve_a, i * ASTEPS + 1)
                    dve.tensor_tensor(qT[:, p], rt[:, 0], rt[:, 1], ALU.add).then_inc(q_copied, 1)
                for u in range(2):
                    dve.wait_ge(s_ready, i * 2 + u + 1)
                    s = ps_s[:, u, :, 0:GRP * SK].rearrange("p g (h k) -> p g h k", h=GRP)
                    m_u = mx[:, p, u].rearrange("p (g h) -> p g h", g=2)
                    if mask is not None:
                        if u == 0:
                            dve.wait_ge(bias_ready, i + 1)
                        s_m = ms[:, u].rearrange("p (g h) k -> p g h k", g=2)
                        for g in range(2):
                            last = dve.tensor_tensor(s_m[:, g], s[:, g],
                                                     mb[:, p, :].unsqueeze(1).broadcast_to([P, GRP, SK]), ALU.add)
                        last.then_inc(dve_a, 1)
                        dve.wait_ge(dve_a, i * ASTEPS + (1 if rope else 0) + 2 * u + 1)
                        s = s_m
                    dve.tensor_reduce(m_u, s, AX.X, ALU.max).then_inc(dve_a, 1)
                    dve.wait_ge(dve_a, i * ASTEPS + (1 if rope else 0) + (2 * u + 2 if mask is not None else u + 1))
                    for g in range(2):
                        last = dve.tensor_tensor(pr[:, p, u].rearrange("p (g h) k -> p g h k", g=2)[:, g], s[:, g],
                                                 m_u[:, g].unsqueeze(2).broadcast_to([P, GRP, SK]), ALU.subtract)
                    last.then_inc(sub_ready, 1)

            ASTEPS = (1 if rope else 0) + (4 if mask is not None else 2)
            BSTEPS = 3

            def behind(i, p, t):
                dve.wait_ge(av_ready, i + 1)
                ov = ps_o[:, 0:H * (DK + 1)].rearrange("p (h e) -> p h e", h=H)
                dve.reciprocal(rs[:].unsqueeze(2), ov[:, :, DK:DK + 1]).then_inc(dve_b, 1)
                dve.wait_ge(dve_b, i * BSTEPS + 1)
                dve.tensor_tensor(o[:].rearrange("p (h e) -> p h e", h=H), ov[:, :, 0:DK],
                                  rs[:].unsqueeze(2).broadcast_to([P, H, DK]), ALU.mult).then_inc(o_ready, 1)
                dve.wait_ge(xr_loaded[p], (t + 1) * 16)
                dve.wait_ge(stored[p], (t + 1) * 16)
                dve.wait_ge(out_ready, i + 1)
                dve.tensor_tensor(xo[:, p, :], ps_o[:, 0:D], xr[:, p, :], ALU.add).then_inc(res_done, 1)
                dve.wait_ge(res_done, i + 2)
                dve.bn_stats(st[:], xo[:, p, :]).then_inc(dve_b, 1)
                dve.wait_ge(dve_b, i * BSTEPS + 2)
                dve.nop(nofuse=True)
                dve.bn_aggr(ag[:], st[:]).then_inc(dve_b, 1)
                dve.wait_ge(dve_b, i * BSTEPS + 3)
                dve.nop(nofuse=True)
                dve.tensor_copy(mv[:, bass.ds(i, 1), :], ag[:].unsqueeze(1))

            ahead(0, 0, 0)
            with dve.Fori(0, TILES // 2 - 1) as t:
                ahead(t * 2 + 1, 1, t)
                behind(t * 2, 0, t)
                ahead(t * 2 + 2, 0, t + 1)
                behind(t * 2 + 1, 1, t)
            ahead(TILES - 1, 1, TILES // 2 - 1)
            behind(TILES - 2, 0, TILES // 2 - 1)
            behind(TILES - 1, 1, TILES // 2 - 1)


KH = PH * TOPK
NF = 32
PARTS = 3
SEL = 2 + PARTS
PAIRS = TILES // 2
TG = 32
TB = 8


def product_keys(nc, x_in, mv, xnT_d, sel_d, w_q, keysT, norm_w, ident_d, identb_d, iota8_d):
    with ExitStack() as ctx:
        def sb(name, shape, dt=F32):
            return ctx.enter_context(nc.sbuf_tensor("pk_" + name, shape, dt))

        def sem(name):
            return ctx.enter_context(nc.semaphore("pk_" + name))

        def ps(name, shape, dt=F32):
            return ctx.enter_context(nc.psum_tensor("pk_" + name, shape, dt))

        NS = 2 * PH
        ident, identb = sb("ident", [P, P]), sb("identb", [P, P], BF16)
        wq, kT = sb("wq", [P, NS, D]), sb("kT", [P, NS, NKEYS])
        nw = sb("nw", [P, DC])
        iota8 = sb("iota8", [P, TOPK, TOPK])
        fold = sb("fold", [P, DC, NS * NKEYS])
        scale = sb("scale", [P, TILES])
        x, y, xT = sb("x", [P, 2, D]), sb("y", [P, 2, D]), sb("xT", [P, 2, DC, P])
        sim = sb("sim", [P, 2, NS, NKEYS])
        top, topi, topf = sb("top", [P, NS, TOPK]), sb("topi", [P, NS, TOPK], U32), sb("topf", [P, NS, TOPK])
        grid = sb("grid", [P, PH, TOPK, TOPK])
        best, bi = sb("best", [P, PH, TOPK]), sb("bi", [P, PH, TOPK], U32)
        ab, abf = sb("ab", [P, 2, PH, TOPK], U32), sb("abf", [P, 2, PH, TOPK])
        eq = sb("eq", [P, 2, PH, TOPK, TOPK])
        ij = sb("ij", [P, 2, PH, TOPK])
        far = sb("far", [P, PH, TOPK])
        w, r1, r2 = sb("w", [P, PH, TOPK]), sb("r1", [P, PH, TOPK]), sb("r2", [P, PH, TOPK])
        sel = sb("sel", [P, 2, SEL, 2, KH], BF16)
        selT = sb("selT", [P, 2, SEL, P], BF16)
        ps_f, ps_y, ps_s = ps("ps_f", [P, 2, BANK]), ps("ps_y", [P, BANK]), ps("ps_s", [P, 2, BANK])
        ps_t = ps("ps_t", [P, SEL, P], BF16)

        consts, fold_ready, fold_copied = sem("consts"), sem("fold_ready"), sem("fold_copied")
        x_loaded = [sem(f"x_loaded{p}") for p in range(2)]
        xT_stored = [sem(f"xT_stored{p}") for p in range(2)]
        sel_stored = [sem(f"sel_stored{p}") for p in range(2)]
        y_ready, yT_ready, xT_ready, s_ready, sim_ready = (sem(n) for n in (
            "y_ready", "yT_ready", "xT_ready", "s_ready", "sim_ready"))
        chain, sel_ready, selT_ready, selT_copied = (sem(n) for n in ("chain", "sel_ready", "selT_ready", "selT_copied"))
        scale_dve, scale_act = row_scale(nc, ctx, None, mv, scale, True, "pk_ln")
        STEPS = 17
        block = ctx.enter_context(nc.Block())

        @block.sync
        def _(sp):
            for dst, src in ((wq, w_q), (kT, keysT), (nw, norm_w), (ident, ident_d), (identb, identb_d), (iota8, iota8_d)):
                sp.dma_start(dst[:], src).then_inc(consts, 16)
            for p in range(2):
                sp.sem_inc(xT_stored[p], 16)
                sp.sem_inc(sel_stored[p], 16)
                sp.dma_start(x[:, p, :], x_in[p]).then_inc(x_loaded[p], 16)

            def stores(i, m, q):
                sp.wait_ge(xT_ready, i + 1)
                sp.nop(nofuse=True)
                sp.dma_start(xnT_d[m, :, :, q, :], xT[:, q]).then_inc(xT_stored[q], 16)

            with sp.Fori(0, PAIRS - 1) as m:
                for q in range(2):
                    i = m * 2 + q
                    sp.wait_ge(y_ready, i + 1)
                    sp.nop(nofuse=True)
                    sp.dma_start(x[:, q, :], x_in[i + 2]).then_inc(x_loaded[q], 16)
                    stores(i, m, q)
            for q in range(2):
                stores(TILES - 2 + q, PAIRS - 1, q)
                sp.wait_ge(xT_stored[q], 16 * (PAIRS + 1))

        @block.tensor
        def _(pe):
            pe.wait_ge(consts, 16 * 6)
            pe.sem_inc(selT_ready, 2)
            for c in range(DC):
                if c:
                    pe.wait_ge(fold_copied, c)
                for s in range(NS):
                    last = pe.matmul(ps_f[:, s // PH, (s % PH) * NKEYS:(s % PH + 1) * NKEYS],
                                     wq[:, s, c * P:(c + 1) * P], kT[:, s, :], start=True, stop=True)
                last.then_inc(fold_ready, 1)
            pe.wait_ge(fold_copied, DC)

            def selections(m, p):
                pe.wait_ge(sel_ready, m + 1)
                pe.wait_ge(selT_copied, m + 1)
                for k in range(SEL):
                    last = pe.transpose(ps_t[:, k, :], sel[:, p, k].rearrange("p q k -> p (q k)"), identb[:])
                last.then_inc(selT_ready, 1)

            def tile(i, q):
                pe.wait_ge(y_ready, i + 1)
                for k in range(DC):
                    last = pe.transpose(ps_y[:, k * P:(k + 1) * P], y[:, q, k * P:(k + 1) * P], ident[:])
                last.then_inc(yT_ready, 1)
                pe.wait_ge(xT_ready, i + 1)
                if not (isinstance(i, int) and i == 0):
                    pe.wait_ge(sim_ready, i)
                for g in range(2):
                    for k in range(DC):
                        last = pe.matmul(ps_s[:, g, :], xT[:, q, k, :], fold[:, k, g * BANK:(g + 1) * BANK],
                                         start=(k == 0), stop=(k == DC - 1))
                last.then_inc(s_ready, 1)

            for q in range(2):
                tile(q, q)
            with pe.Fori(0, PAIRS // 2 - 1) as mm:
                for p in range(2):
                    m = mm * 2 + p
                    for q in range(2):
                        tile(m * 2 + 2 + q, q)
                    selections(m, p)
            m = PAIRS - 2
            for q in range(2):
                tile(m * 2 + 2 + q, q)
            selections(m, 0)
            selections(m + 1, 1)

        @block.scalar
        def _(act):
            scale_act(act)
            act.wait_ge(consts, 16 * 6)
            act.sem_inc(selT_copied, 1)
            for c in range(DC):
                act.wait_ge(fold_ready, c + 1)
                act.activation(fold[:, c, :], ps_f[:].rearrange("p g n -> p (g n)"), ACT.Copy).then_inc(fold_copied, 1)

            def tile(i, m, q):
                act.wait_ge(yT_ready, i + 1)
                act.wait_ge(xT_stored[q], m * 16 + 16)
                for k in range(DC):
                    last = act.activation(xT[:, q, k, :], ps_y[:, k * P:(k + 1) * P], ACT.Copy, scale=nw[:, k:k + 1])
                last.then_inc(xT_ready, 1)
                act.wait_ge(s_ready, i + 1)
                if not (isinstance(i, int) and i < 2):
                    act.wait_ge(chain, (i - 2) * STEPS + 2)
                act.activation(sim[:, q].rearrange("p s k -> p (s k)"), ps_s[:].rearrange("p g n -> p (g n)"),
                               ACT.Copy).then_inc(sim_ready, 1)

            def selections(m, mm, p):
                act.wait_ge(selT_ready, m + 3)
                act.wait_ge(sel_stored[p], mm * 16 + 16)
                act.activation(selT[:, p], ps_t[:], ACT.Copy).then_inc(selT_copied, 1)
                act.wait_ge(selT_copied, m + 2)
                act.dma_start(sel_d[m], selT[:, p]).then_inc(sel_stored[p], 16)

            for q in range(2):
                tile(q, 0, q)
            with act.Fori(0, PAIRS // 2 - 1) as mm:
                for p in range(2):
                    m = mm * 2 + p
                    for q in range(2):
                        tile(m * 2 + 2 + q, m + 1, q)
                    selections(m, mm, p)
            m = PAIRS - 2
            for q in range(2):
                tile(m * 2 + 2 + q, m + 1, q)
            selections(m, PAIRS // 2 - 1, 0)
            selections(m + 1, PAIRS // 2 - 1, 1)
            for p in range(2):
                act.wait_ge(sel_stored[p], 16 * (PAIRS // 2 + 1))

        @block.vector
        def _(dve):
            scale_dve(dve)
            dve.wait_ge(consts, 16 * 6)

            def norm(i, m, q):
                dve.wait_ge(x_loaded[q], m * 16 + 16)
                if not (isinstance(i, int) and i < 2):
                    dve.wait_ge(yT_ready, i - 1)
                dve.tensor_scalar(y[:, q, :], x[:, q, :], mv[:, bass.ds(i, 1), 0], scale[:, bass.ds(i, 1)],
                                  ALU.subtract, ALU.mult).then_inc(y_ready, 1)

            def winners(i, m, p, q):
                n = [0]

                def settle(ins):
                    n[0] += 1
                    ins.then_inc(chain, 1)
                    dve.wait_ge(chain, i * STEPS + n[0])
                    dve.nop(nofuse=True)

                dve.wait_ge(sim_ready, i + 1)
                dve.nop(nofuse=True)
                for s in range(NS):
                    last = dve.max(top[:, s, :], sim[:, q, s, :])
                settle(last)
                for s in range(NS):
                    last = dve.max_index(topi[:, s, :], top[:, s, :], sim[:, q, s, :])
                settle(last)
                dve.tensor_copy(topf[:], topi[:])
                t2 = top[:].rearrange("p (h s) k -> p h s k", s=2)
                for h in range(PH):
                    last = dve.tensor_tensor(grid[:, h], t2[:, h, 0].unsqueeze(2).broadcast_to([P, TOPK, TOPK]),
                                             t2[:, h, 1].unsqueeze(1).broadcast_to([P, TOPK, TOPK]), ALU.add)
                settle(last)
                for h in range(PH):
                    last = dve.max(best[:, h, :], grid[:, h].rearrange("p a b -> p (a b)"))
                settle(last)
                for h in range(PH):
                    last = dve.max_index(bi[:, h, :], best[:, h, :], grid[:, h].rearrange("p a b -> p (a b)"))
                settle(last)
                dve.tensor_scalar(ab[:, 0], bi[:], 3, None, ALU.logical_shift_right)
                settle(dve.tensor_scalar(ab[:, 1], bi[:], 7, None, ALU.bitwise_and))
                settle(dve.tensor_copy(abf[:], ab[:]))
                for s in range(2):
                    last = dve.tensor_tensor(eq[:, s], abf[:, s].unsqueeze(2).broadcast_to([P, PH, TOPK, TOPK]),
                                             iota8[:].unsqueeze(1).broadcast_to([P, PH, TOPK, TOPK]), ALU.is_equal)
                settle(last)
                tf = topf[:].rearrange("p (h s) k -> p s h k", s=2)
                for s in range(2):
                    last = dve.tensor_tensor(eq[:, s], eq[:, s],
                                             tf[:, s].unsqueeze(3).broadcast_to([P, PH, TOPK, TOPK]), ALU.mult)
                settle(last)
                for s in range(2):
                    last = dve.tensor_reduce(ij[:, s], eq[:, s].rearrange("p h c k -> p h k c"), AX.X, ALU.add)
                settle(last)
                settle(dve.tensor_scalar(far[:], ij[:, 1], float(NF), None, ALU.is_ge))
                if q == 0:
                    dve.wait_ge(selT_ready, m + 1)

                def kind(k):
                    return sel[:, p, k, q].rearrange("p (h k) -> p h k", h=PH)
                dve.scalar_tensor_tensor(kind(0), ij[:, 0], 2.0, far[:], ALU.mult, ALU.add)
                settle(dve.scalar_tensor_tensor(r1[:], far[:], -float(NF), ij[:, 1], ALU.mult, ALU.add))
                dve.tensor_scalar(kind(1), r1[:], float(NF * q), None, ALU.add)
                settle(dve.tensor_scalar(w[:], best[:], 0.0, None, ALU.max))
                settle(dve.tensor_copy(kind(2), w[:]))
                settle(dve.tensor_tensor(r1[:], w[:], kind(2), ALU.subtract))
                settle(dve.tensor_copy(kind(3), r1[:]))
                settle(dve.tensor_tensor(r2[:], r1[:], kind(3), ALU.subtract))
                last = dve.tensor_copy(kind(4), r2[:])
                if q == 1:
                    last.then_inc(sel_ready, 1)
                assert n[0] == STEPS, n[0]

            for q in range(2):
                norm(q, 0, q)
            with dve.Fori(0, PAIRS // 2 - 1) as mm:
                for p in range(2):
                    m = mm * 2 + p
                    for q in range(2):
                        norm(m * 2 + 2 + q, m + 1, q)
                        winners(m * 2 + q, m, p, q)
            m = PAIRS - 2
            for q in range(2):
                norm(m * 2 + 2 + q, m + 1, q)
                winners(m * 2 + q, m, 0, q)
            for q in range(2):
                winners(m * 2 + 2 + q, m + 1, 1, q)


def experts(nc, x_in, x_out, mv, xnT_d, sel_d, down_d, up_d, iota_d):
    with ExitStack() as ctx:
        def sb(name, shape, dt=F32):
            return ctx.enter_context(nc.sbuf_tensor("ex_" + name, shape, dt))

        def sem(name):
            return ctx.enter_context(nc.semaphore("ex_" + name))

        def ps(name, shape, dt=F32):
            return ctx.enter_context(nc.psum_tensor("ex_" + name, shape, dt))

        T2 = 2 * P
        NB = P // TB
        NG = P // TG
        BPG = NB // NG
        down, up = sb("down", [P, DC, NF, P]), sb("up", [P, NF, D])
        iota = sb("iota", [P, P, TG], BF16)
        xb = sb("xb", [P, 2, DC, T2])
        hid = sb("hid", [P, 2, NF, T2])
        sel = sb("sel", [P, 2, SEL, P], BF16)
        rows = sb("rows", [P, 2, P, TG], BF16)
        eq = sb("eq", [P, 2 * NF, TG], BF16)
        cols = sb("cols", [P, 2, PARTS, 2 * NF, TG], BF16)
        xr = sb("xr", [P, 2, D])
        xo = sb("xo", [P, 2, D])
        st, ag = sb("st", [P, 2, 6]), sb("ag", [P, 2, 2])
        ps_h, ps_w, ps_o = ps("ps_h", [P, 2, 2, T2]), ps("ps_w", [P, 2, TB, 2, NF]), ps("ps_o", [P, 2, D])

        consts, down_loaded = sem("consts"), sem("down_loaded")
        xb_loaded = [sem(f"xb_loaded{p}") for p in range(2)]
        sel_loaded = [sem(f"sel_loaded{p}") for p in range(2)]
        xr_loaded, stored = sem("xr_loaded"), sem("stored")
        h_ready, hid_ready, one_hot, eq_ready, w_ready, weighted = (sem(n) for n in (
            "h_ready", "hid_ready", "one_hot", "eq_ready", "w_ready", "weighted"))
        out_ready, summed, stats = sem("out_ready"), sem("summed"), sem("stats")
        block = ctx.enter_context(nc.Block())
        HG = NF // 2

        @block.sync
        def _(sp):
            sp.dma_start(down[:], down_d).then_inc(down_loaded, 16)

            def load(m, p):
                sp.dma_start(xb[:, p], xnT_d[m].rearrange("p c q t -> p c (q t)")).then_inc(xb_loaded[p], 16)
                sp.dma_start(sel[:, p], sel_d[m]).then_inc(sel_loaded[p], 16)

            def residual(m):
                for q in range(2):
                    sp.dma_start(xr[:, q, :], x_in[m * 2 + q]).then_inc(xr_loaded, 16)

            def store(m):
                sp.wait_ge(summed, m * 2 + 2)
                for q in range(2):
                    sp.dma_start(x_out[m * 2 + q], xo[:, q, :]).then_inc(stored, 16)

            for p in range(2):
                load(p, p)
            sp.dma_start(iota[:], iota_d).then_inc(consts, 16)
            sp.dma_start(up[:], up_d).then_inc(consts, 16)
            residual(0)
            with sp.Fori(0, PAIRS // 2 - 1) as mm:
                for p in range(2):
                    m = mm * 2 + p
                    sp.wait_ge(out_ready, m + 1)
                    sp.nop(nofuse=True)
                    sp.wait_ge(one_hot, (m + 1) * NG)
                    load(m + 2, p)
                    store(m)
                    residual(m + 1)
            store(PAIRS - 2)
            residual(PAIRS - 1)
            store(PAIRS - 1)
            sp.wait_ge(stored, 16 * TILES)

        @block.tensor
        def _(pe):
            pe.wait_ge(down_loaded, 16)

            def hidden(m, mm, p, g):
                if g == 0:
                    pe.wait_ge(xb_loaded[p], mm * 16 + 16)
                n = m * HG + g
                if not (isinstance(n, int) and n < 2):
                    pe.wait_ge(hid_ready, n - 1)
                for j in range(2):
                    for c in range(DC):
                        last = pe.matmul(ps_h[:, g % 2, j, :], down[:, c, 2 * g + j, :], xb[:, p, c, :],
                                         start=(c == 0), stop=(c == DC - 1))
                last.then_inc(h_ready, 1)

            def weights(m, g):
                n = m * NB + g
                if g % BPG == 0:
                    pe.wait_ge(one_hot, m * NG + g // BPG + 1)
                if not (isinstance(n, int) and n < 2):
                    pe.wait_ge(weighted, n - 1)
                buf = (g // BPG) % 2
                for t in range(TB):
                    at = (g % BPG) * TB + t
                    for k in range(PARTS):
                        last = pe.matmul(ps_w[:, g % 2, t].rearrange("p q f -> p (q f)"), rows[:, buf, :, at],
                                         cols[:, buf, k, :, at], start=(k == 0), stop=(k == PARTS - 1))
                last.then_inc(w_ready, 1)

            def outputs(m, p):
                pe.wait_ge(weighted, (m + 1) * NB)
                if not (isinstance(m, int) and m == 0):
                    pe.wait_ge(summed, m * 2)
                for q in range(2):
                    for f in range(NF):
                        last = pe.matmul(ps_o[:, q, :], hid[:, p, f, q * P:(q + 1) * P], up[:, f, :],
                                         start=(f == 0), stop=(f == NF - 1))
                last.then_inc(out_ready, 1)

            for g in range(HG):
                hidden(0, 0, 0, g)
            pe.wait_ge(consts, 32)
            for g in range(HG):
                hidden(1, 0, 1, g)
                weights(0, g)
            outputs(0, 0)
            with pe.Fori(0, PAIRS // 2 - 1) as mm:
                for p in range(2):
                    m = mm * 2 + 1 + p
                    for g in range(HG):
                        hidden(m + 1, mm + 1, p, g)
                        weights(m, g)
                    outputs(m, 1 - p)
            for g in range(HG):
                weights(PAIRS - 1, g)
            outputs(PAIRS - 1, 1)

        @block.scalar
        def _(act):
            def gelus(m, p):
                if not (isinstance(m, int) and m < 2):
                    act.wait_ge(out_ready, m - 1)
                for g in range(HG):
                    act.wait_ge(h_ready, m * HG + g + 1)
                    act.activation(hid[:, p, 2 * g:2 * g + 2, :], ps_h[:, g % 2], ACT.Gelu).then_inc(hid_ready, 1)

            gelus(0, 0)
            gelus(1, 1)
            with act.Fori(1, PAIRS // 2) as mm:
                for p in range(2):
                    gelus(mm * 2 + p, p)

        @block.vector
        def _(dve):
            dve.wait_ge(consts, 32)

            def expand(m, mm, p, k):
                if k == 0:
                    dve.wait_ge(sel_loaded[p], mm * 16 + 16)
                buf = k % 2
                if not (isinstance(m, int) and m == 0 and k < 2):
                    dve.wait_ge(w_ready, m * NB + (k - 1) * BPG)
                    dve.wait_ge(one_hot, m * NG + k)
                elif k == 1:
                    dve.wait_ge(one_hot, 1)
                at = slice(k * TG, (k + 1) * TG)
                dve.tensor_tensor(rows[:, buf], sel[:, p, 0, at].unsqueeze(1).broadcast_to([P, P, TG]), iota[:],
                                  ALU.is_equal)
                dve.tensor_tensor(eq[:], sel[:, p, 1, at].unsqueeze(1).broadcast_to([P, 2 * NF, TG]),
                                  iota[:, 0:2 * NF, :], ALU.is_equal).then_inc(eq_ready, 1)
                dve.wait_ge(eq_ready, m * NG + k + 1)
                for j in range(PARTS):
                    last = dve.tensor_tensor(cols[:, buf, j], eq[:],
                                             sel[:, p, 2 + j, at].unsqueeze(1).broadcast_to([P, 2 * NF, TG]), ALU.mult)
                last.then_inc(one_hot, 1)

            def weigh(m, p, k):
                if k == 0:
                    dve.wait_ge(hid_ready, m * HG + HG)
                for g in range(k * BPG, (k + 1) * BPG):
                    dve.wait_ge(w_ready, m * NB + g + 1)
                    v = hid[:, p].rearrange("p f (q t) -> p t q f", q=2)[:, g * TB:(g + 1) * TB]
                    dve.tensor_tensor(v, v, ps_w[:, g % 2], ALU.mult).then_inc(weighted, 1)

            def finish(m):
                dve.wait_ge(out_ready, m + 1)
                dve.wait_ge(xr_loaded, m * 32 + 32)
                if not (isinstance(m, int) and m == 0):
                    dve.wait_ge(stored, m * 32)
                for q in range(2):
                    dve.tensor_tensor(xo[:, q, :], ps_o[:, q, :], xr[:, q, :], ALU.add).then_inc(summed, 1)
                dve.wait_ge(summed, m * 2 + 2)
                dve.bn_stats(st[:, 0, :], xo[:, 0, :])
                dve.bn_stats(st[:, 1, :], xo[:, 1, :]).then_inc(stats, 1)
                dve.wait_ge(stats, m * 2 + 1)
                dve.nop(nofuse=True)
                dve.bn_aggr(ag[:, 0, :], st[:, 0, :])
                dve.bn_aggr(ag[:, 1, :], st[:, 1, :]).then_inc(stats, 1)
                dve.wait_ge(stats, m * 2 + 2)
                dve.nop(nofuse=True)
                dve.tensor_copy(mv[:, bass.ds(m * 2, 2), :], ag[:])

            expand(0, 0, 0, 0)
            for k in range(NG):
                expand(*((0, 0, 0, k + 1) if k < NG - 1 else (1, 0, 1, 0)))
                weigh(0, 0, k)
            with dve.Fori(0, PAIRS // 2 - 1) as mm:
                for p in range(2):
                    m = mm * 2 + 1 + p
                    for k in range(NG):
                        if k < NG - 1:
                            expand(m, mm + p, 1 - p, k + 1)
                        else:
                            expand(m + 1, mm + 1, p, 0)
                        if k == 0:
                            finish(m - 1)
                        weigh(m, 1 - p, k)
            m = PAIRS - 1
            for k in range(NG):
                if k < NG - 1:
                    expand(m, PAIRS // 2 - 1, 1, k + 1)
                if k == 0:
                    finish(m - 1)
                weigh(m, 1, k)
            finish(m)


def route(nc, x_in, mv, slots_d, gates, take, wr_d, br_d, upper_d, ident_d, iota_d):
    with ExitStack() as ctx:
        def sb(name, shape, dt=F32):
            return ctx.enter_context(nc.sbuf_tensor("rt_" + name, shape, dt))

        def sem(name):
            return ctx.enter_context(nc.semaphore("rt_" + name))

        def ps(name, shape, dt=F32):
            return ctx.enter_context(nc.psum_tensor("rt_" + name, shape, dt))

        TE = [P, TILES, E8]
        ident, upper, ones = sb("ident", [P, P]), sb("upper", [P, P]), sb("ones", [P, P])
        wr, br = sb("wr", [P, DC, E8]), sb("br", [P, E8])
        iota = sb("iota", [P, E8])
        scale = sb("scale", [P, TILES])
        x, y = sb("x", [P, 2, D]), sb("y", [P, 2, D])
        yall = sb("yall", [P, TILES, D])
        yT = sb("yT", [P, DC, P])
        lg, d, ex, eq, oh, pos, inc = (sb(n, TE) for n in ("lg", "d", "ex", "eq", "oh", "pos", "inc"))
        one_row = sb("one_row", [P, TILES])
        mx, se, first, rank, keep, slot, away = (sb(n, [P, TILES]) for n in (
            "mx", "se", "first", "rank", "keep", "slot", "away"))
        put = sb("put", [P, TILES], U32)
        zero = sb("zero", [P, 8 * D])
        ps_y, ps_l, ps_c = ps("ps_y", [P, BANK]), ps("ps_l", [P, BANK]), ps("ps_c", [P, 2, BANK])

        consts, zeroed, zeros_ready = sem("consts"), sem("zeroed"), sem("zeros_ready")
        x_loaded = [sem(f"x_loaded{p}") for p in range(2)]
        y_ready, yT_ready, yT_copied, l_ready, l_copied, ones_ready = (sem(n) for n in (
            "y_ready", "yT_ready", "yT_copied", "l_ready", "l_copied", "ones_ready"))
        chain, d_ready, ex_ready, oh_ready, counted, put_ready, gated, scattered = (sem(n) for n in (
            "chain", "d_ready", "ex_ready", "oh_ready", "counted", "put_ready", "gated", "scattered"))
        scale_dve, scale_act = row_scale(nc, ctx, None, mv, scale, False, "rt_ln")
        block = ctx.enter_context(nc.Block())
        NZ = E8 * CAP // (8 * P)

        @block.sync
        def _(sp):
            for dst, src in ((ident, ident_d), (upper, upper_d), (wr, wr_d), (br, br_d), (iota, iota_d)):
                sp.dma_start(dst[:], src).then_inc(consts, 16)
            for p in range(2):
                sp.dma_start(x[:, p, :], x_in[p]).then_inc(x_loaded[p], 16)
            sp.wait_ge(zeros_ready, 1)
            for z in range(NZ):
                sp.dma_start(slots_d[z * 8 * P:(z + 1) * 8 * P, :].rearrange("(p r) d -> p (r d)", p=P),
                             zero[:]).then_inc(zeroed, 16)
            with sp.Fori(0, TILES // 2 - 1) as t:
                for p in range(2):
                    i = t * 2 + p
                    sp.wait_ge(y_ready, i + 1)
                    sp.nop(nofuse=True)
                    sp.dma_start(x[:, p, :], x_in[i + 2]).then_inc(x_loaded[p], 16)

        @block.gpsimd
        def _(pool):
            pool.memset(zero[:], 0.0).then_inc(zeros_ready, 1)
            pool.wait_ge(zeroed, 16 * NZ)
            pool.wait_ge(put_ready, 1)
            for i in range(TILES):
                pool.wait_ge(gated, i + 1)
                pool.indirect_dma_start(slots_d, bass.IndirectOffsetOnAxis(ap=put[:, i:i + 1], axis=0),
                                        yall[:, i, :], None, bounds_check=E8 * CAP - 1,
                                        oob_is_err=False).then_inc(scattered, 16)
            pool.wait_ge(scattered, 16 * TILES)

        @block.tensor
        def _(pe):
            pe.wait_ge(consts, 16 * 5)

            def tile(i, p):
                pe.wait_ge(y_ready, i + 1)
                for k in range(DC):
                    last = pe.transpose(ps_y[:, k * P:(k + 1) * P], y[:, p, k * P:(k + 1) * P], ident[:])
                last.then_inc(yT_ready, 1)
                pe.wait_ge(yT_copied, i + 1)
                if not (isinstance(i, int) and i == 0):
                    pe.wait_ge(l_copied, i)
                for k in range(DC):
                    last = pe.matmul(ps_l[:, 0:E8], yT[:, k, :], wr[:, k, :], start=(k == 0), stop=(k == DC - 1))
                last.then_inc(l_ready, 1)

            for p in range(2):
                tile(p, p)
            with pe.Fori(1, TILES // 2) as t:
                for p in range(2):
                    tile(t * 2 + p, p)
            pe.wait_ge(ones_ready, 1)
            pe.wait_ge(oh_ready, 1)
            flat = oh[:].rearrange("p t e -> p (t e)")
            pe.matmul(ps_c[:, 0, 0:TILES * E8], upper[:], flat, start=True, stop=True)
            pe.matmul(ps_c[:, 1, 0:TILES * E8], ones[:], flat, start=True, stop=True).then_inc(counted, 1)

        @block.scalar
        def _(act):
            scale_act(act)

            def tile(i):
                act.wait_ge(yT_ready, i + 1)
                act.activation(yT[:], ps_y[:, 0:D].rearrange("p (c t) -> p c t", c=DC), ACT.Copy).then_inc(yT_copied, 1)
                act.wait_ge(l_ready, i + 1)
                act.nop(nofuse=True)
                act.activation(lg[:, bass.ds(i, 1), :], ps_l[:, 0:E8].unsqueeze(1), ACT.Copy).then_inc(l_copied, 1)

            with act.Fori(0, TILES) as i:
                tile(i)
            act.wait_ge(d_ready, 1)
            act.activation(ex[:], d[:], ACT.Exp).then_inc(ex_ready, 1)

        @block.vector
        def _(dve):
            scale_dve(dve)
            dve.memset(one_row[:], 1.0)
            dve.memset(ones[:], 1.0).then_inc(ones_ready, 1)

            def tile(i, t, p):
                dve.wait_ge(x_loaded[p], t * 16 + 16)
                if not (isinstance(i, int) and i < 2):
                    dve.wait_ge(yT_ready, i - 1)
                dve.nop(nofuse=True)
                dve.tensor_scalar(yall[:, bass.ds(i, 1), :], x[:, p, :].unsqueeze(1), mv[:, bass.ds(i, 1), 0],
                                  scale[:, bass.ds(i, 1)], ALU.subtract, ALU.mult)
                dve.tensor_scalar(y[:, p, :], x[:, p, :], mv[:, bass.ds(i, 1), 0],
                                  scale[:, bass.ds(i, 1)], ALU.subtract, ALU.mult).then_inc(y_ready, 1)

            for p in range(2):
                tile(p, 0, p)
            with dve.Fori(1, TILES // 2) as t:
                for p in range(2):
                    tile(t * 2 + p, t, p)
            dve.wait_ge(l_copied, TILES)
            dve.wait_ge(consts, 16 * 5)
            n = [0]

            def settle(ins):
                n[0] += 1
                ins.then_inc(chain, 1)
                dve.wait_ge(chain, n[0])

            def over_experts(a):
                return a[:].unsqueeze(2).broadcast_to(TE)

            iota_b = iota[:].unsqueeze(1).broadcast_to(TE)
            settle(dve.tensor_tensor(lg[:], lg[:], br[:].unsqueeze(1).broadcast_to(TE), ALU.add))
            settle(dve.tensor_reduce(mx[:], lg[:], AX.X, ALU.max))
            dve.tensor_tensor(d[:], lg[:], over_experts(mx), ALU.subtract).then_inc(d_ready, 1)
            dve.wait_ge(d_ready, 1)
            settle(dve.tensor_scalar(eq[:], d[:], 0.0, None, ALU.is_equal))
            settle(dve.tensor_tensor(eq[:], eq[:], iota_b, ALU.mult))
            settle(dve.tensor_reduce(first[:], eq[:], AX.X, ALU.min))
            dve.tensor_tensor(oh[:], over_experts(first), iota_b, ALU.is_equal).then_inc(oh_ready, 1)
            dve.wait_ge(ex_ready, 1)
            settle(dve.tensor_reduce(se[:], ex[:], AX.X, ALU.add))
            settle(dve.reciprocal(gates[:], se[:]))
            dve.wait_ge(counted, 1)
            totals = ps_c[:, 1, 0:TILES * E8].rearrange("p (t e) -> p t e", e=E8)
            settle(dve.tensor_copy(pos[:], totals))
            for e in range(E8):
                last = dve.tensor_tensor_scan(inc[:, :, e], one_row[:], pos[:, :, e], 0.0, ALU.mult, ALU.add)
            settle(last)
            settle(dve.tensor_tensor(inc[:], inc[:], pos[:], ALU.subtract))
            settle(dve.tensor_tensor(pos[:], inc[:], ps_c[:, 0, 0:TILES * E8].rearrange("p (t e) -> p t e", e=E8), ALU.add))
            settle(dve.tensor_tensor(pos[:], pos[:], oh[:], ALU.mult))
            settle(dve.tensor_reduce(rank[:], pos[:], AX.X, ALU.add))
            settle(dve.tensor_scalar(keep[:], rank[:], float(CAP), None, ALU.is_lt))
            settle(dve.tensor_scalar(first[:], first[:], float(E8), float(CAP), ALU.add, ALU.mult))
            settle(dve.tensor_tensor(slot[:], first[:], rank[:], ALU.add))
            settle(dve.tensor_tensor(gates[:], gates[:], keep[:], ALU.mult))
            settle(dve.tensor_tensor(slot[:], slot[:], keep[:], ALU.mult))
            dve.tensor_copy(take[:], slot[:])
            settle(dve.tensor_scalar(away[:], keep[:], -float(4 * N), float(4 * N), ALU.mult, ALU.add))
            settle(dve.tensor_tensor(away[:], away[:], slot[:], ALU.add))
            dve.tensor_copy(put[:], away[:]).then_inc(put_ready, 1)
            for i in range(TILES):
                dve.tensor_scalar(yall[:, i, :], yall[:, i, :], gates[:, i:i + 1], None, ALU.mult).then_inc(gated, 1)


def routed_experts(nc, slots_d, eo_d, w1_d, b1_d, w2_d, b2_d, ident_d):
    with ExitStack() as ctx:
        def sb(name, shape, dt=F32):
            return ctx.enter_context(nc.sbuf_tensor("re_" + name, shape, dt))

        def sem(name):
            return ctx.enter_context(nc.semaphore("re_" + name))

        def ps(name, shape, dt=F32):
            return ctx.enter_context(nc.psum_tensor("re_" + name, shape, dt))

        ST = CAP // P
        ident, b1 = sb("ident", [P, P]), sb("b1", [P, E8, DC])
        w1, w2, b2 = sb("w1", [P, 2, DC, D]), sb("w2", [P, 2, DC, D]), sb("b2", [P, 2, D])
        ei, eT, hT, eo = sb("ei", [P, 2, ST, D]), sb("eT", [P, DC, CAP]), sb("hT", [P, DC, CAP]), sb("eo", [P, 2, ST, D])
        ps_t, ps_h, ps_e = ps("ps_t", [P, DC, CAP]), ps("ps_h", [P, DC, CAP]), ps("ps_e", [P, ST, D])
        consts = sem("consts")
        loaded = [sem(f"loaded{p}") for p in range(2)]
        stored = [sem(f"stored{p}") for p in range(2)]
        t_ready, t_copied, h_ready, h_copied, e_ready, e_copied = (sem(n) for n in (
            "t_ready", "t_copied", "h_ready", "h_copied", "e_ready", "e_copied"))
        block = ctx.enter_context(nc.Block())

        @block.sync
        def _(sp):
            for dst, src in ((ident, ident_d), (b1, b1_d)):
                sp.dma_start(dst[:], src).then_inc(consts, 16)
            for e in range(E8):
                p = e % 2
                if e >= 2:
                    sp.wait_ge(e_copied, e - 1)
                sp.dma_start(ei[:, p], slots_d[e * CAP:(e + 1) * CAP, :].rearrange("(s p) d -> p s d", p=P)).then_inc(loaded[p], 16)
                sp.dma_start(w1[:, p], w1_d[e]).then_inc(loaded[p], 16)
                sp.dma_start(w2[:, p], w2_d[e]).then_inc(loaded[p], 16)
                sp.dma_start(b2[:, p], b2_d[e]).then_inc(loaded[p], 16)

        @block.tensor
        def _(pe):
            pe.wait_ge(consts, 32)
            for e in range(E8):
                p = e % 2
                pe.wait_ge(loaded[p], 64 * (e // 2 + 1))
                for k in range(DC):
                    for s in range(ST):
                        last = pe.transpose(ps_t[:, k, s * P:(s + 1) * P], ei[:, p, s, k * P:(k + 1) * P], ident[:])
                last.then_inc(t_ready, 1)
                pe.wait_ge(t_copied, e + 1)
                for f in range(DC):
                    for k in range(DC):
                        last = pe.matmul(ps_h[:, f, :], w1[:, p, k, f * P:(f + 1) * P], eT[:, k, :],
                                         start=(k == 0), stop=(k == DC - 1))
                last.then_inc(h_ready, 1)
                pe.wait_ge(h_copied, e + 1)
                if e >= 1:
                    pe.wait_ge(e_copied, e)
                for s in range(ST):
                    for f in range(DC):
                        last = pe.matmul(ps_e[:, s, :], hT[:, f, s * P:(s + 1) * P], w2[:, p, f, :],
                                         start=(f == 0), stop=(f == DC - 1))
                last.then_inc(e_ready, 1)

        @block.scalar
        def _(act):
            for e in range(E8):
                p = e % 2
                act.wait_ge(t_ready, e + 1)
                act.activation(eT[:], ps_t[:], ACT.Copy).then_inc(t_copied, 1)
                act.wait_ge(h_ready, e + 1)
                for f in range(DC):
                    last = act.activation(hT[:, f, :], ps_h[:, f, :], ACT.Relu, bias=b1[:, e, f:f + 1])
                last.then_inc(h_copied, 1)
                act.wait_ge(e_copied, e + 1)
                act.dma_start(eo_d[e * CAP:(e + 1) * CAP, :].rearrange("(s p) d -> p s d", p=P), eo[:, p]).then_inc(stored[p], 16)
            for p in range(2):
                act.wait_ge(stored[p], 16 * (E8 // 2))

        @block.vector
        def _(dve):
            for e in range(E8):
                p = e % 2
                dve.wait_ge(e_ready, e + 1)
                if e >= 2:
                    dve.wait_ge(stored[p], 16 * (e // 2))
                dve.tensor_tensor(eo[:, p], ps_e[:], b2[:, p].unsqueeze(1).broadcast_to([P, ST, D]), ALU.add).then_inc(e_copied, 1)


def combine(nc, x_in, out, eo_d, gates, take):
    with ExitStack() as ctx:
        R = 4
        x = ctx.enter_context(nc.sbuf_tensor("cb_x", [P, TILES, D], F32))
        row = ctx.enter_context(nc.sbuf_tensor("cb_row", [P, R, D], F32))
        x_loaded = [ctx.enter_context(nc.semaphore(f"cb_x_loaded{g}")) for g in range(4)]
        row_loaded = [ctx.enter_context(nc.semaphore(f"cb_row_loaded{r}")) for r in range(R)]
        summed = ctx.enter_context(nc.semaphore("cb_summed"))
        stored = ctx.enter_context(nc.semaphore("cb_stored"))
        block = ctx.enter_context(nc.Block())
        G = TILES // 4

        @block.sync
        def _(sp):
            for g in range(4):
                sp.dma_start(x[:, g * G:(g + 1) * G, :],
                             x_in[g * G:(g + 1) * G].rearrange("t p d -> p t d")).then_inc(x_loaded[g], 16)
            for g in range(8):
                n = TILES // 8
                sp.wait_ge(summed, (g + 1) * n)
                sp.dma_start(out[g * n:(g + 1) * n].rearrange("t p d -> p t d"), x[:, g * n:(g + 1) * n, :]).then_inc(stored, 16)
            sp.wait_ge(stored, 16 * 8)

        @block.gpsimd
        def _(pool):
            for i in range(TILES):
                if i >= R:
                    pool.wait_ge(summed, i - R + 1)
                pool.indirect_dma_start(row[:, i % R, :], None, eo_d,
                                        bass.IndirectOffsetOnAxis(ap=take[:, i:i + 1], axis=0)).then_inc(row_loaded[i % R], 16)

        @block.vector
        def _(dve):
            for i in range(TILES):
                if i % G == 0:
                    dve.wait_ge(x_loaded[i // G], 16)
                dve.wait_ge(row_loaded[i % R], 16 * (i // R + 1))
                dve.scalar_tensor_tensor(x[:, i, :], row[:, i % R, :], gates[:, i:i + 1], x[:, i, :],
                                         ALU.mult, ALU.add).then_inc(summed, 1)


def program(nc, x, ctxT, mask, a0, a1, pk, me, c, out):
    def rows(name):
        return nc.dram_tensor(name, [TILES, P, D], F32).ap()

    x1, x2, x3 = rows("x1"), rows("x2"), rows("x3")
    xnT_d = nc.dram_tensor("xnT_d", [PAIRS, P, DC, 2, P], F32).ap()
    sel_d = nc.dram_tensor("sel_d", [PAIRS, P, SEL, P], BF16).ap()
    slots_d = nc.dram_tensor("slots_d", [E8 * CAP, D], F32).ap()
    eo_d = nc.dram_tensor("eo_d", [E8 * CAP, D], F32).ap()
    with ExitStack() as ctx:
        mv = ctx.enter_context(nc.sbuf_tensor("mv", [P, TILES, 2], F32))
        gates = ctx.enter_context(nc.sbuf_tensor("gates", [P, TILES], F32))
        take = ctx.enter_context(nc.sbuf_tensor("take", [P, TILES], U32))
        first_stats(nc, x, mv[:])
        attention(nc, "a0", x, x1, mv[:], ctxT, *a0, c["bmask"], c["ident"])
        product_keys(nc, x1, mv[:], xnT_d, sel_d, pk["w_q"], pk["keysT"], pk["norm_w"], c["ident"], c["identb"], c["iota8"])
        experts(nc, x1, x2, mv[:], xnT_d, sel_d, pk["down"], pk["up"], c["iota"])
        attention(nc, "a1", x2, x3, mv[:], ctxT, *a1[:4], c["bmask"], c["ident"],
                  rope=(a1[4], a1[5], c["cos"], c["sin"]), mask=mask)
        route(nc, x3, mv[:], slots_d, gates, take, me["wr"], me["br"], c["upper"], c["ident"], c["iota_e"])
        routed_experts(nc, slots_d, eo_d, me["w1"], me["b1"], me["w2"], me["b2"], c["ident"])
        combine(nc, x3, out, eo_d, gates, take)


def layouts(np, a):
    def rowchunks(w):
        return w.reshape(DC, P, -1).transpose(1, 0, 2)

    def halves_exchanged(w):
        return w.reshape(H, 2, DK // 2, D)[:, ::-1].reshape(D, D)

    L0, L1 = "L0_xattn_W_", "L1_xattn_W_"
    return {
        "x": a["x"].reshape(TILES, P, D),
        "ctxT": rowchunks(a["ctx_1024"].transpose(2, 0, 1).reshape(D, B * SK)),
        "mask": a["mask_Bx1xSxS2_ik0"].reshape(TILES, P, SK),
        **{f"a0_{n}": rowchunks(a[L0 + n].T) for n in "qkvo"},
        **{f"a1_{n}": rowchunks(a[L1 + n].T) for n in "qkvo"},
        **{f"a1_{n}r": rowchunks(halves_exchanged(a[L1 + n]).T) for n in "qk"},
        "w_q": a["L0_ffn_w_q"].reshape(2 * PH, P, D).transpose(1, 0, 2),
        "keysT": a["L0_ffn_keys"].transpose(3, 0, 2, 1).reshape(P, 2 * PH, NKEYS),
        "norm_w": a["L0_ffn_norm_w"].reshape(DC, P).T,
        "down": a["L0_ffn_expert_down"].reshape(P, NF, DC, P).transpose(3, 2, 1, 0),
        "up": a["L0_ffn_expert_up"].reshape(P, NF, D),
        "wr": rowchunks(a["L1_ffn_Wr"]),
        "br": np.broadcast_to(a["L1_ffn_br"][None], (P, E8)),
        "w1": a["L1_ffn_W1"].reshape(E8, DC, P, D).transpose(0, 2, 1, 3),
        "b1": a["L1_ffn_b1"].reshape(E8, DC, P).transpose(2, 0, 1),
        "w2": a["L1_ffn_W2"].reshape(E8, DC, P, D).transpose(0, 2, 1, 3),
        "b2": np.broadcast_to(a["L1_ffn_b2"][:, None], (E8, P, D)),
    }


def constants(np, bf16):
    inv = (1.0 / 10000.0 ** (np.arange(0, DK, 2, dtype=np.float32) / DK)).astype(np.float32)
    angle = np.outer(inv, np.arange(S, dtype=np.float32)).astype(np.float32)
    cos, sin = np.cos(angle), np.sin(angle)
    eye = np.eye(P, dtype=np.float32)
    return {
        "bmask": np.repeat(np.eye(HU, dtype=np.float32), DK, axis=0),
        "ident": eye,
        "identb": eye.astype(bf16),
        "iota8": np.broadcast_to(np.arange(TOPK, dtype=np.float32)[None, :, None], (P, TOPK, TOPK)),
        "iota": np.broadcast_to(np.arange(P, dtype=np.float32)[None, :, None], (P, P, TG)).astype(bf16),
        "iota_e": np.broadcast_to(np.arange(E8, dtype=np.float32)[None] - E8, (P, E8)),
        "upper": np.triu(np.ones((P, P), np.float32)),
        "cos": np.tile(np.concatenate([cos, cos]), (HU, 1)).astype(np.float32),
        "sin": np.tile(np.concatenate([-sin, sin]), (HU, 1)).astype(np.float32),
    }


def kernel(**inputs):
    import ml_dtypes
    import numpy as np
    import concourse.bacc as bacc
    from concourse.bass_utils import run_bass_kernel_spmd as run

    a = layouts(np, {k: np.asarray(v) for k, v in inputs.items()})
    c = constants(np, ml_dtypes.bfloat16)
    nc = bacc.Bacc("TRN2", target_bir_lowering=False, num_devices=1)
    arrays, aps = {}, {}
    for name, v in {**a, **c}.items():
        v = np.ascontiguousarray(v)
        arrays[f"in_{name}"] = v
        aps[name] = nc.dram_tensor(f"in_{name}", v.shape, mybir.dt.from_np(v.dtype), kind="ExternalInput").ap()
    out = nc.dram_tensor("out", [TILES, P, D], F32, kind="ExternalOutput").ap()
    program(nc, aps["x"], aps["ctxT"], aps["mask"],
            [aps[f"a0_{n}"] for n in "qkvo"],
            [aps[f"a1_{n}"] for n in "qkvo"] + [aps["a1_qr"], aps["a1_kr"]],
            aps, aps, aps, out)
    r = run(nc, [arrays], core_ids=[0])
    return r.results[0]["out"].reshape(B, S, D)
```

```python
from contextlib import ExitStack

import concourse.bass as bass
from concourse import mybir

F32 = mybir.dt.float32
BF16 = mybir.dt.bfloat16
I32 = mybir.dt.int32
U32 = mybir.dt.uint32
ALU = mybir.AluOpType
ACT = mybir.ActivationFunctionType
AX = mybir.AxisListType

P = 128
D = 256
DC = D // P
B, S, SK = 4, 1024, 77
N = B * S
TILES = N // P
TPB = S // P
H, DK = 16, 16
HU = H // 2
GRP = 4
BANK = 512
LN_EPS = 1e-5
RMS_EPS = 1e-6
PH, NKEYS, TOPK = 8, 64, 8
E8, CAP = 8, N // 8


def row_scale(nc, ctx, block, mv, scale, rms, name):
    var = mv[:, :, 1]
    a = ctx.enter_context(nc.sbuf_tensor(name + "_a", [P, TILES], F32))
    root = ctx.enter_context(nc.sbuf_tensor(name + "_root", [P, TILES], F32))
    r = ctx.enter_context(nc.sbuf_tensor(name + "_r", [P, TILES], F32))
    t = ctx.enter_context(nc.sbuf_tensor(name + "_t", [P, TILES], F32))
    a_ready = ctx.enter_context(nc.semaphore(name + "_a_ready"))
    root_ready = ctx.enter_context(nc.semaphore(name + "_root_ready"))
    step = ctx.enter_context(nc.semaphore(name + "_step"))
    rounds = 2 if rms else 1

    def on_vector(dve):
        n = 0
        for k in range(rounds):
            if k == 0:
                dve.tensor_scalar(a[:], var, LN_EPS, None, ALU.add).then_inc(a_ready, 1)
            else:
                dve.tensor_tensor(t[:], scale[:], scale[:], ALU.mult).then_inc(step, 1)
                n += 1
                dve.wait_ge(step, n)
                dve.tensor_tensor(t[:], t[:], var, ALU.mult).then_inc(step, 1)
                n += 1
                dve.wait_ge(step, n)
                dve.tensor_scalar(a[:], t[:], RMS_EPS, None, ALU.add).then_inc(a_ready, 1)
            dve.wait_ge(root_ready, k + 1)
            dve.reciprocal(r[:], root[:]).then_inc(step, 1)
            n += 1
            dve.wait_ge(step, n)
            dve.tensor_tensor(t[:], r[:], r[:], ALU.mult).then_inc(step, 1)
            n += 1
            dve.wait_ge(step, n)
            dve.wait_ge(a_ready, k + 1)
            dve.tensor_tensor(t[:], t[:], a[:], ALU.mult).then_inc(step, 1)
            n += 1
            dve.wait_ge(step, n)
            dve.tensor_scalar(t[:], t[:], -0.5, 1.5, ALU.mult, ALU.add).then_inc(step, 1)
            n += 1
            dve.wait_ge(step, n)
            if k == 0:
                dve.tensor_tensor(scale[:], r[:], t[:], ALU.mult).then_inc(step, 1)
            else:
                dve.tensor_tensor(r[:], r[:], t[:], ALU.mult).then_inc(step, 1)
                n += 1
                dve.wait_ge(step, n)
                dve.tensor_tensor(scale[:], scale[:], r[:], ALU.mult).then_inc(step, 1)
            n += 1
            dve.wait_ge(step, n)

    def on_scalar(act):
        for k in range(rounds):
            act.wait_ge(a_ready, k + 1)
            act.activation(root[:], a[:], ACT.Sqrt).then_inc(root_ready, 1)

    return on_vector, on_scalar


def first_stats(nc, x_in, mv):
    with ExitStack() as ctx:
        x = ctx.enter_context(nc.sbuf_tensor("fs_x", [P, TILES, D], F32))
        st = ctx.enter_context(nc.sbuf_tensor("fs_st", [P, TILES, 6], F32))
        loaded = [ctx.enter_context(nc.semaphore(f"fs_loaded{g}")) for g in range(4)]
        sums_ready = ctx.enter_context(nc.semaphore("fs_sums_ready"))
        block = ctx.enter_context(nc.Block())
        G = TILES // 4

        @block.sync
        def _(sp):
            for g in range(4):
                sp.dma_start(x[:, g * G:(g + 1) * G, :],
                             x_in[g * G:(g + 1) * G].rearrange("t p d -> p t d")).then_inc(loaded[g], 16)

        @block.vector
        def _(dve):
            for t in range(TILES):
                if t % G == 0:
                    dve.wait_ge(loaded[t // G], 16)
                dve.bn_stats(st[:, t, :], x[:, t, :]).then_inc(sums_ready, 1)
            for t in range(TILES):
                dve.wait_ge(sums_ready, t + 1)
                dve.bn_aggr(mv[:, t, :], st[:, t, :])


def attention(nc, tag, x_in, x_out, mv, ctxT, wqT, wkT, wvT, woT, bmask, ident_d, rope=None, mask=None,
              identb_d=None):
    with ExitStack() as ctx:
        def sb(name, shape, dt=F32):
            return ctx.enter_context(nc.sbuf_tensor(f"{tag}_{name}", shape, dt))

        def sem(name):
            return ctx.enter_context(nc.semaphore(f"{tag}_{name}"))

        QU = H // GRP
        ident = sb("ident", [P, P])
        bm = sb("bm", [P, HU])
        cT = sb("cT", [P, DC, B * SK])
        wq, wk, wv, wo = (sb(n, [P, DC, D]) for n in ("wq", "wk", "wv", "wo"))
        keys_bd = sb("keys_bd", [P, DC, B, HU, SK])
        vals = sb("vals", [SK, B, H, DK + 1])
        scale = sb("scale", [P, TILES])
        xa = sb("xa", [P, 2, D])
        xr = sb("xr", [P, 2, D])
        xo = sb("xo", [P, 2, D])
        y = sb("y", [P, 2, D])
        yoT = sb("yoT", [P, 2, DC, P])
        qT = sb("qT", [P, 2, DC, P])
        pr = sb("pr", [P, 2, QU, GRP, SK])
        mx = sb("mx", [P, 2, QU, GRP])
        pT = sb("pT", [SK, 2, GRP, P])
        rs = sb("rs", [P, H])
        o = sb("o", [P, D])
        st = sb("st", [P, 6])
        ag = sb("ag", [P, 2])
        if rope:
            wqr, wkr = sb("wqr", [P, DC, D]), sb("wkr", [P, DC, D])
            cos, sin = sb("cos", [P, S]), sb("sin", [P, S])
            rk = sb("rk", [P, B, SK])
            rt = sb("rt", [P, 2, DC, P])
        if mask is not None:
            mi = sb("mi", [P, 2, SK], I32)
            mb = sb("mb", [P, 2, SK], BF16)
            identb = sb("identb", [P, P], BF16)

        def ps(name, shape):
            return ctx.enter_context(nc.psum_tensor(f"{tag}_{name}", shape, F32))

        ps_s = ps("ps_s", [P, 2, BANK])
        ps_t = ps("ps_t", [P, 2, GRP, P])
        ps_m = ps("ps_m", [P, 2, DC, P])
        ps_q = ps("ps_q", [P, 2, DC, P])
        ps_v = ps("ps_v", [P, BANK])
        ps_w = ps("ps_w", [P, BANK])

        consts = sem("consts")
        proj_ready, proj_used, dve_setup, setup_done = (sem(n) for n in (
            "proj_ready", "proj_used", "dve_setup", "setup_done"))
        xa_loaded = [sem(f"xa_loaded{p}") for p in range(2)]
        xr_loaded = [sem(f"xr_loaded{p}") for p in range(2)]
        stored = [sem(f"stored{p}") for p in range(2)]
        y_ready, yo_ready, yo_copied, q_ready, turned, q_copied = (sem(n) for n in (
            "y_ready", "yo_ready", "yo_copied", "q_ready", "turned", "q_copied"))
        s_ready, max_ready, sub_ready, p_ready, pT_ready, pT_copied = (sem(n) for n in (
            "s_ready", "max_ready", "sub_ready", "p_ready", "pT_ready", "pT_copied"))
        av_ready, sum_inv, o_ready, out_ready, res_done, stats = (sem(n) for n in (
            "av_ready", "sum_inv", "o_ready", "out_ready", "res_done", "stats"))

        scale_dve, scale_act = row_scale(nc, ctx, None, mv, scale, False, tag + "_ln")
        NCONST = 7 + (4 if rope else 0) + (1 if mask is not None else 0)
        NXA = 16 * (2 if mask is not None else 1)
        FIRST, LAST = 2, TILES - 5

        def inside(k):
            return not isinstance(k, int) or 0 <= k < TILES

        def steps(eng, step):
            for i in range(-3, FIRST):
                step(i, 0, i)
            with eng.Fori(FIRST // 2, (LAST + 1) // 2) as t:
                for c in range(2):
                    step(t * 2 + c, t, c)
            for i in range(LAST + 1, TILES + 1):
                step(i, 0, i)

        block = ctx.enter_context(nc.Block())

        @block.sync
        def _(sp):
            sp.dma_start(cT[:], ctxT).then_inc(consts, 16)
            sp.dma_start(wk[:], wkT).then_inc(consts, 16)
            sp.dma_start(wv[:], wvT).then_inc(consts, 16)
            sp.dma_start(wq[:], wqT).then_inc(consts, 16)
            sp.dma_start(wo[:], woT).then_inc(consts, 16)
            sp.dma_start(bm[:], bmask).then_inc(consts, 16)
            sp.dma_start(ident[:], ident_d).then_inc(consts, 16)
            if rope:
                sp.dma_start(wqr[:], rope[0]).then_inc(consts, 16)
                sp.dma_start(wkr[:], rope[1]).then_inc(consts, 16)
                sp.dma_start(cos[:], rope[2]).then_inc(consts, 16)
                sp.dma_start(sin[:], rope[3]).then_inc(consts, 16)
            if mask is not None:
                sp.dma_start(identb[:], identb_d).then_inc(consts, 16)

            def store(i, p):
                sp.wait_ge(res_done, i + 1)
                sp.nop(nofuse=True)
                sp.dma_start(x_out[i], xo[:, p, :]).then_inc(stored[p], 16)

            for p in range(2):
                sp.sem_inc(stored[p], 16)
                sp.dma_start(xr[:, p, :], x_in[p]).then_inc(xr_loaded[p], 16)
            with sp.Fori(0, TILES // 2 - 1) as t:
                for p in range(2):
                    i = t * 2 + p
                    store(i, p)
                    sp.dma_start(xr[:, p, :], x_in[i + 2]).then_inc(xr_loaded[p], 16)
            for p in range(2):
                store(TILES - 2 + p, p)
            for p in range(2):
                sp.wait_ge(stored[p], 16 * (TILES // 2 + 1))

        @block.gpsimd
        def _(pool):
            def load(i, p):
                pool.dma_start(xa[:, p, :], x_in[i]).then_inc(xa_loaded[p], 16)
                if mask is not None:
                    pool.dma_start(mi[:, p, :], mask[i]).then_inc(xa_loaded[p], 16)

            for p in range(2):
                load(p, p)
            with pool.Fori(0, TILES // 2 - 1) as t:
                for p in range(2):
                    i = t * 2 + p
                    pool.wait_ge(y_ready, i + 1)
                    pool.nop(nofuse=True)
                    load(i + 2, p)

        @block.tensor
        def _(pe):
            pe.wait_ge(consts, 16 * NCONST)
            n = 0
            for c in range(DC):
                for w in ((wk, wkr) if rope else (wk,)):
                    if n >= 2:
                        pe.wait_ge(proj_used, n - 1)
                    for k in range(DC):
                        last = pe.matmul(ps_s[:, n % 2, 0:B * SK], w[:, k, c * P:(c + 1) * P], cT[:, k, :],
                                         start=(k == 0), stop=(k == DC - 1))
                    last.then_inc(proj_ready, 1)
                    n += 1
            for b in range(B):
                if n >= 2:
                    pe.wait_ge(proj_used, n - 1)
                for k in range(DC):
                    last = pe.matmul(ps_s[0:SK, n % 2, 0:D], cT[:, k, b * SK:(b + 1) * SK], wv[:, k, :],
                                     start=(k == 0), stop=(k == DC - 1))
                last.then_inc(proj_ready, 1)
                n += 1
            pe.wait_ge(setup_done, 1)

            def scores(j, p, k):
                if not inside(j):
                    return
                if k == 0:
                    pe.wait_ge(q_copied, j + 1)
                if not (isinstance(j, int) and 4 * j + k < 2):
                    pe.wait_ge(sub_ready, j * QU + k - 1)
                bank = ps_s[:, k % 2, 0:GRP * SK]
                if mask is not None:
                    pe.matmul(bank, identb[:], mb[:, p, :].unsqueeze(1).broadcast_to([P, GRP, SK]), start=True, stop=False)
                pe.matmul(bank, qT[:, p, k // 2, :], keys_bd[:, k // 2, j // TPB, (k % 2) * GRP:(k % 2 + 1) * GRP, :],
                          start=(mask is None), stop=True).then_inc(s_ready, 1)

            def transposed_weights(i, p, k):
                if not inside(i):
                    return
                if k % 2 == 0:
                    pe.wait_ge(p_ready, i * 2 + k // 2 + 1)
                for h in range(GRP):
                    last = pe.transpose(ps_t[0:SK, k % 2, h, :], pr[:, p, k, h, :], ident[:])
                last.then_inc(pT_ready, 1)

            def weighted_values(i, k):
                if not inside(i):
                    return
                pe.wait_ge(pT_copied, i * QU + k + 1)
                if k == 0 and not (isinstance(i, int) and i == 0):
                    pe.wait_ge(o_ready, i)
                for h in range(GRP):
                    g = k * GRP + h
                    last = pe.matmul(ps_v[:, g * (DK + 1):(g + 1) * (DK + 1)], pT[:, k % 2, h, :],
                                     vals[:, i // TPB, g, :], start=True, stop=True)
                if k == QU - 1:
                    last.then_inc(av_ready, 1)

            def step(i, t, c):
                if isinstance(i, int) and i == -3:
                    return
                scores(i + 1, (c + 1) % 2, 0)
                transposed_weights(i, c % 2, 0)
                if inside(i + 2):
                    pe.wait_ge(y_ready, i + 3)
                    for k in range(DC):
                        last = pe.transpose(ps_m[:, 0, k, :], y[:, c % 2, k * P:(k + 1) * P], ident[:])
                if inside(i - 1):
                    pe.wait_ge(o_ready, i)
                    for k in range(DC):
                        last = pe.transpose(ps_m[:, 1, k, :], o[:, k * P:(k + 1) * P], ident[:])
                last.then_inc(yo_ready, 1)
                transposed_weights(i, c % 2, 1)
                scores(i + 1, (c + 1) % 2, 1)
                weighted_values(i, 0)
                transposed_weights(i, c % 2, 2)
                pe.wait_ge(yo_copied, i + 3)
                if inside(i + 2):
                    if not (isinstance(i, int) and i == -2):
                        pe.wait_ge(q_copied, i + 2)
                    for r, w in enumerate((wq, wqr) if rope else (wq,)):
                        for m in range(DC):
                            for k in range(DC):
                                last = pe.matmul(ps_q[:, r, m, :], w[:, k, m * P:(m + 1) * P], yoT[:, 0, k, :],
                                                 start=(k == 0), stop=(k == DC - 1))
                    last.then_inc(q_ready, 1)
                scores(i + 1, (c + 1) % 2, 2)
                weighted_values(i, 1)
                transposed_weights(i, c % 2, 3)
                if inside(i - 1):
                    if not (isinstance(i, int) and i == 1):
                        pe.wait_ge(res_done, i - 1)
                    for k in range(DC):
                        last = pe.matmul(ps_w[:, 0:D], yoT[:, 1, k, :], wo[:, k, :], start=(k == 0), stop=(k == DC - 1))
                    last.then_inc(out_ready, 1)
                scores(i + 1, (c + 1) % 2, 3)
                weighted_values(i, 2)
                weighted_values(i, 3)

            steps(pe, step)

        @block.scalar
        def _(act):
            scale_act(act)

            def copy_weights(i, k):
                if inside(i):
                    act.wait_ge(pT_ready, i * QU + k + 1)
                    act.activation(pT[:, k % 2], ps_t[0:SK, k % 2], ACT.Copy).then_inc(pT_copied, 1)

            def exps(j, p, e):
                if inside(j):
                    act.wait_ge(sub_ready, j * QU + 2 * e + 2)
                    act.activation(pr[:, p, 2 * e:2 * e + 2], pr[:, p, 2 * e:2 * e + 2], ACT.Exp,
                                   scale=float(DK) ** -0.5).then_inc(p_ready, 1)

            def step(i, t, c):
                if isinstance(i, int) and i == -3:
                    return
                copy_weights(i, 0)
                act.wait_ge(yo_ready, i + 3)
                a, b = (0 if inside(i + 2) else 1), (2 if inside(i - 1) else 1)
                act.activation(yoT[:, a:b], ps_m[:, a:b], ACT.Copy).then_inc(yo_copied, 1)
                copy_weights(i, 1)
                exps(i + 1, (c + 1) % 2, 0)
                copy_weights(i, 2)
                if not rope and inside(i + 2):
                    act.wait_ge(q_ready, i + 3)
                    act.activation(qT[:, c % 2], ps_q[:, 0], ACT.Copy).then_inc(q_copied, 1)
                copy_weights(i, 3)
                exps(i + 1, (c + 1) % 2, 1)

            steps(act, step)

        @block.vector
        def _(dve):
            scale_dve(dve)
            dve.wait_ge(consts, 16 * NCONST)
            n, m = 0, 0
            for c in range(DC):
                if rope:
                    dve.wait_ge(proj_ready, n + 1)
                    if c:
                        dve.wait_ge(dve_setup, m)
                    cos_b = cos[:, 0:SK].unsqueeze(1).broadcast_to([P, B, SK])
                    sin_b = sin[:, 0:SK].unsqueeze(1).broadcast_to([P, B, SK])
                    k0 = ps_s[:, n % 2, 0:B * SK].rearrange("p (b k) -> p b k", b=B)
                    k1 = ps_s[:, (n + 1) % 2, 0:B * SK].rearrange("p (b k) -> p b k", b=B)
                    dve.tensor_tensor(rk[:], k0, cos_b, ALU.mult).then_inc(proj_used, 1)
                    dve.wait_ge(proj_ready, n + 2)
                    tmp = pr[:, 0, 0].rearrange("p h k -> p (h k)").rearrange("p (b k) -> p b k", b=B)
                    dve.tensor_tensor(tmp, k1, sin_b, ALU.mult).then_inc(proj_used, 1)
                    dve.wait_ge(proj_used, n + 2)
                    dve.tensor_tensor(rk[:], rk[:], tmp, ALU.add).then_inc(dve_setup, 1)
                    m += 1
                    dve.wait_ge(dve_setup, m)
                    n += 2
                    for b in range(B):
                        last = dve.tensor_tensor(keys_bd[:, c, b], rk[:, b].unsqueeze(1).broadcast_to([P, HU, SK]),
                                                 bm[:].unsqueeze(2).broadcast_to([P, HU, SK]), ALU.mult)
                    last.then_inc(dve_setup, 1)
                    m += 1
                else:
                    dve.wait_ge(proj_ready, n + 1)
                    for b in range(B):
                        last = dve.tensor_tensor(
                            keys_bd[:, c, b],
                            ps_s[:, n % 2, b * SK:(b + 1) * SK].unsqueeze(1).broadcast_to([P, HU, SK]),
                            bm[:].unsqueeze(2).broadcast_to([P, HU, SK]), ALU.mult)
                    last.then_inc(proj_used, 1)
                    n += 1
            dve.memset(vals[:, :, :, DK:DK + 1], 1.0)
            for b in range(B):
                dve.wait_ge(proj_ready, n + 1)
                last = dve.tensor_copy(vals[:, b, :, 0:DK], ps_s[0:SK, n % 2, 0:D].rearrange("p (h d) -> p h d", h=H))
                last.then_inc(proj_used, 1)
                n += 1
            dve.wait_ge(proj_used, n)
            dve.sem_inc(setup_done, 1)

            def normalise(j, half, p):
                if not inside(j):
                    return
                dve.wait_ge(xa_loaded[p], (half + 1) * NXA)
                if mask is not None:
                    dve.tensor_scalar(mb[:, p, :], mi[:, p, :], 0.0, -3e38, ALU.is_equal, ALU.mult)
                dve.tensor_scalar(y[:, p, :], xa[:, p, :], mv[:, bass.ds(j, 1), 0], scale[:, bass.ds(j, 1)],
                                  ALU.subtract, ALU.mult).then_inc(y_ready, 1)

            def less_max(j, p, k):
                if not inside(j):
                    return
                dve.wait_ge(s_ready, j * QU + k + 1)
                s = ps_s[:, k % 2, 0:GRP * SK].rearrange("p (h k) -> p h k", h=GRP)
                dve.tensor_reduce(mx[:, p, k], s, AX.X, ALU.max).then_inc(max_ready, 1)
                dve.wait_ge(max_ready, j * QU + k + 1)
                dve.tensor_tensor(pr[:, p, k], s, mx[:, p, k].unsqueeze(2).broadcast_to([P, GRP, SK]),
                                  ALU.subtract).then_inc(sub_ready, 1)

            def rotate(j, p):
                if not (rope and inside(j)):
                    return
                off = (j % TPB) * P
                dve.wait_ge(q_ready, j + 1)
                for r, tab in ((0, cos), (1, sin)):
                    last = dve.tensor_tensor(rt[:, r], ps_q[:, r],
                                             tab[:, bass.ds(off, P)].unsqueeze(1).broadcast_to([P, DC, P]), ALU.mult)
                last.then_inc(turned, 1)
                dve.wait_ge(turned, j + 1)
                dve.tensor_tensor(qT[:, p], rt[:, 0], rt[:, 1], ALU.add).then_inc(q_copied, 1)

            def step(i, t, c):
                less_max(i + 1, (c + 1) % 2, 0)
                less_max(i + 1, (c + 1) % 2, 1)
                less_max(i + 1, (c + 1) % 2, 2)
                rotate(i + 2, c % 2)
                if inside(i - 1):
                    q, half = (c - 1) % 2, t + (c - 1) // 2
                    dve.wait_ge(xr_loaded[q], (half + 1) * 16)
                    dve.wait_ge(stored[q], (half + 1) * 16)
                    dve.wait_ge(out_ready, i)
                    dve.tensor_tensor(xo[:, q, :], ps_w[:, 0:D], xr[:, q, :], ALU.add).then_inc(res_done, 1)
                less_max(i + 1, (c + 1) % 2, 3)
                if inside(i):
                    dve.wait_ge(av_ready, i + 1)
                    ov = ps_v[:, 0:H * (DK + 1)].rearrange("p (h e) -> p h e", h=H)
                    dve.reciprocal(rs[:].unsqueeze(2), ov[:, :, DK:DK + 1]).then_inc(sum_inv, 1)
                    dve.wait_ge(sum_inv, i + 1)
                    dve.tensor_tensor(o[:].rearrange("p (h e) -> p h e", h=H), ov[:, :, 0:DK],
                                      rs[:].unsqueeze(2).broadcast_to([P, H, DK]), ALU.mult).then_inc(o_ready, 1)
                if inside(i - 1):
                    dve.wait_ge(res_done, i)
                    dve.bn_stats(st[:], xo[:, q, :]).then_inc(stats, 1)
                normalise(i + 3, t + (c + 3) // 2, (c + 3) % 2)
                if inside(i - 1):
                    dve.wait_ge(stats, i * 2 - 1)
                    dve.nop(nofuse=True)
                    dve.bn_aggr(ag[:], st[:]).then_inc(stats, 1)
                    dve.wait_ge(stats, i * 2)
                    dve.nop(nofuse=True)
                    dve.tensor_copy(mv[:, bass.ds(i - 1, 1), :], ag[:].unsqueeze(1))

            steps(dve, step)


KH = PH * TOPK
NF = 32
PARTS = 3
SEL = 2 + PARTS
PAIRS = TILES // 2
TG = 32
TB = 8


def product_keys(nc, x_in, mv, xnT_d, sel_d, w_q, keysT, norm_w, ident_d, identb_d, iota8_d):
    with ExitStack() as ctx:
        def sb(name, shape, dt=F32):
            return ctx.enter_context(nc.sbuf_tensor("pk_" + name, shape, dt))

        def sem(name):
            return ctx.enter_context(nc.semaphore("pk_" + name))

        def ps(name, shape, dt=F32):
            return ctx.enter_context(nc.psum_tensor("pk_" + name, shape, dt))

        NS = 2 * PH
        ident, identb = sb("ident", [P, P]), sb("identb", [P, P], BF16)
        wq, kT = sb("wq", [P, NS, D]), sb("kT", [P, NS, NKEYS])
        nw = sb("nw", [P, DC])
        iota8 = sb("iota8", [P, TOPK, TOPK])
        fold = sb("fold", [P, DC, NS * NKEYS])
        scale = sb("scale", [P, TILES])
        x, y, xT = sb("x", [P, 2, D]), sb("y", [P, 2, D]), sb("xT", [P, 2, DC, P])
        sim = sb("sim", [P, 2, NS, NKEYS])
        top, topi, topf = sb("top", [P, NS, TOPK]), sb("topi", [P, NS, TOPK], U32), sb("topf", [P, NS, TOPK])
        grid = sb("grid", [P, PH, TOPK, TOPK])
        best, bi = sb("best", [P, PH, TOPK]), sb("bi", [P, PH, TOPK], U32)
        ab, abf = sb("ab", [P, 2, PH, TOPK], U32), sb("abf", [P, 2, PH, TOPK])
        eq = sb("eq", [P, 2, PH, TOPK, TOPK])
        ij = sb("ij", [P, 2, PH, TOPK])
        far = sb("far", [P, PH, TOPK])
        w, r1, r2 = sb("w", [P, PH, TOPK]), sb("r1", [P, PH, TOPK]), sb("r2", [P, PH, TOPK])
        sel = sb("sel", [P, 2, SEL, 2, KH], BF16)
        selT = sb("selT", [P, 2, SEL, P], BF16)
        ps_f, ps_y, ps_s = ps("ps_f", [P, 2, BANK]), ps("ps_y", [P, BANK]), ps("ps_s", [P, 2, BANK])
        ps_t = ps("ps_t", [P, SEL, P], BF16)

        consts, fold_ready, fold_copied = sem("consts"), sem("fold_ready"), sem("fold_copied")
        x_loaded = [sem(f"x_loaded{p}") for p in range(2)]
        xT_stored = [sem(f"xT_stored{p}") for p in range(2)]
        sel_stored = [sem(f"sel_stored{p}") for p in range(2)]
        y_ready, yT_ready, xT_ready, s_ready, sim_ready = (sem(n) for n in (
            "y_ready", "yT_ready", "xT_ready", "s_ready", "sim_ready"))
        chain, sel_ready, selT_ready, selT_copied = (sem(n) for n in ("chain", "sel_ready", "selT_ready", "selT_copied"))
        scale_dve, scale_act = row_scale(nc, ctx, None, mv, scale, True, "pk_ln")
        STEPS = 17
        block = ctx.enter_context(nc.Block())

        @block.sync
        def _(sp):
            for dst, src in ((wq, w_q), (kT, keysT), (nw, norm_w), (ident, ident_d), (identb, identb_d), (iota8, iota8_d)):
                sp.dma_start(dst[:], src).then_inc(consts, 16)
            for p in range(2):
                sp.sem_inc(xT_stored[p], 16)
                sp.sem_inc(sel_stored[p], 16)
                sp.dma_start(x[:, p, :], x_in[p]).then_inc(x_loaded[p], 16)

            def stores(i, m, q):
                sp.wait_ge(xT_ready, i + 1)
                sp.nop(nofuse=True)
                sp.dma_start(xnT_d[m, :, :, q, :], xT[:, q]).then_inc(xT_stored[q], 16)

            with sp.Fori(0, PAIRS - 1) as m:
                for q in range(2):
                    i = m * 2 + q
                    sp.wait_ge(y_ready, i + 1)
                    sp.nop(nofuse=True)
                    sp.dma_start(x[:, q, :], x_in[i + 2]).then_inc(x_loaded[q], 16)
                    stores(i, m, q)
            for q in range(2):
                stores(TILES - 2 + q, PAIRS - 1, q)
                sp.wait_ge(xT_stored[q], 16 * (PAIRS + 1))

        @block.tensor
        def _(pe):
            pe.wait_ge(consts, 16 * 6)
            pe.sem_inc(selT_ready, 2)
            for c in range(DC):
                if c:
                    pe.wait_ge(fold_copied, c)
                for s in range(NS):
                    last = pe.matmul(ps_f[:, s // PH, (s % PH) * NKEYS:(s % PH + 1) * NKEYS],
                                     wq[:, s, c * P:(c + 1) * P], kT[:, s, :], start=True, stop=True)
                last.then_inc(fold_ready, 1)
            pe.wait_ge(fold_copied, DC)

            def selections(m, p):
                pe.wait_ge(sel_ready, m + 1)
                pe.wait_ge(selT_copied, m + 1)
                for k in range(SEL):
                    last = pe.transpose(ps_t[:, k, :], sel[:, p, k].rearrange("p q k -> p (q k)"), identb[:])
                last.then_inc(selT_ready, 1)

            def tile(i, q):
                pe.wait_ge(y_ready, i + 1)
                for k in range(DC):
                    last = pe.transpose(ps_y[:, k * P:(k + 1) * P], y[:, q, k * P:(k + 1) * P], ident[:])
                last.then_inc(yT_ready, 1)
                pe.wait_ge(xT_ready, i + 1)
                if not (isinstance(i, int) and i == 0):
                    pe.wait_ge(sim_ready, i)
                for g in range(2):
                    for k in range(DC):
                        last = pe.matmul(ps_s[:, g, :], xT[:, q, k, :], fold[:, k, g * BANK:(g + 1) * BANK],
                                         start=(k == 0), stop=(k == DC - 1))
                last.then_inc(s_ready, 1)

            for q in range(2):
                tile(q, q)
            with pe.Fori(0, PAIRS // 2 - 1) as mm:
                for p in range(2):
                    m = mm * 2 + p
                    for q in range(2):
                        tile(m * 2 + 2 + q, q)
                    selections(m, p)
            m = PAIRS - 2
            for q in range(2):
                tile(m * 2 + 2 + q, q)
            selections(m, 0)
            selections(m + 1, 1)

        @block.scalar
        def _(act):
            scale_act(act)
            act.wait_ge(consts, 16 * 6)
            act.sem_inc(selT_copied, 1)
            for c in range(DC):
                act.wait_ge(fold_ready, c + 1)
                act.activation(fold[:, c, :], ps_f[:].rearrange("p g n -> p (g n)"), ACT.Copy).then_inc(fold_copied, 1)

            def tile(i, m, q):
                act.wait_ge(yT_ready, i + 1)
                act.wait_ge(xT_stored[q], m * 16 + 16)
                for k in range(DC):
                    last = act.activation(xT[:, q, k, :], ps_y[:, k * P:(k + 1) * P], ACT.Copy, scale=nw[:, k:k + 1])
                last.then_inc(xT_ready, 1)
                act.wait_ge(s_ready, i + 1)
                if not (isinstance(i, int) and i < 2):
                    act.wait_ge(chain, (i - 2) * STEPS + 2)
                act.activation(sim[:, q].rearrange("p s k -> p (s k)"), ps_s[:].rearrange("p g n -> p (g n)"),
                               ACT.Copy).then_inc(sim_ready, 1)

            def selections(m, mm, p):
                act.wait_ge(selT_ready, m + 3)
                act.wait_ge(sel_stored[p], mm * 16 + 16)
                act.activation(selT[:, p], ps_t[:], ACT.Copy).then_inc(selT_copied, 1)
                act.wait_ge(selT_copied, m + 2)
                act.dma_start(sel_d[m], selT[:, p]).then_inc(sel_stored[p], 16)

            for q in range(2):
                tile(q, 0, q)
            with act.Fori(0, PAIRS // 2 - 1) as mm:
                for p in range(2):
                    m = mm * 2 + p
                    for q in range(2):
                        tile(m * 2 + 2 + q, m + 1, q)
                    selections(m, mm, p)
            m = PAIRS - 2
            for q in range(2):
                tile(m * 2 + 2 + q, m + 1, q)
            selections(m, PAIRS // 2 - 1, 0)
            selections(m + 1, PAIRS // 2 - 1, 1)
            for p in range(2):
                act.wait_ge(sel_stored[p], 16 * (PAIRS // 2 + 1))

        @block.vector
        def _(dve):
            scale_dve(dve)
            dve.wait_ge(consts, 16 * 6)

            def norm(i, m, q):
                dve.wait_ge(x_loaded[q], m * 16 + 16)
                if not (isinstance(i, int) and i < 2):
                    dve.wait_ge(yT_ready, i - 1)
                dve.tensor_scalar(y[:, q, :], x[:, q, :], mv[:, bass.ds(i, 1), 0], scale[:, bass.ds(i, 1)],
                                  ALU.subtract, ALU.mult).then_inc(y_ready, 1)

            def winners(i, m, p, q):
                n = [0]

                def settle(ins):
                    n[0] += 1
                    ins.then_inc(chain, 1)
                    dve.wait_ge(chain, i * STEPS + n[0])
                    dve.nop(nofuse=True)

                dve.wait_ge(sim_ready, i + 1)
                dve.nop(nofuse=True)
                for s in range(NS):
                    last = dve.max(top[:, s, :], sim[:, q, s, :])
                settle(last)
                for s in range(NS):
                    last = dve.max_index(topi[:, s, :], top[:, s, :], sim[:, q, s, :])
                settle(last)
                dve.tensor_copy(topf[:], topi[:])
                t2 = top[:].rearrange("p (h s) k -> p h s k", s=2)
                for h in range(PH):
                    last = dve.tensor_tensor(grid[:, h], t2[:, h, 0].unsqueeze(2).broadcast_to([P, TOPK, TOPK]),
                                             t2[:, h, 1].unsqueeze(1).broadcast_to([P, TOPK, TOPK]), ALU.add)
                settle(last)
                for h in range(PH):
                    last = dve.max(best[:, h, :], grid[:, h].rearrange("p a b -> p (a b)"))
                settle(last)
                for h in range(PH):
                    last = dve.max_index(bi[:, h, :], best[:, h, :], grid[:, h].rearrange("p a b -> p (a b)"))
                settle(last)
                dve.tensor_scalar(ab[:, 0], bi[:], 3, None, ALU.logical_shift_right)
                settle(dve.tensor_scalar(ab[:, 1], bi[:], 7, None, ALU.bitwise_and))
                settle(dve.tensor_copy(abf[:], ab[:]))
                for s in range(2):
                    last = dve.tensor_tensor(eq[:, s], abf[:, s].unsqueeze(2).broadcast_to([P, PH, TOPK, TOPK]),
                                             iota8[:].unsqueeze(1).broadcast_to([P, PH, TOPK, TOPK]), ALU.is_equal)
                settle(last)
                tf = topf[:].rearrange("p (h s) k -> p s h k", s=2)
                for s in range(2):
                    last = dve.tensor_tensor(eq[:, s], eq[:, s],
                                             tf[:, s].unsqueeze(3).broadcast_to([P, PH, TOPK, TOPK]), ALU.mult)
                settle(last)
                for s in range(2):
                    last = dve.tensor_reduce(ij[:, s], eq[:, s].rearrange("p h c k -> p h k c"), AX.X, ALU.add)
                settle(last)
                settle(dve.tensor_scalar(far[:], ij[:, 1], float(NF), None, ALU.is_ge))
                if q == 0:
                    dve.wait_ge(selT_ready, m + 1)

                def kind(k):
                    return sel[:, p, k, q].rearrange("p (h k) -> p h k", h=PH)
                dve.scalar_tensor_tensor(kind(0), ij[:, 0], 2.0, far[:], ALU.mult, ALU.add)
                settle(dve.scalar_tensor_tensor(r1[:], far[:], -float(NF), ij[:, 1], ALU.mult, ALU.add))
                dve.tensor_scalar(kind(1), r1[:], float(NF * q), None, ALU.add)
                settle(dve.tensor_scalar(w[:], best[:], 0.0, None, ALU.max))
                settle(dve.tensor_copy(kind(2), w[:]))
                settle(dve.tensor_tensor(r1[:], w[:], kind(2), ALU.subtract))
                settle(dve.tensor_copy(kind(3), r1[:]))
                settle(dve.tensor_tensor(r2[:], r1[:], kind(3), ALU.subtract))
                last = dve.tensor_copy(kind(4), r2[:])
                if q == 1:
                    last.then_inc(sel_ready, 1)
                assert n[0] == STEPS, n[0]

            for q in range(2):
                norm(q, 0, q)
            with dve.Fori(0, PAIRS // 2 - 1) as mm:
                for p in range(2):
                    m = mm * 2 + p
                    for q in range(2):
                        norm(m * 2 + 2 + q, m + 1, q)
                        winners(m * 2 + q, m, p, q)
            m = PAIRS - 2
            for q in range(2):
                norm(m * 2 + 2 + q, m + 1, q)
                winners(m * 2 + q, m, 0, q)
            for q in range(2):
                winners(m * 2 + 2 + q, m + 1, 1, q)


def experts(nc, x_in, x_out, mv, xnT_d, sel_d, down_d, up_d, iota_d):
    with ExitStack() as ctx:
        def sb(name, shape, dt=F32):
            return ctx.enter_context(nc.sbuf_tensor("ex_" + name, shape, dt))

        def sem(name):
            return ctx.enter_context(nc.semaphore("ex_" + name))

        def ps(name, shape, dt=F32):
            return ctx.enter_context(nc.psum_tensor("ex_" + name, shape, dt))

        T2 = 2 * P
        NB = P // TB
        NG = P // TG
        BPG = NB // NG
        down, up = sb("down", [P, DC, NF, P]), sb("up", [P, NF, D])
        iota = sb("iota", [P, P, TG], BF16)
        xb = sb("xb", [P, 2, DC, T2])
        hid = sb("hid", [P, 2, NF, T2])
        sel = sb("sel", [P, 2, SEL, P], BF16)
        rows = sb("rows", [P, 2, P, TG], BF16)
        eq = sb("eq", [P, 2 * NF, TG], BF16)
        cols = sb("cols", [P, 2, PARTS, 2 * NF, TG], BF16)
        xr = sb("xr", [P, 2, D])
        xo = sb("xo", [P, 2, D])
        st, ag = sb("st", [P, 2, 6]), sb("ag", [P, 2, 2])
        ps_h, ps_w, ps_o = ps("ps_h", [P, 2, 2, T2]), ps("ps_w", [P, 2, TB, 2, NF]), ps("ps_o", [P, 2, D])

        consts, down_loaded = sem("consts"), sem("down_loaded")
        xb_loaded = [sem(f"xb_loaded{p}") for p in range(2)]
        sel_loaded = [sem(f"sel_loaded{p}") for p in range(2)]
        xr_loaded, stored = sem("xr_loaded"), sem("stored")
        h_ready, hid_ready, one_hot, eq_ready, w_ready, weighted = (sem(n) for n in (
            "h_ready", "hid_ready", "one_hot", "eq_ready", "w_ready", "weighted"))
        out_ready, summed, stats = sem("out_ready"), sem("summed"), sem("stats")
        block = ctx.enter_context(nc.Block())
        HG = NF // 2

        @block.sync
        def _(sp):
            sp.dma_start(down[:], down_d).then_inc(down_loaded, 16)

            def load(m, p):
                sp.dma_start(xb[:, p], xnT_d[m].rearrange("p c q t -> p c (q t)")).then_inc(xb_loaded[p], 16)
                sp.dma_start(sel[:, p], sel_d[m]).then_inc(sel_loaded[p], 16)

            def residual(m):
                for q in range(2):
                    sp.dma_start(xr[:, q, :], x_in[m * 2 + q]).then_inc(xr_loaded, 16)

            def store(m):
                sp.wait_ge(summed, m * 2 + 2)
                for q in range(2):
                    sp.dma_start(x_out[m * 2 + q], xo[:, q, :]).then_inc(stored, 16)

            for p in range(2):
                load(p, p)
            sp.dma_start(iota[:], iota_d).then_inc(consts, 16)
            sp.dma_start(up[:], up_d).then_inc(consts, 16)
            residual(0)
            with sp.Fori(0, PAIRS // 2 - 1) as mm:
                for p in range(2):
                    m = mm * 2 + p
                    sp.wait_ge(out_ready, m + 1)
                    sp.nop(nofuse=True)
                    sp.wait_ge(one_hot, (m + 1) * NG)
                    load(m + 2, p)
                    store(m)
                    residual(m + 1)
            store(PAIRS - 2)
            residual(PAIRS - 1)
            store(PAIRS - 1)
            sp.wait_ge(stored, 16 * TILES)

        @block.tensor
        def _(pe):
            pe.wait_ge(down_loaded, 16)

            def hidden(m, mm, p, g):
                if g == 0:
                    pe.wait_ge(xb_loaded[p], mm * 16 + 16)
                n = m * HG + g
                if not (isinstance(n, int) and n < 2):
                    pe.wait_ge(hid_ready, n - 1)
                for j in range(2):
                    for c in range(DC):
                        last = pe.matmul(ps_h[:, g % 2, j, :], down[:, c, 2 * g + j, :], xb[:, p, c, :],
                                         start=(c == 0), stop=(c == DC - 1))
                last.then_inc(h_ready, 1)

            def weights(m, g):
                n = m * NB + g
                if g % BPG == 0:
                    pe.wait_ge(one_hot, m * NG + g // BPG + 1)
                if not (isinstance(n, int) and n < 2):
                    pe.wait_ge(weighted, n - 1)
                buf = (g // BPG) % 2
                for t in range(TB):
                    at = (g % BPG) * TB + t
                    for k in range(PARTS):
                        last = pe.matmul(ps_w[:, g % 2, t].rearrange("p q f -> p (q f)"), rows[:, buf, :, at],
                                         cols[:, buf, k, :, at], start=(k == 0), stop=(k == PARTS - 1))
                last.then_inc(w_ready, 1)

            def outputs(m, p):
                pe.wait_ge(weighted, (m + 1) * NB)
                if not (isinstance(m, int) and m == 0):
                    pe.wait_ge(summed, m * 2)
                for q in range(2):
                    for f in range(NF):
                        last = pe.matmul(ps_o[:, q, :], hid[:, p, f, q * P:(q + 1) * P], up[:, f, :],
                                         start=(f == 0), stop=(f == NF - 1))
                last.then_inc(out_ready, 1)

            for g in range(HG):
                hidden(0, 0, 0, g)
            pe.wait_ge(consts, 32)
            for g in range(HG):
                hidden(1, 0, 1, g)
                weights(0, g)
            outputs(0, 0)
            with pe.Fori(0, PAIRS // 2 - 1) as mm:
                for p in range(2):
                    m = mm * 2 + 1 + p
                    for g in range(HG):
                        hidden(m + 1, mm + 1, p, g)
                        weights(m, g)
                    outputs(m, 1 - p)
            for g in range(HG):
                weights(PAIRS - 1, g)
            outputs(PAIRS - 1, 1)

        @block.scalar
        def _(act):
            def gelus(m, p):
                if not (isinstance(m, int) and m < 2):
                    act.wait_ge(out_ready, m - 1)
                for g in range(HG):
                    act.wait_ge(h_ready, m * HG + g + 1)
                    act.activation(hid[:, p, 2 * g:2 * g + 2, :], ps_h[:, g % 2], ACT.Gelu).then_inc(hid_ready, 1)

            gelus(0, 0)
            gelus(1, 1)
            with act.Fori(1, PAIRS // 2) as mm:
                for p in range(2):
                    gelus(mm * 2 + p, p)

        @block.vector
        def _(dve):
            dve.wait_ge(consts, 32)

            def expand(m, mm, p, k):
                if k == 0:
                    dve.wait_ge(sel_loaded[p], mm * 16 + 16)
                buf = k % 2
                if not (isinstance(m, int) and m == 0 and k < 2):
                    dve.wait_ge(w_ready, m * NB + (k - 1) * BPG)
                    dve.wait_ge(one_hot, m * NG + k)
                elif k == 1:
                    dve.wait_ge(one_hot, 1)
                at = slice(k * TG, (k + 1) * TG)
                dve.tensor_tensor(rows[:, buf], sel[:, p, 0, at].unsqueeze(1).broadcast_to([P, P, TG]), iota[:],
                                  ALU.is_equal)
                dve.tensor_tensor(eq[:], sel[:, p, 1, at].unsqueeze(1).broadcast_to([P, 2 * NF, TG]),
                                  iota[:, 0:2 * NF, :], ALU.is_equal).then_inc(eq_ready, 1)
                dve.wait_ge(eq_ready, m * NG + k + 1)
                for j in range(PARTS):
                    last = dve.tensor_tensor(cols[:, buf, j], eq[:],
                                             sel[:, p, 2 + j, at].unsqueeze(1).broadcast_to([P, 2 * NF, TG]), ALU.mult)
                last.then_inc(one_hot, 1)

            def weigh(m, p, k):
                if k == 0:
                    dve.wait_ge(hid_ready, m * HG + HG)
                for g in range(k * BPG, (k + 1) * BPG):
                    dve.wait_ge(w_ready, m * NB + g + 1)
                    v = hid[:, p].rearrange("p f (q t) -> p t q f", q=2)[:, g * TB:(g + 1) * TB]
                    dve.tensor_tensor(v, v, ps_w[:, g % 2], ALU.mult).then_inc(weighted, 1)

            def finish(m):
                dve.wait_ge(out_ready, m + 1)
                dve.wait_ge(xr_loaded, m * 32 + 32)
                if not (isinstance(m, int) and m == 0):
                    dve.wait_ge(stored, m * 32)
                for q in range(2):
                    dve.tensor_tensor(xo[:, q, :], ps_o[:, q, :], xr[:, q, :], ALU.add).then_inc(summed, 1)
                dve.wait_ge(summed, m * 2 + 2)
                dve.bn_stats(st[:, 0, :], xo[:, 0, :])
                dve.bn_stats(st[:, 1, :], xo[:, 1, :]).then_inc(stats, 1)
                dve.wait_ge(stats, m * 2 + 1)
                dve.nop(nofuse=True)
                dve.bn_aggr(ag[:, 0, :], st[:, 0, :])
                dve.bn_aggr(ag[:, 1, :], st[:, 1, :]).then_inc(stats, 1)
                dve.wait_ge(stats, m * 2 + 2)
                dve.nop(nofuse=True)
                dve.tensor_copy(mv[:, bass.ds(m * 2, 2), :], ag[:])

            expand(0, 0, 0, 0)
            for k in range(NG):
                expand(*((0, 0, 0, k + 1) if k < NG - 1 else (1, 0, 1, 0)))
                weigh(0, 0, k)
            with dve.Fori(0, PAIRS // 2 - 1) as mm:
                for p in range(2):
                    m = mm * 2 + 1 + p
                    for k in range(NG):
                        if k < NG - 1:
                            expand(m, mm + p, 1 - p, k + 1)
                        else:
                            expand(m + 1, mm + 1, p, 0)
                        if k == 0:
                            finish(m - 1)
                        weigh(m, 1 - p, k)
            m = PAIRS - 1
            for k in range(NG):
                if k < NG - 1:
                    expand(m, PAIRS // 2 - 1, 1, k + 1)
                if k == 0:
                    finish(m - 1)
                weigh(m, 1, k)
            finish(m)


def route(nc, x_in, mv, slots_d, gates, take, wr_d, br_d, upper_d, ident_d, iota_d):
    with ExitStack() as ctx:
        def sb(name, shape, dt=F32):
            return ctx.enter_context(nc.sbuf_tensor("rt_" + name, shape, dt))

        def sem(name):
            return ctx.enter_context(nc.semaphore("rt_" + name))

        def ps(name, shape, dt=F32):
            return ctx.enter_context(nc.psum_tensor("rt_" + name, shape, dt))

        TE = [P, TILES, E8]
        ident, upper, ones = sb("ident", [P, P]), sb("upper", [P, P]), sb("ones", [P, P])
        wr, br = sb("wr", [P, DC, E8]), sb("br", [P, E8])
        iota = sb("iota", [P, E8])
        scale = sb("scale", [P, TILES])
        x, y = sb("x", [P, 2, D]), sb("y", [P, 2, D])
        yall = sb("yall", [P, TILES, D])
        yT = sb("yT", [P, DC, P])
        lg, d, ex, eq, oh, pos, inc = (sb(n, TE) for n in ("lg", "d", "ex", "eq", "oh", "pos", "inc"))
        one_row = sb("one_row", [P, TILES])
        mx, se, first, rank, keep, slot, away = (sb(n, [P, TILES]) for n in (
            "mx", "se", "first", "rank", "keep", "slot", "away"))
        put = sb("put", [P, TILES], U32)
        zero = sb("zero", [P, 8 * D])
        ps_y, ps_l, ps_c = ps("ps_y", [P, BANK]), ps("ps_l", [P, BANK]), ps("ps_c", [P, 2, BANK])

        consts, zeroed, zeros_ready = sem("consts"), sem("zeroed"), sem("zeros_ready")
        x_loaded = [sem(f"x_loaded{p}") for p in range(2)]
        y_ready, yT_ready, yT_copied, l_ready, l_copied, ones_ready = (sem(n) for n in (
            "y_ready", "yT_ready", "yT_copied", "l_ready", "l_copied", "ones_ready"))
        chain, d_ready, ex_ready, oh_ready, counted, put_ready, gated, scattered = (sem(n) for n in (
            "chain", "d_ready", "ex_ready", "oh_ready", "counted", "put_ready", "gated", "scattered"))
        scale_dve, scale_act = row_scale(nc, ctx, None, mv, scale, False, "rt_ln")
        block = ctx.enter_context(nc.Block())
        NZ = E8 * CAP // (8 * P)

        @block.sync
        def _(sp):
            for dst, src in ((ident, ident_d), (upper, upper_d), (wr, wr_d), (br, br_d), (iota, iota_d)):
                sp.dma_start(dst[:], src).then_inc(consts, 16)
            for p in range(2):
                sp.dma_start(x[:, p, :], x_in[p]).then_inc(x_loaded[p], 16)
            sp.wait_ge(zeros_ready, 1)
            for z in range(NZ):
                sp.dma_start(slots_d[z * 8 * P:(z + 1) * 8 * P, :].rearrange("(p r) d -> p (r d)", p=P),
                             zero[:]).then_inc(zeroed, 16)
            with sp.Fori(0, TILES // 2 - 1) as t:
                for p in range(2):
                    i = t * 2 + p
                    sp.wait_ge(y_ready, i + 1)
                    sp.nop(nofuse=True)
                    sp.dma_start(x[:, p, :], x_in[i + 2]).then_inc(x_loaded[p], 16)

        @block.gpsimd
        def _(pool):
            pool.memset(zero[:], 0.0).then_inc(zeros_ready, 1)
            pool.wait_ge(zeroed, 16 * NZ)
            pool.wait_ge(put_ready, 1)
            for i in range(TILES):
                pool.wait_ge(gated, i + 1)
                pool.indirect_dma_start(slots_d, bass.IndirectOffsetOnAxis(ap=put[:, i:i + 1], axis=0),
                                        yall[:, i, :], None, bounds_check=E8 * CAP - 1,
                                        oob_is_err=False).then_inc(scattered, 16)
            pool.wait_ge(scattered, 16 * TILES)

        @block.tensor
        def _(pe):
            pe.wait_ge(consts, 16 * 5)

            def tile(i, p):
                pe.wait_ge(y_ready, i + 1)
                for k in range(DC):
                    last = pe.transpose(ps_y[:, k * P:(k + 1) * P], y[:, p, k * P:(k + 1) * P], ident[:])
                last.then_inc(yT_ready, 1)
                pe.wait_ge(yT_copied, i + 1)
                if not (isinstance(i, int) and i == 0):
                    pe.wait_ge(l_copied, i)
                for k in range(DC):
                    last = pe.matmul(ps_l[:, 0:E8], yT[:, k, :], wr[:, k, :], start=(k == 0), stop=(k == DC - 1))
                last.then_inc(l_ready, 1)

            for p in range(2):
                tile(p, p)
            with pe.Fori(1, TILES // 2) as t:
                for p in range(2):
                    tile(t * 2 + p, p)
            pe.wait_ge(ones_ready, 1)
            pe.wait_ge(oh_ready, 1)
            flat = oh[:].rearrange("p t e -> p (t e)")
            pe.matmul(ps_c[:, 0, 0:TILES * E8], upper[:], flat, start=True, stop=True)
            pe.matmul(ps_c[:, 1, 0:TILES * E8], ones[:], flat, start=True, stop=True).then_inc(counted, 1)

        @block.scalar
        def _(act):
            scale_act(act)

            def tile(i):
                act.wait_ge(yT_ready, i + 1)
                act.activation(yT[:], ps_y[:, 0:D].rearrange("p (c t) -> p c t", c=DC), ACT.Copy).then_inc(yT_copied, 1)
                act.wait_ge(l_ready, i + 1)
                act.nop(nofuse=True)
                act.activation(lg[:, bass.ds(i, 1), :], ps_l[:, 0:E8].unsqueeze(1), ACT.Copy).then_inc(l_copied, 1)

            with act.Fori(0, TILES) as i:
                tile(i)
            act.wait_ge(d_ready, 1)
            act.activation(ex[:], d[:], ACT.Exp).then_inc(ex_ready, 1)

        @block.vector
        def _(dve):
            scale_dve(dve)
            dve.memset(one_row[:], 1.0)
            dve.memset(ones[:], 1.0).then_inc(ones_ready, 1)

            def tile(i, t, p):
                dve.wait_ge(x_loaded[p], t * 16 + 16)
                if not (isinstance(i, int) and i < 2):
                    dve.wait_ge(yT_ready, i - 1)
                dve.nop(nofuse=True)
                dve.tensor_scalar(yall[:, bass.ds(i, 1), :], x[:, p, :].unsqueeze(1), mv[:, bass.ds(i, 1), 0],
                                  scale[:, bass.ds(i, 1)], ALU.subtract, ALU.mult)
                dve.tensor_scalar(y[:, p, :], x[:, p, :], mv[:, bass.ds(i, 1), 0],
                                  scale[:, bass.ds(i, 1)], ALU.subtract, ALU.mult).then_inc(y_ready, 1)

            for p in range(2):
                tile(p, 0, p)
            with dve.Fori(1, TILES // 2) as t:
                for p in range(2):
                    tile(t * 2 + p, t, p)
            dve.wait_ge(l_copied, TILES)
            dve.wait_ge(consts, 16 * 5)
            n = [0]

            def settle(ins):
                n[0] += 1
                ins.then_inc(chain, 1)
                dve.wait_ge(chain, n[0])

            def over_experts(a):
                return a[:].unsqueeze(2).broadcast_to(TE)

            iota_b = iota[:].unsqueeze(1).broadcast_to(TE)
            settle(dve.tensor_tensor(lg[:], lg[:], br[:].unsqueeze(1).broadcast_to(TE), ALU.add))
            settle(dve.tensor_reduce(mx[:], lg[:], AX.X, ALU.max))
            dve.tensor_tensor(d[:], lg[:], over_experts(mx), ALU.subtract).then_inc(d_ready, 1)
            dve.wait_ge(d_ready, 1)
            settle(dve.tensor_scalar(eq[:], d[:], 0.0, None, ALU.is_equal))
            settle(dve.tensor_tensor(eq[:], eq[:], iota_b, ALU.mult))
            settle(dve.tensor_reduce(first[:], eq[:], AX.X, ALU.min))
            dve.tensor_tensor(oh[:], over_experts(first), iota_b, ALU.is_equal).then_inc(oh_ready, 1)
            dve.wait_ge(ex_ready, 1)
            settle(dve.tensor_reduce(se[:], ex[:], AX.X, ALU.add))
            settle(dve.reciprocal(gates[:], se[:]))
            dve.wait_ge(counted, 1)
            totals = ps_c[:, 1, 0:TILES * E8].rearrange("p (t e) -> p t e", e=E8)
            settle(dve.tensor_copy(pos[:], totals))
            for e in range(E8):
                last = dve.tensor_tensor_scan(inc[:, :, e], one_row[:], pos[:, :, e], 0.0, ALU.mult, ALU.add)
            settle(last)
            settle(dve.tensor_tensor(inc[:], inc[:], pos[:], ALU.subtract))
            settle(dve.tensor_tensor(pos[:], inc[:], ps_c[:, 0, 0:TILES * E8].rearrange("p (t e) -> p t e", e=E8), ALU.add))
            settle(dve.tensor_tensor(pos[:], pos[:], oh[:], ALU.mult))
            settle(dve.tensor_reduce(rank[:], pos[:], AX.X, ALU.add))
            settle(dve.tensor_scalar(keep[:], rank[:], float(CAP), None, ALU.is_lt))
            settle(dve.tensor_scalar(first[:], first[:], float(E8), float(CAP), ALU.add, ALU.mult))
            settle(dve.tensor_tensor(slot[:], first[:], rank[:], ALU.add))
            settle(dve.tensor_tensor(gates[:], gates[:], keep[:], ALU.mult))
            settle(dve.tensor_tensor(slot[:], slot[:], keep[:], ALU.mult))
            dve.tensor_copy(take[:], slot[:])
            settle(dve.tensor_scalar(away[:], keep[:], -float(4 * N), float(4 * N), ALU.mult, ALU.add))
            settle(dve.tensor_tensor(away[:], away[:], slot[:], ALU.add))
            dve.tensor_copy(put[:], away[:]).then_inc(put_ready, 1)
            for i in range(TILES):
                dve.tensor_scalar(yall[:, i, :], yall[:, i, :], gates[:, i:i + 1], None, ALU.mult).then_inc(gated, 1)


def routed_experts(nc, slots_d, eo_d, w1_d, b1_d, w2_d, b2_d, ident_d):
    with ExitStack() as ctx:
        def sb(name, shape, dt=F32):
            return ctx.enter_context(nc.sbuf_tensor("re_" + name, shape, dt))

        def sem(name):
            return ctx.enter_context(nc.semaphore("re_" + name))

        def ps(name, shape, dt=F32):
            return ctx.enter_context(nc.psum_tensor("re_" + name, shape, dt))

        ST = CAP // P
        ident, b1 = sb("ident", [P, P]), sb("b1", [P, E8, DC])
        w1, w2, b2 = sb("w1", [P, 2, DC, D]), sb("w2", [P, 2, DC, D]), sb("b2", [P, 2, D])
        ei, eT, hT, eo = sb("ei", [P, 2, ST, D]), sb("eT", [P, DC, CAP]), sb("hT", [P, DC, CAP]), sb("eo", [P, 2, ST, D])
        ps_t, ps_h, ps_e = ps("ps_t", [P, DC, CAP]), ps("ps_h", [P, DC, CAP]), ps("ps_e", [P, ST, D])
        consts = sem("consts")
        loaded = [sem(f"loaded{p}") for p in range(2)]
        stored = [sem(f"stored{p}") for p in range(2)]
        t_ready, t_copied, h_ready, h_copied, e_ready, e_copied = (sem(n) for n in (
            "t_ready", "t_copied", "h_ready", "h_copied", "e_ready", "e_copied"))
        block = ctx.enter_context(nc.Block())

        @block.sync
        def _(sp):
            for dst, src in ((ident, ident_d), (b1, b1_d)):
                sp.dma_start(dst[:], src).then_inc(consts, 16)
            for e in range(E8):
                p = e % 2
                if e >= 2:
                    sp.wait_ge(e_copied, e - 1)
                sp.dma_start(ei[:, p], slots_d[e * CAP:(e + 1) * CAP, :].rearrange("(s p) d -> p s d", p=P)).then_inc(loaded[p], 16)
                sp.dma_start(w1[:, p], w1_d[e]).then_inc(loaded[p], 16)
                sp.dma_start(w2[:, p], w2_d[e]).then_inc(loaded[p], 16)
                sp.dma_start(b2[:, p], b2_d[e]).then_inc(loaded[p], 16)

        @block.tensor
        def _(pe):
            pe.wait_ge(consts, 32)
            for e in range(E8):
                p = e % 2
                pe.wait_ge(loaded[p], 64 * (e // 2 + 1))
                for k in range(DC):
                    for s in range(ST):
                        last = pe.transpose(ps_t[:, k, s * P:(s + 1) * P], ei[:, p, s, k * P:(k + 1) * P], ident[:])
                last.then_inc(t_ready, 1)
                pe.wait_ge(t_copied, e + 1)
                for f in range(DC):
                    for k in range(DC):
                        last = pe.matmul(ps_h[:, f, :], w1[:, p, k, f * P:(f + 1) * P], eT[:, k, :],
                                         start=(k == 0), stop=(k == DC - 1))
                last.then_inc(h_ready, 1)
                pe.wait_ge(h_copied, e + 1)
                if e >= 1:
                    pe.wait_ge(e_copied, e)
                for s in range(ST):
                    for f in range(DC):
                        last = pe.matmul(ps_e[:, s, :], hT[:, f, s * P:(s + 1) * P], w2[:, p, f, :],
                                         start=(f == 0), stop=(f == DC - 1))
                last.then_inc(e_ready, 1)

        @block.scalar
        def _(act):
            for e in range(E8):
                p = e % 2
                act.wait_ge(t_ready, e + 1)
                act.activation(eT[:], ps_t[:], ACT.Copy).then_inc(t_copied, 1)
                act.wait_ge(h_ready, e + 1)
                for f in range(DC):
                    last = act.activation(hT[:, f, :], ps_h[:, f, :], ACT.Relu, bias=b1[:, e, f:f + 1])
                last.then_inc(h_copied, 1)
                act.wait_ge(e_copied, e + 1)
                act.dma_start(eo_d[e * CAP:(e + 1) * CAP, :].rearrange("(s p) d -> p s d", p=P), eo[:, p]).then_inc(stored[p], 16)
            for p in range(2):
                act.wait_ge(stored[p], 16 * (E8 // 2))

        @block.vector
        def _(dve):
            for e in range(E8):
                p = e % 2
                dve.wait_ge(e_ready, e + 1)
                if e >= 2:
                    dve.wait_ge(stored[p], 16 * (e // 2))
                dve.tensor_tensor(eo[:, p], ps_e[:], b2[:, p].unsqueeze(1).broadcast_to([P, ST, D]), ALU.add).then_inc(e_copied, 1)


def combine(nc, x_in, out, eo_d, gates, take):
    with ExitStack() as ctx:
        R = 4
        x = ctx.enter_context(nc.sbuf_tensor("cb_x", [P, TILES, D], F32))
        row = ctx.enter_context(nc.sbuf_tensor("cb_row", [P, R, D], F32))
        x_loaded = [ctx.enter_context(nc.semaphore(f"cb_x_loaded{g}")) for g in range(4)]
        row_loaded = [ctx.enter_context(nc.semaphore(f"cb_row_loaded{r}")) for r in range(R)]
        summed = ctx.enter_context(nc.semaphore("cb_summed"))
        stored = ctx.enter_context(nc.semaphore("cb_stored"))
        block = ctx.enter_context(nc.Block())
        G = TILES // 4

        @block.sync
        def _(sp):
            for g in range(4):
                sp.dma_start(x[:, g * G:(g + 1) * G, :],
                             x_in[g * G:(g + 1) * G].rearrange("t p d -> p t d")).then_inc(x_loaded[g], 16)
            for g in range(8):
                n = TILES // 8
                sp.wait_ge(summed, (g + 1) * n)
                sp.dma_start(out[g * n:(g + 1) * n].rearrange("t p d -> p t d"), x[:, g * n:(g + 1) * n, :]).then_inc(stored, 16)
            sp.wait_ge(stored, 16 * 8)

        @block.gpsimd
        def _(pool):
            for i in range(TILES):
                if i >= R:
                    pool.wait_ge(summed, i - R + 1)
                pool.indirect_dma_start(row[:, i % R, :], None, eo_d,
                                        bass.IndirectOffsetOnAxis(ap=take[:, i:i + 1], axis=0)).then_inc(row_loaded[i % R], 16)

        @block.vector
        def _(dve):
            for i in range(TILES):
                if i % G == 0:
                    dve.wait_ge(x_loaded[i // G], 16)
                dve.wait_ge(row_loaded[i % R], 16 * (i // R + 1))
                dve.scalar_tensor_tensor(x[:, i, :], row[:, i % R, :], gates[:, i:i + 1], x[:, i, :],
                                         ALU.mult, ALU.add).then_inc(summed, 1)


def program(nc, x, ctxT, mask, a0, a1, pk, me, c, out):
    def rows(name):
        return nc.dram_tensor(name, [TILES, P, D], F32).ap()

    x1, x2, x3 = rows("x1"), rows("x2"), rows("x3")
    xnT_d = nc.dram_tensor("xnT_d", [PAIRS, P, DC, 2, P], F32).ap()
    sel_d = nc.dram_tensor("sel_d", [PAIRS, P, SEL, P], BF16).ap()
    slots_d = nc.dram_tensor("slots_d", [E8 * CAP, D], F32).ap()
    eo_d = nc.dram_tensor("eo_d", [E8 * CAP, D], F32).ap()
    with ExitStack() as ctx:
        mv = ctx.enter_context(nc.sbuf_tensor("mv", [P, TILES, 2], F32))
        gates = ctx.enter_context(nc.sbuf_tensor("gates", [P, TILES], F32))
        take = ctx.enter_context(nc.sbuf_tensor("take", [P, TILES], U32))
        first_stats(nc, x, mv[:])
        attention(nc, "a0", x, x1, mv[:], ctxT, *a0, c["bmask"], c["ident"])
        product_keys(nc, x1, mv[:], xnT_d, sel_d, pk["w_q"], pk["keysT"], pk["norm_w"], c["ident"], c["identb"], c["iota8"])
        experts(nc, x1, x2, mv[:], xnT_d, sel_d, pk["down"], pk["up"], c["iota"])
        attention(nc, "a1", x2, x3, mv[:], ctxT, *a1[:4], c["bmask"], c["ident"],
                  rope=(a1[4], a1[5], c["cos"], c["sin"]), mask=mask, identb_d=c["identb"])
        route(nc, x3, mv[:], slots_d, gates, take, me["wr"], me["br"], c["upper"], c["ident"], c["iota_e"])
        routed_experts(nc, slots_d, eo_d, me["w1"], me["b1"], me["w2"], me["b2"], c["ident"])
        combine(nc, x3, out, eo_d, gates, take)


def layouts(np, a):
    def rowchunks(w):
        return w.reshape(DC, P, -1).transpose(1, 0, 2)

    def halves_exchanged(w):
        return w.reshape(H, 2, DK // 2, D)[:, ::-1].reshape(D, D)

    L0, L1 = "L0_xattn_W_", "L1_xattn_W_"
    return {
        "x": a["x"].reshape(TILES, P, D),
        "ctxT": rowchunks(a["ctx_1024"].transpose(2, 0, 1).reshape(D, B * SK)),
        "mask": a["mask_Bx1xSxS2_ik0"].reshape(TILES, P, SK),
        **{f"a0_{n}": rowchunks(a[L0 + n].T) for n in "qkvo"},
        **{f"a1_{n}": rowchunks(a[L1 + n].T) for n in "qkvo"},
        **{f"a1_{n}r": rowchunks(halves_exchanged(a[L1 + n]).T) for n in "qk"},
        "w_q": a["L0_ffn_w_q"].reshape(2 * PH, P, D).transpose(1, 0, 2),
        "keysT": a["L0_ffn_keys"].transpose(3, 0, 2, 1).reshape(P, 2 * PH, NKEYS),
        "norm_w": a["L0_ffn_norm_w"].reshape(DC, P).T,
        "down": a["L0_ffn_expert_down"].reshape(P, NF, DC, P).transpose(3, 2, 1, 0),
        "up": a["L0_ffn_expert_up"].reshape(P, NF, D),
        "wr": rowchunks(a["L1_ffn_Wr"]),
        "br": np.broadcast_to(a["L1_ffn_br"][None], (P, E8)),
        "w1": a["L1_ffn_W1"].reshape(E8, DC, P, D).transpose(0, 2, 1, 3),
        "b1": a["L1_ffn_b1"].reshape(E8, DC, P).transpose(2, 0, 1),
        "w2": a["L1_ffn_W2"].reshape(E8, DC, P, D).transpose(0, 2, 1, 3),
        "b2": np.broadcast_to(a["L1_ffn_b2"][:, None], (E8, P, D)),
    }


def constants(np, bf16):
    inv = (1.0 / 10000.0 ** (np.arange(0, DK, 2, dtype=np.float32) / DK)).astype(np.float32)
    angle = np.outer(inv, np.arange(S, dtype=np.float32)).astype(np.float32)
    cos, sin = np.cos(angle), np.sin(angle)
    eye = np.eye(P, dtype=np.float32)
    return {
        "bmask": np.repeat(np.eye(HU, dtype=np.float32), DK, axis=0),
        "ident": eye,
        "identb": eye.astype(bf16),
        "iota8": np.broadcast_to(np.arange(TOPK, dtype=np.float32)[None, :, None], (P, TOPK, TOPK)),
        "iota": np.broadcast_to(np.arange(P, dtype=np.float32)[None, :, None], (P, P, TG)).astype(bf16),
        "iota_e": np.broadcast_to(np.arange(E8, dtype=np.float32)[None] - E8, (P, E8)),
        "upper": np.triu(np.ones((P, P), np.float32)),
        "cos": np.tile(np.concatenate([cos, cos]), (HU, 1)).astype(np.float32),
        "sin": np.tile(np.concatenate([-sin, sin]), (HU, 1)).astype(np.float32),
    }


def kernel(**inputs):
    import ml_dtypes
    import numpy as np
    import concourse.bacc as bacc
    from concourse.bass_utils import run_bass_kernel_spmd as run

    a = layouts(np, {k: np.asarray(v) for k, v in inputs.items()})
    c = constants(np, ml_dtypes.bfloat16)
    nc = bacc.Bacc("TRN2", target_bir_lowering=False, num_devices=1)
    arrays, aps = {}, {}
    for name, v in {**a, **c}.items():
        v = np.ascontiguousarray(v)
        arrays[f"in_{name}"] = v
        aps[name] = nc.dram_tensor(f"in_{name}", v.shape, mybir.dt.from_np(v.dtype), kind="ExternalInput").ap()
    out = nc.dram_tensor("out", [TILES, P, D], F32, kind="ExternalOutput").ap()
    program(nc, aps["x"], aps["ctxT"], aps["mask"],
            [aps[f"a0_{n}"] for n in "qkvo"],
            [aps[f"a1_{n}"] for n in "qkvo"] + [aps["a1_qr"], aps["a1_kr"]],
            aps, aps, aps, out)
    r = run(nc, [arrays], core_ids=[0])
    return r.results[0]["out"].reshape(B, S, D)
```

```python
from contextlib import ExitStack

import concourse.bass as bass
from concourse import mybir

F32 = mybir.dt.float32
BF16 = mybir.dt.bfloat16
F16 = mybir.dt.float16
I32 = mybir.dt.int32
U32 = mybir.dt.uint32
ALU = mybir.AluOpType
ACT = mybir.ActivationFunctionType
AX = mybir.AxisListType

P = 128
D = 256
DC = D // P
B, S, SK = 4, 1024, 77
N = B * S
TILES = N // P
TPB = S // P
H, DK = 16, 16
HU = H // 2
GRP = 4
BANK = 512
LN_EPS = 1e-5
RMS_EPS = 1e-6
PH, NKEYS, TOPK = 8, 64, 8
E8, CAP = 8, N // 8


def row_scale(nc, ctx, mv, scale, rms, name):
    var = mv[:, :, 1]
    a = ctx.enter_context(nc.sbuf_tensor(name + "_a", [P, TILES], F32))
    root = ctx.enter_context(nc.sbuf_tensor(name + "_root", [P, TILES], F32))
    r = ctx.enter_context(nc.sbuf_tensor(name + "_r", [P, TILES], F32))
    t = ctx.enter_context(nc.sbuf_tensor(name + "_t", [P, TILES], F32))
    a_ready = ctx.enter_context(nc.semaphore(name + "_a_ready"))
    root_ready = ctx.enter_context(nc.semaphore(name + "_root_ready"))
    step = ctx.enter_context(nc.semaphore(name + "_step"))
    rounds = 2 if rms else 1

    def on_vector(dve):
        n = 0
        for k in range(rounds):
            if k == 0:
                dve.tensor_scalar(a[:], var, LN_EPS, None, ALU.add).then_inc(a_ready, 1)
            else:
                dve.tensor_tensor(t[:], scale[:], scale[:], ALU.mult).then_inc(step, 1)
                n += 1
                dve.wait_ge(step, n)
                dve.tensor_tensor(t[:], t[:], var, ALU.mult).then_inc(step, 1)
                n += 1
                dve.wait_ge(step, n)
                dve.tensor_scalar(a[:], t[:], RMS_EPS, None, ALU.add).then_inc(a_ready, 1)
            dve.wait_ge(root_ready, k + 1)
            dve.reciprocal(r[:], root[:]).then_inc(step, 1)
            n += 1
            dve.wait_ge(step, n)
            dve.tensor_tensor(t[:], r[:], r[:], ALU.mult).then_inc(step, 1)
            n += 1
            dve.wait_ge(step, n)
            dve.wait_ge(a_ready, k + 1)
            dve.tensor_tensor(t[:], t[:], a[:], ALU.mult).then_inc(step, 1)
            n += 1
            dve.wait_ge(step, n)
            dve.tensor_scalar(t[:], t[:], -0.5, 1.5, ALU.mult, ALU.add).then_inc(step, 1)
            n += 1
            dve.wait_ge(step, n)
            if k == 0:
                dve.tensor_tensor(scale[:], r[:], t[:], ALU.mult).then_inc(step, 1)
            else:
                dve.tensor_tensor(r[:], r[:], t[:], ALU.mult).then_inc(step, 1)
                n += 1
                dve.wait_ge(step, n)
                dve.tensor_tensor(scale[:], scale[:], r[:], ALU.mult).then_inc(step, 1)
            n += 1
            dve.wait_ge(step, n)

    def on_scalar(act):
        for k in range(rounds):
            act.wait_ge(a_ready, k + 1)
            act.activation(root[:], a[:], ACT.Sqrt).then_inc(root_ready, 1)

    return on_vector, on_scalar


def attention(nc, tag, x_in, x_out, mv, ctxT, wqT, wkT, wvT, woT, bmask, ident_d, rope=None, mask=None,
              identb_d=None, keep=None, also=(), fresh=False):
    with ExitStack() as ctx:
        def sb(name, shape, dt=F32):
            return ctx.enter_context(nc.sbuf_tensor(f"{tag}_{name}", shape, dt))

        def sem(name):
            return ctx.enter_context(nc.semaphore(f"{tag}_{name}"))

        QU = H // GRP
        UW = HU * SK
        UC = -(-UW // P)
        GROUPS = (0, UC // 2 + 1, UC)
        VW = HU * (DK + 1)
        ident = sb("ident", [P, P])
        bm = sb("bm", [P, HU])
        cT = sb("cT", [P, DC, B * SK])
        wq, wk, wv, wo = (sb(n, [P, DC, D]) for n in ("wq", "wk", "wv", "wo"))
        keys_bd = sb("keys_bd", [P, DC, B, HU, SK])
        vals = sb("vals", [SK, B, H, DK + 1])
        vals_bd = sb("vals_bd", [P, B, 2 * UC, VW])
        scale = sb("scale", [P, TILES])
        xa = sb("xa", [P, 2, D])
        xr = sb("xr", [P, 2, D])
        if keep is None:
            xo = sb("xo", [P, 2, D])
        y = sb("y", [P, 2, D])
        yoT = sb("yoT", [P, 2, DC, P])
        qT = sb("qT", [P, 2, DC, P])
        pr = sb("pr", [P, 2, 2, UC * P])
        mx = sb("mx", [P, 2, QU, GRP])
        pT = sb("pT", [P, 2, GROUPS[1], P])
        rs = sb("rs", [P, H])
        o = sb("o", [P, D])
        st = sb("st", [P, 6])
        ag = sb("ag", [P, 2])
        if fresh:
            x_all, st_all = sb("x_all", [P, TILES, D]), sb("st_all", [P, TILES, 6])
        if rope:
            wkr = sb("wkr", [P, DC, D])
            cos_k, sin_k = sb("cos_k", [P, SK]), sb("sin_k", [P, SK])
            cos, sin = sb("cos", [P, TPB, DK // 2]), sb("sin", [P, TPB, 2, DK // 2])
            rk = sb("rk", [P, B, SK])
            rt = sb("rt", [P, 2, H, 2, DK // 2])
            qr = sb("qr", [P, D])
        if mask is not None:
            mi = sb("mi", [P, 2, SK], I32)
            mb = sb("mb", [P, 2, SK], BF16)
            identb = sb("identb", [P, P], BF16)

        def ps(name, shape):
            return ctx.enter_context(nc.psum_tensor(f"{tag}_{name}", shape, F32))

        ps_s = ps("ps_s", [P, 2, BANK])
        ps_t = ps("ps_t", [P, 2, GRP, P])
        ps_m = ps("ps_m", [P, 2, DC, P])
        ps_q = ps("ps_q", [P, 2, DC, P])
        ps_v = ps("ps_v", [P, BANK])
        ps_w = ps("ps_w", [P, BANK])

        context_loaded, consts = sem("context_loaded"), sem("consts")
        if fresh:
            fresh_sums, fresh_ready = sem("fresh_sums"), sem("fresh_ready")
            all_loaded = [sem(f"all_loaded{g}") for g in range(4)]
        if rope:
            keys_turned, turned, rotated, qT_ready = (sem(n) for n in ("keys_turned", "turned", "rotated", "qT_ready"))
        if mask is not None:
            mask_ready = sem("mask_ready")
        proj_ready, proj_used, setup_done = (sem(n) for n in ("proj_ready", "proj_used", "setup_done"))
        zeroed, spread, spread_too = sem("zeroed"), sem("spread"), sem("spread_too")
        xa_loaded = [sem(f"xa_loaded{p}") for p in range(2)]
        xr_loaded = [sem(f"xr_loaded{p}") for p in range(2)]
        stored = [sem(f"stored{p}") for p in range(2)]
        y_ready, yo_ready, yo_copied, q_ready, q_copied = (sem(n) for n in (
            "y_ready", "yo_ready", "yo_copied", "q_ready", "q_copied"))
        s_ready, max_ready, sub_ready, p_ready, pT_ready, pT_copied = (sem(n) for n in (
            "s_ready", "max_ready", "sub_ready", "p_ready", "pT_ready", "pT_copied"))
        av_ready, sum_inv, o_ready, out_ready, res_done, stats = (sem(n) for n in (
            "av_ready", "sum_inv", "o_ready", "out_ready", "res_done", "stats"))

        scale_dve, scale_act = row_scale(nc, ctx, mv, scale, False, tag + "_ln")
        NCONST = 5 + (5 if rope else 0) + (1 if mask is not None else 0)
        NXA = 16 * (2 if mask is not None else 1)
        FIRST, LAST = 2, TILES - 5

        def inside(k):
            return not isinstance(k, int) or 0 <= k < TILES

        def steps(eng, step):
            for i in range(-3, FIRST):
                step(i, 0, i)
            with eng.Fori(FIRST // 2, (LAST + 1) // 2) as t:
                for c in range(2):
                    step(t * 2 + c, t, c)
            for i in range(LAST + 1, TILES + 1):
                step(i, 0, i)

        pieces = []
        for u in range(2):
            for h in range(HU):
                cut = min(SK, -(h * SK) % P)
                pieces += [(u, h, k, n) for k, n in ((0, cut), (cut, SK - cut)) if n]

        CUT = len(pieces) * 2 // 3

        def spread_values(eng, part, done):
            eng.wait_ge(zeroed, 1)
            eng.wait_ge(proj_used, B)
            for u, h, k, n in part:
                c, at = divmod(h * SK + k, P)
                eng.dma_start(vals_bd[at:at + n, :, u * UC + c, h * (DK + 1):(h + 1) * (DK + 1)],
                              vals[k:k + n, :, u * HU + h, :]).then_inc(done, 16)

        def sums(i, p):
            return xo[:, p:p + 1, :] if keep is None else keep[:, bass.ds(i, 1), 0:D]

        block = ctx.enter_context(nc.Block())

        @block.sync
        def _(sp):
            sp.dma_start(cT[:], ctxT).then_inc(context_loaded, 16)
            sp.dma_start(wv[:], wvT).then_inc(context_loaded, 16)
            for dst, src in ((wk, wkT), (bm, bmask), (ident, ident_d), (wq, wqT), (wo, woT)):
                sp.dma_start(dst[:], src).then_inc(consts, 16)
            if rope:
                for dst, src in zip((wkr, cos_k, sin_k, cos, sin), rope):
                    sp.dma_start(dst[:], src).then_inc(consts, 16)
            if mask is not None:
                sp.dma_start(identb[:], identb_d).then_inc(consts, 16)

            def store(i, p):
                sp.wait_ge(res_done, i + 1)
                sp.nop(nofuse=True)
                sp.dma_start(x_out[i].unsqueeze(1), sums(i, p)).then_inc(stored[p], 16)

            for p in range(2):
                sp.sem_inc(stored[p], 16)
                sp.dma_start(xr[:, p, :], x_in[p]).then_inc(xr_loaded[p], 16)
            spread_values(sp, pieces[:CUT], spread)
            for dst, src, done in also:
                sp.dma_start(dst, src).then_inc(done, 16)
            with sp.Fori(0, TILES // 2 - 1) as t:
                for p in range(2):
                    i = t * 2 + p
                    store(i, p)
                    sp.dma_start(xr[:, p, :], x_in[i + 2]).then_inc(xr_loaded[p], 16)
            for p in range(2):
                store(TILES - 2 + p, p)
            for p in range(2):
                sp.wait_ge(stored[p], 16 * (TILES // 2 + 1))

        @block.gpsimd
        def _(pool):
            pool.memset(vals_bd[:], 0.0).then_inc(zeroed, 1)

            def load(i, p):
                pool.dma_start(xa[:, p, :], x_in[i]).then_inc(xa_loaded[p], 16)
                if mask is not None:
                    pool.dma_start(mi[:, p, :], mask[i]).then_inc(xa_loaded[p], 16)

            for p in range(2):
                load(p, p)
            spread_values(pool, pieces[CUT:], spread_too)
            with pool.Fori(0, TILES // 2 - 1) as t:
                for p in range(2):
                    i = t * 2 + p
                    pool.wait_ge(y_ready, i + 1)
                    pool.nop(nofuse=True)
                    if mask is not None:
                        pool.wait_ge(mask_ready, i + 1)
                        pool.nop(nofuse=True)
                    load(i + 2, p)

        @block.tensor
        def _(pe):
            pe.wait_ge(context_loaded, 32)
            n = 0
            for b in range(B):
                if n >= 2:
                    pe.wait_ge(proj_used, n - 1)
                for k in range(DC):
                    last = pe.matmul(ps_s[0:SK, n % 2, 0:D], cT[:, k, b * SK:(b + 1) * SK], wv[:, k, :],
                                     start=(k == 0), stop=(k == DC - 1))
                last.then_inc(proj_ready, 1)
                n += 1
            pe.wait_ge(consts, 16 * NCONST)
            for c in range(DC):
                for w in ((wk, wkr) if rope else (wk,)):
                    pe.wait_ge(proj_used, n - 1)
                    for k in range(DC):
                        last = pe.matmul(ps_s[:, n % 2, 0:B * SK], w[:, k, c * P:(c + 1) * P], cT[:, k, :],
                                         start=(k == 0), stop=(k == DC - 1))
                    last.then_inc(proj_ready, 1)
                    n += 1
            pe.wait_ge(setup_done, 1)

            def scores(j, p, k):
                if not inside(j):
                    return
                if k == 0:
                    pe.wait_ge(q_copied, j + 1)
                    if mask is not None:
                        pe.wait_ge(mask_ready, j + 1)
                if not (isinstance(j, int) and 4 * j + k < 2):
                    pe.wait_ge(sub_ready, j * QU + k - 1)
                bank = ps_s[:, k % 2, 0:GRP * SK]
                if mask is not None:
                    pe.matmul(bank, identb[:], mb[:, p, :].unsqueeze(1).broadcast_to([P, GRP, SK]), start=True, stop=False)
                pe.matmul(bank, qT[:, p, k // 2, :], keys_bd[:, k // 2, j // TPB, (k % 2) * GRP:(k % 2 + 1) * GRP, :],
                          start=(mask is None), stop=True).then_inc(s_ready, 1)

            def transposed_weights(i, p, k):
                if not inside(i):
                    return
                if k % 2 == 0:
                    pe.wait_ge(p_ready, i * 2 + k // 2 + 1)
                for c in range(GROUPS[k % 2], GROUPS[k % 2 + 1]):
                    last = pe.transpose(ps_t[:, k % 2, c - GROUPS[k % 2], :], pr[:, p, k // 2, c * P:(c + 1) * P], ident[:])
                last.then_inc(pT_ready, 1)

            def weighted_values(i, k):
                if not inside(i):
                    return
                pe.wait_ge(pT_copied, i * QU + k + 1)
                if isinstance(i, int) and i == 0 and k == 0:
                    pe.wait_ge(spread, 16 * CUT)
                    pe.wait_ge(spread_too, 16 * (len(pieces) - CUT))
                if k == 0 and not (isinstance(i, int) and i == 0):
                    pe.wait_ge(o_ready, i)
                u = k // 2
                for c in range(GROUPS[k % 2], GROUPS[k % 2 + 1]):
                    last = pe.matmul(ps_v[:, u * VW:(u + 1) * VW], pT[:, k % 2, c - GROUPS[k % 2], :],
                                     vals_bd[:, i // TPB, u * UC + c, :], start=(c == 0), stop=(c == UC - 1))
                if k == QU - 1:
                    last.then_inc(av_ready, 1)

            def step(i, t, c):
                if isinstance(i, int) and i == -3:
                    return
                scores(i + 1, (c + 1) % 2, 0)
                transposed_weights(i, c % 2, 0)
                transposed_weights(i, c % 2, 1)
                if inside(i + 2):
                    pe.wait_ge(y_ready, i + 3)
                    for k in range(DC):
                        last = pe.transpose(ps_m[:, 0, k, :], y[:, c % 2, k * P:(k + 1) * P], ident[:])
                if inside(i - 1):
                    pe.wait_ge(o_ready, i)
                    for k in range(DC):
                        last = pe.transpose(ps_m[:, 1, k, :], o[:, k * P:(k + 1) * P], ident[:])
                last.then_inc(yo_ready, 1)
                scores(i + 1, (c + 1) % 2, 1)
                weighted_values(i, 0)
                transposed_weights(i, c % 2, 2)
                pe.wait_ge(yo_copied, i + 3)
                if inside(i + 2):
                    if not (isinstance(i, int) and i == -2):
                        pe.wait_ge(q_copied, i + 2)
                    if rope:
                        for k in range(DC):
                            last = pe.matmul(ps_q[:, 0].rearrange("p c t -> p (c t)"), yoT[:, 0, k, :], wq[:, k, :],
                                             start=(k == 0), stop=(k == DC - 1))
                    else:
                        for m in range(DC):
                            for k in range(DC):
                                last = pe.matmul(ps_q[:, 0, m, :], wq[:, k, m * P:(m + 1) * P], yoT[:, 0, k, :],
                                                 start=(k == 0), stop=(k == DC - 1))
                    last.then_inc(q_ready, 1)
                scores(i + 1, (c + 1) % 2, 2)
                weighted_values(i, 1)
                transposed_weights(i, c % 2, 3)
                if inside(i - 1):
                    if not (isinstance(i, int) and i == 1):
                        pe.wait_ge(res_done, i - 1)
                    for k in range(DC):
                        last = pe.matmul(ps_w[:, 0:D], yoT[:, 1, k, :], wo[:, k, :], start=(k == 0), stop=(k == DC - 1))
                    last.then_inc(out_ready, 1)
                weighted_values(i, 2)
                if rope and inside(i + 2):
                    pe.wait_ge(rotated, i + 3)
                    for k in range(DC):
                        last = pe.transpose(ps_q[:, 1, k, :], qr[:, k * P:(k + 1) * P], ident[:])
                    last.then_inc(qT_ready, 1)
                scores(i + 1, (c + 1) % 2, 3)
                weighted_values(i, 3)

            steps(pe, step)

        @block.scalar
        def _(act):
            for g in range(4 if fresh else 0):
                at = slice(g * TILES // 4, (g + 1) * TILES // 4)
                act.dma_start(x_all[:, at, :], x_in[at].rearrange("t p d -> p t d")).then_inc(all_loaded[g], 16)
            if not fresh:
                scale_act(act)
            if fresh:
                scale_act(act)

            def copy_weights(i, k):
                if inside(i):
                    act.wait_ge(pT_ready, i * QU + k + 1)
                    n = GROUPS[k % 2 + 1] - GROUPS[k % 2]
                    act.activation(pT[:, k % 2, 0:n], ps_t[:, k % 2, 0:n], ACT.Copy).then_inc(pT_copied, 1)

            def exps(j, p, e):
                if inside(j):
                    act.wait_ge(sub_ready, j * QU + 2 * e + 2)
                    act.activation(pr[:, p, e, 0:UW], pr[:, p, e, 0:UW], ACT.Exp,
                                   scale=float(DK) ** -0.5).then_inc(p_ready, 1)

            def step(i, t, c):
                if isinstance(i, int) and i == -3:
                    return
                copy_weights(i, 0)
                copy_weights(i, 1)
                act.wait_ge(yo_ready, i + 3)
                a, b = (0 if inside(i + 2) else 1), (2 if inside(i - 1) else 1)
                act.activation(yoT[:, a:b], ps_m[:, a:b], ACT.Copy).then_inc(yo_copied, 1)
                exps(i + 1, (c + 1) % 2, 0)
                copy_weights(i, 2)
                if not rope and inside(i + 2):
                    act.wait_ge(q_ready, i + 3)
                    act.activation(qT[:, c % 2], ps_q[:, 0], ACT.Copy).then_inc(q_copied, 1)
                copy_weights(i, 3)
                if rope and inside(i + 2):
                    act.wait_ge(qT_ready, i + 3)
                    act.activation(qT[:, c % 2], ps_q[:, 1], ACT.Copy).then_inc(q_copied, 1)
                exps(i + 1, (c + 1) % 2, 1)

            steps(act, step)

        @block.vector
        def _(dve):
            def statistics(first, last):
                n = TILES // 4
                for g in range(first, last):
                    dve.wait_ge(all_loaded[g], 16)
                    for i in range(g * n, (g + 1) * n):
                        dve.bn_stats(st_all[:, i, :], x_all[:, i, :]).then_inc(fresh_sums, 1)
                    for i in range(g * n, (g + 1) * n):
                        dve.wait_ge(fresh_sums, i + 1)
                        dve.bn_aggr(mv[:, i, :], st_all[:, i, :]).then_inc(fresh_ready, 1)

            n, m = 0, 0
            if not fresh:
                scale_dve(dve)
            dve.memset(vals[:, :, :, DK:DK + 1], 1.0)
            dve.memset(pr[:, :, :, UW:UC * P], 0.0)
            for b in range(B):
                dve.wait_ge(proj_ready, n + 1)
                last = dve.tensor_copy(vals[:, b, :, 0:DK], ps_s[0:SK, n % 2, 0:D].rearrange("p (h d) -> p h d", h=H))
                last.then_inc(proj_used, 1)
                n += 1
            if fresh:
                statistics(0, 2)
            dve.wait_ge(consts, 16 * NCONST)
            for c in range(DC):
                if rope:
                    dve.wait_ge(proj_ready, n + 1)
                    if c:
                        dve.wait_ge(keys_turned, m)
                    cos_b = cos_k[:].unsqueeze(1).broadcast_to([P, B, SK])
                    sin_b = sin_k[:].unsqueeze(1).broadcast_to([P, B, SK])
                    k0 = ps_s[:, n % 2, 0:B * SK].rearrange("p (b k) -> p b k", b=B)
                    k1 = ps_s[:, (n + 1) % 2, 0:B * SK].rearrange("p (b k) -> p b k", b=B)
                    dve.tensor_tensor(rk[:], k0, cos_b, ALU.mult).then_inc(proj_used, 1)
                    dve.wait_ge(proj_ready, n + 2)
                    tmp = pr[:, 0, 0, 0:B * SK].rearrange("p (b k) -> p b k", b=B)
                    dve.tensor_tensor(tmp, k1, sin_b, ALU.mult).then_inc(proj_used, 1)
                    dve.wait_ge(proj_used, n + 2)
                    dve.tensor_tensor(rk[:], rk[:], tmp, ALU.add).then_inc(keys_turned, 1)
                    m += 1
                    dve.wait_ge(keys_turned, m)
                    n += 2
                    for b in range(B):
                        last = dve.tensor_tensor(keys_bd[:, c, b], rk[:, b].unsqueeze(1).broadcast_to([P, HU, SK]),
                                                 bm[:].unsqueeze(2).broadcast_to([P, HU, SK]), ALU.mult)
                    last.then_inc(keys_turned, 1)
                    m += 1
                else:
                    dve.wait_ge(proj_ready, n + 1)
                    for b in range(B):
                        last = dve.tensor_tensor(
                            keys_bd[:, c, b],
                            ps_s[:, n % 2, b * SK:(b + 1) * SK].unsqueeze(1).broadcast_to([P, HU, SK]),
                            bm[:].unsqueeze(2).broadcast_to([P, HU, SK]), ALU.mult)
                    last.then_inc(proj_used, 1)
                    n += 1
            dve.wait_ge(proj_used, n)
            dve.sem_inc(setup_done, 1)
            if fresh:
                statistics(2, 4)
                dve.wait_ge(fresh_ready, TILES)
                scale_dve(dve)

            def normalise(j, half, p):
                if not inside(j):
                    return
                dve.wait_ge(xa_loaded[p], (half + 1) * NXA)
                dve.tensor_scalar(y[:, p, :], xa[:, p, :], mv[:, bass.ds(j, 1), 0], scale[:, bass.ds(j, 1)],
                                  ALU.subtract, ALU.mult).then_inc(y_ready, 1)

            def bias(j, half, p):
                if mask is not None and inside(j):
                    dve.wait_ge(xa_loaded[p], (half + 1) * NXA)
                    dve.tensor_scalar(mb[:, p, :], mi[:, p, :], 0.0, -3e38, ALU.is_equal, ALU.mult).then_inc(mask_ready, 1)

            def less_max(j, p, k):
                if not inside(j):
                    return
                dve.wait_ge(s_ready, j * QU + k + 1)
                s = ps_s[:, k % 2, 0:GRP * SK].rearrange("p (h k) -> p h k", h=GRP)
                to = pr[:, p, k // 2, (k % 2) * GRP * SK:(k % 2 + 1) * GRP * SK].rearrange("p (h k) -> p h k", h=GRP)
                dve.tensor_reduce(mx[:, p, k], s, AX.X, ALU.max).then_inc(max_ready, 1)
                dve.wait_ge(max_ready, j * QU + k + 1)
                dve.tensor_tensor(to, s, mx[:, p, k].unsqueeze(2).broadcast_to([P, GRP, SK]),
                                  ALU.subtract).then_inc(sub_ready, 1)

            def rotate(j, p):
                if not (rope and inside(j)):
                    return
                dve.wait_ge(q_ready, j + 1)
                q = ps_q[:, 0].rearrange("p c (h s e) -> p (c h) s e", s=2, e=DK // 2)
                at = bass.ds(j % TPB, 1)
                dve.tensor_tensor(rt[:, 0].rearrange("p h s e -> p (h s) e"), q.rearrange("p h s e -> p (h s) e"),
                                  cos[:, at, :].broadcast_to([P, 2 * H, DK // 2]), ALU.mult)
                for s in range(2):
                    last = dve.tensor_tensor(rt[:, 1, :, s, :], q[:, :, 1 - s, :],
                                             sin[:, at, s, :].broadcast_to([P, H, DK // 2]), ALU.mult)
                last.then_inc(turned, 1)
                dve.wait_ge(turned, j + 1)
                if not (isinstance(j, int) and j == 0):
                    dve.wait_ge(qT_ready, j)
                dve.tensor_tensor(qr[:].rearrange("p (h s e) -> p h s e", s=2, e=DK // 2), rt[:, 0], rt[:, 1],
                                  ALU.add).then_inc(rotated, 1)

            def step(i, t, c):
                less_max(i + 1, (c + 1) % 2, 0)
                less_max(i + 1, (c + 1) % 2, 1)
                normalise(i + 3, t + (c + 3) // 2, (c + 3) % 2)
                rotate(i + 2, c % 2)
                less_max(i + 1, (c + 1) % 2, 2)
                if inside(i - 1):
                    q, half = (c - 1) % 2, t + (c - 1) // 2
                    dve.wait_ge(xr_loaded[q], (half + 1) * 16)
                    dve.wait_ge(stored[q], (half + 1) * 16)
                    dve.wait_ge(out_ready, i)
                    dve.tensor_tensor(sums(i - 1, q), ps_w[:, 0:D].unsqueeze(1), xr[:, q:q + 1, :], ALU.add).then_inc(res_done, 1)
                less_max(i + 1, (c + 1) % 2, 3)
                bias(i + 3, t + (c + 3) // 2, (c + 3) % 2)
                if inside(i):
                    dve.wait_ge(av_ready, i + 1)
                    ov = ps_v[:, 0:H * (DK + 1)].rearrange("p (h e) -> p h e", h=H)
                    dve.reciprocal(rs[:].unsqueeze(2), ov[:, :, DK:DK + 1]).then_inc(sum_inv, 1)
                    dve.wait_ge(sum_inv, i + 1)
                    dve.tensor_tensor(o[:].rearrange("p (h e) -> p h e", h=H), ov[:, :, 0:DK],
                                      rs[:].unsqueeze(2).broadcast_to([P, H, DK]), ALU.mult).then_inc(o_ready, 1)
                if inside(i - 1):
                    dve.wait_ge(res_done, i)
                    dve.nop(nofuse=True)
                    dve.bn_stats(st[:], sums(i - 1, q).rearrange("p a d -> p (a d)")).then_inc(stats, 1)
                if inside(i - 1):
                    dve.wait_ge(stats, i * 2 - 1)
                    dve.nop(nofuse=True)
                    dve.bn_aggr(ag[:], st[:]).then_inc(stats, 1)
                    dve.wait_ge(stats, i * 2)
                    dve.nop(nofuse=True)
                    dve.tensor_copy(mv[:, bass.ds(i - 1, 1), :], ag[:].unsqueeze(1))

            steps(dve, step)


KH = PH * TOPK
NF = 32
PARTS = 2
SEL = 2 + PARTS
PAIRS = TILES // 2
WS = 2.0 ** 15
YS, DS = 2.0 ** 11, 2.0 ** 14
TG = 16
TB = 8


class ProductKeys:

    def __init__(self, nc, ctx):
        NS = 2 * PH
        self.hid = ctx.enter_context(nc.sbuf_tensor("pb_hid", [P, 2, NF, 2 * P], F32))
        self.nw = ctx.enter_context(nc.sbuf_tensor("pb_nw", [P, DC], F32))
        self.wq = self.hid[:, 0, 0:NS, :]
        self.kT = self.hid[:, 0, NS:NS + NS * NKEYS // (2 * P), :].rearrange("p a (b k) -> p (a b) k", k=NKEYS)
        self.raw = self.hid[:, 1].rearrange("p f t -> p (f t)").rearrange("p (c n) -> p c n", c=DC)
        self.keys_loaded = ctx.enter_context(nc.semaphore("pb_keys_loaded"))
        self.down_loaded = ctx.enter_context(nc.semaphore("pb_down_loaded"))

    def loads(self, a):
        return [(self.wq, a["w_q"], self.keys_loaded), (self.kT, a["keysT"], self.keys_loaded),
                (self.nw[:], a["norm_w"], self.keys_loaded),
                (self.raw, a["down"].rearrange("p c f r -> p c (f r)"), self.down_loaded)]


def product_key_experts(nc, x_in, x_out, mv, pk, up_d, ident_d, identh_d, iota8_d, iota_d):
    with ExitStack() as ctx:
        def sb(name, shape, dt=F32):
            return ctx.enter_context(nc.sbuf_tensor("pe_" + name, shape, dt))

        def sem(name):
            return ctx.enter_context(nc.semaphore("pe_" + name))

        def ps(name, shape, dt=F32):
            return ctx.enter_context(nc.psum_tensor("pe_" + name, shape, dt))

        NS = 2 * PH
        T2 = 2 * P
        NB = P // TB
        NG = P // TG
        BPG = NB // NG
        HG = NF // 2
        down_hi, down_lo = sb("down_hi", [P, DC, NF, P], F16), sb("down_lo", [P, DC, NF, P], F16)
        up = sb("up", [P, NF, D])
        fold_hi, fold_lo = sb("fold_hi", [P, DC, NS * NKEYS], F16), sb("fold_lo", [P, DC, NS * NKEYS], F16)
        xT = sb("xT", [P, 2, DC, T2])
        x_hi, x_lo = sb("x_hi", [P, 2, DC, T2], F16), sb("x_lo", [P, 2, DC, T2], F16)
        hid, nw, wq, kT, raw = pk.hid, pk.nw, pk.wq, pk.kT, pk.raw
        fold = hid[:, 0, NS + NS // 4:NS + NS // 4 + NS * NKEYS * DC // T2, :].rearrange("p a b -> p (a b)")
        peak, peaks, most = sb("peak", [P, DC]), sb("peaks", [P, 2]), sb("most", [1, 2])
        one_row = sb("one_row", [1, P])
        unit, fit, back = sb("unit", [P, 2]), sb("fit", [P, 2]), sb("back", [P, 2])
        to_fit = sb("to_fit", [P, DC])
        ident, identh = sb("ident", [P, P]), sb("identh", [P, P], F16)
        scale = sb("scale", [P, TILES])
        x, y = sb("x", [P, 2, D]), sb("y", [P, 2, D])
        iota8 = sb("iota8", [P, TOPK, TOPK], BF16)
        sim = sb("sim", [P, 2, NS, NKEYS])
        HS = 2 * PH
        top, topi = sb("top", [P, 2 * NS, TOPK]), sb("topi", [P, 2 * NS, TOPK], U32)
        topf = sb("topf", [P, 2 * NS, TOPK], BF16)
        grid = sb("grid", [P, HS, TOPK, TOPK])
        best, bi = sb("best", [P, HS, TOPK]), sb("bi", [P, HS, TOPK], U32)
        ab, abf = sb("ab", [P, 2, HS, TOPK], U32), sb("abf", [P, 2, HS, TOPK], BF16)
        hit = sb("hit", [P, 2, HS, TOPK, TOPK], BF16)
        ij = sb("ij", [P, 2, HS, TOPK])
        far, col = sb("far", [P, HS, TOPK]), sb("col", [P, HS, TOPK])
        w = sb("w", [P, HS, TOPK])
        w_max, w_inv = sb("w_max", [P, 2]), sb("w_inv", [P, 2])
        w_unit = sb("w_unit", [P, 2, 2])
        sel = sb("sel", [P, SEL, 2, KH], F16)
        selT = sb("selT", [P, SEL, P], F16)
        iota = sb("iota", [P, P, TG], F16)
        rows = sb("rows", [P, 2, P, TG], F16)
        eq = sb("eq", [P, 2 * NF, TG], F16)
        cols = sb("cols", [P, 2, PARTS, 2 * NF, TG], F16)
        xr, xo = sb("xr", [P, 2, D]), sb("xo", [P, 2, D])
        st, ag = sb("st", [P, 2, 6]), sb("ag", [P, 2, 2])
        ps_h, ps_w, ps_o = ps("ps_h", [P, 2, 2, T2]), ps("ps_w", [P, 2, TB, 2, NF]), ps("ps_o", [P, 2, D])
        ps_s, ps_t = ps("ps_s", [P, 2, BANK]), ps("ps_t", [P, DC, T2])
        ps_sel = ps_t[:].rearrange("p c t -> p (c t)").bitcast(F16)[:, 0:SEL * P].rearrange("p (k t) -> p k t", k=SEL)

        consts, up_loaded = sem("consts"), sem("up_loaded")
        limit, most_ready, fit_ready, hi_ready, down_split, x_split = (sem(n) for n in (
            "limit", "most_ready", "fit_ready", "hi_ready", "down_split", "x_split"))
        fit_step = sem("fit_step")
        fold_ready, fold_copied, fold_split = sem("fold_ready"), sem("fold_copied"), sem("fold_split")
        x_loaded, xr_loaded, stored = sem("x_loaded"), sem("xr_loaded"), sem("stored")
        y_ready, yT_ready, xT_ready, s_ready, sim_ready = (sem(n) for n in (
            "y_ready", "yT_ready", "xT_ready", "s_ready", "sim_ready"))
        chain, sel_ready, selT_ready, selT_copied = (sem(n) for n in ("chain", "sel_ready", "selT_ready", "selT_copied"))
        h_ready, hid_ready, one_hot, eq_ready, w_ready, weighted = (sem(n) for n in (
            "h_ready", "hid_ready", "one_hot", "eq_ready", "w_ready", "weighted"))
        out_ready, summed, stats = sem("out_ready"), sem("summed"), sem("stats")
        scale_dve, scale_act = row_scale(nc, ctx, mv, scale, True, "pe_ln")
        STEPS = 12
        block = ctx.enter_context(nc.Block())

        def pair_of(ap, m):
            return ap[bass.ds(m * 2, 2)].rearrange("q p d -> p q d")

        @block.sync
        def _(sp):
            sp.dma_start(x[:], pair_of(x_in, 0)).then_inc(x_loaded, 16)
            for dst, src in ((ident, ident_d), (identh, identh_d), (iota8, iota8_d), (iota, iota_d)):
                sp.dma_start(dst[:], src).then_inc(consts, 16)
            sp.dma_start(up[:], up_d).then_inc(up_loaded, 16)

            def load(m):
                sp.wait_ge(y_ready, m)
                sp.dma_start(x[:], pair_of(x_in, m)).then_inc(x_loaded, 16)

            def residual(m):
                sp.dma_start(xr[:], pair_of(x_in, m)).then_inc(xr_loaded, 16)

            def store(m):
                sp.wait_ge(summed, m * 2 + 2)
                sp.dma_start(pair_of(x_out, m), xo[:]).then_inc(stored, 16)

            load(1)
            load(2)
            residual(0)
            with sp.Fori(0, PAIRS - 3) as m:
                sp.wait_ge(y_ready, m + 3)
                sp.nop(nofuse=True)
                sp.dma_start(x[:], pair_of(x_in, m + 3)).then_inc(x_loaded, 16)
                sp.wait_ge(summed, m * 2 + 2)
                sp.nop(nofuse=True)
                sp.dma_start(pair_of(x_out, m), xo[:]).then_inc(stored, 16)
                residual(m + 1)
            for m in range(PAIRS - 3, PAIRS):
                store(m)
                if m < PAIRS - 1:
                    residual(m + 1)
            sp.wait_ge(stored, 16 * PAIRS)

        @block.tensor
        def _(pe):
            pe.wait_ge(pk.keys_loaded, 48)
            for c in range(DC):
                if c:
                    pe.wait_ge(fold_copied, c)
                for s in range(NS):
                    last = pe.matmul(ps_s[:, s // PH, (s % PH) * NKEYS:(s % PH + 1) * NKEYS],
                                     wq[:, s, c * P:(c + 1) * P], kT[:, s, :], start=True, stop=True)
                last.then_inc(fold_ready, 1)
            pe.wait_ge(consts, 16 * 4)

            def turn(m):
                pe.wait_ge(y_ready, m + 1)
                if not (isinstance(m, int) and m < 2):
                    pe.wait_ge(selT_copied, m - 1)
                elif m == 1:
                    pe.wait_ge(xT_ready, 1)
                for q in range(2):
                    for c in range(DC):
                        last = pe.transpose(ps_t[:, c, q * P:(q + 1) * P], y[:, q, c * P:(c + 1) * P], ident[:])
                last.then_inc(yT_ready, 1)

            def similarities(m, p, q, quarter):
                i = m * 2 + q
                if quarter == 0:
                    if isinstance(i, int) and i == 0:
                        pe.wait_ge(fold_split, 1)
                    else:
                        pe.wait_ge(sim_ready, i)
                g, k = divmod(quarter, DC)
                for n, (x_part, w_part) in enumerate(((x_hi, fold_hi), (x_lo, fold_hi), (x_hi, fold_lo))):
                    last = pe.matmul(ps_s[:, g, :], x_part[:, p, k, q * P:(q + 1) * P], w_part[:, k, g * BANK:(g + 1) * BANK],
                                     start=(k == 0 and n == 0), stop=(k == DC - 1 and n == 2))
                if quarter == 3:
                    last.then_inc(s_ready, 1)

            def hidden(m, p, g):
                if g == 0:
                    pe.wait_ge(x_split, m + 1)
                n = m * HG + g
                if not (isinstance(n, int) and n < 2):
                    pe.wait_ge(hid_ready, n - 1)
                for j in range(2):
                    f = 2 * g + j
                    for c in range(DC):
                        for n, (w_part, x_part) in enumerate(((down_hi, x_hi), (down_hi, x_lo), (down_lo, x_hi))):
                            last = pe.matmul(ps_h[:, g % 2, j, :], w_part[:, c, f, :], x_part[:, p, c, :],
                                             start=(c == 0 and n == 0), stop=(c == DC - 1 and n == 2))
                last.then_inc(h_ready, 1)

            def weights(m, g):
                n = m * NB + g
                if g % BPG == 0:
                    pe.wait_ge(one_hot, m * NG + g // BPG + 1)
                if not (isinstance(n, int) and n < 2):
                    pe.wait_ge(weighted, n - 1)
                buf = (g // BPG) % 2
                for t in range(TB):
                    at = (g % BPG) * TB + t
                    for k in range(PARTS):
                        last = pe.matmul(ps_w[:, g % 2, t].rearrange("p q f -> p (q f)"), rows[:, buf, :, at],
                                         cols[:, buf, k, :, at], start=(k == 0), stop=(k == PARTS - 1))
                last.then_inc(w_ready, 1)

            def outputs(m, p, between=None):
                pe.wait_ge(weighted, (m + 1) * NB)
                if not (isinstance(m, int) and m == 0):
                    pe.wait_ge(summed, m * 2)
                for q in range(2):
                    for f in range(NF):
                        last = pe.matmul(ps_o[:, q, :], hid[:, p, f, q * P:(q + 1) * P], up[:, f, :],
                                         start=(f == 0), stop=(f == NF - 1))
                        if between and q == 1 and f == NF - 12:
                            between()
                last.then_inc(out_ready, 1)

            def selections(m):
                pe.wait_ge(sel_ready, m + 1)
                pe.wait_ge(xT_ready, m + 2 if not (isinstance(m, int) and m == PAIRS - 1) else PAIRS)
                for k in range(SEL):
                    last = pe.transpose(ps_sel[:, k, :], sel[:, k].rearrange("p q k -> p (q k)"), identh[:])
                last.then_inc(selT_ready, 1)

            def step(m, p, turns=True):
                for k in range(NG):
                    for b in range(BPG):
                        weights(m, k * BPG + b)
                    for g in range(k * HG // NG, (k + 1) * HG // NG):
                        hidden(m + 1, 1 - p, g)
                    similarities(m + 1, 1 - p, k * 2 // NG, k % 4)
                if turns:
                    turn(m + 2)
                outputs(m, p, between=lambda: selections(m + 1))

            turn(0)
            pe.wait_ge(limit, 4)
            for k in range(2):
                last = pe.transpose(ps_o[0:1, 0, k * P:(k + 1) * P], peaks[:, k:k + 1], ident[:])
            last.then_inc(most_ready, 1)
            pe.wait_ge(limit, 5)
            pe.matmul(ps_o[:, 1, 0:2], one_row[:], most[:], start=True, stop=True).then_inc(most_ready, 1)
            pe.wait_ge(x_split, 1)
            for q in range(2):
                for quarter in range(4):
                    similarities(0, 0, q, quarter)
            turn(1)
            pe.wait_ge(down_split, 1)
            for g in range(HG):
                hidden(0, 0, g)
            selections(0)
            pe.wait_ge(up_loaded, 16)
            step(0, 0)
            step(1, 1)
            with pe.Fori(1, PAIRS // 2 - 1) as mm:
                for p in range(2):
                    step(mm * 2 + p, p)
            step(PAIRS - 2, 0, turns=False)
            for g in range(NB):
                weights(PAIRS - 1, g)
            outputs(PAIRS - 1, 1)

        @block.scalar
        def _(act):
            act.wait_ge(pk.keys_loaded, 48)
            for c in range(DC):
                act.wait_ge(fold_ready, c + 1)
                act.activation(fold[:, c * NS * NKEYS:(c + 1) * NS * NKEYS], ps_s[:].rearrange("p g n -> p (g n)"), ACT.Copy,
                               scale=nw[:, c:c + 1]).then_inc(fold_copied, 1)
            scale_act(act)
            act.wait_ge(consts, 16 * 4)

            def turned(m, p):
                act.wait_ge(yT_ready, m + 1)
                act.activation(x_hi[:, p], ps_t[:], ACT.Copy, scale=YS)
                act.activation(xT[:, p], ps_t[:], ACT.Copy).then_inc(xT_ready, 1)

            def similarities(m, q):
                i = m * 2 + q
                act.wait_ge(s_ready, i + 1)
                if not (isinstance(m, int) and m == 0):
                    act.wait_ge(chain, (m - 1) * STEPS + 3)
                act.activation(sim[:, q].rearrange("p s k -> p (s k)"), ps_s[:].rearrange("p g n -> p (g n)"),
                               ACT.Copy, scale=back[:, 1:2]).then_inc(sim_ready, 1)

            def gelu(m, p, g):
                if g == 0 and not (isinstance(m, int) and m < 2):
                    act.wait_ge(out_ready, m - 1)
                act.wait_ge(h_ready, m * HG + g + 1)
                act.activation(hid[:, p, 2 * g:2 * g + 2, :], ps_h[:, g % 2], ACT.Gelu,
                               scale=back[:, 0:1]).then_inc(hid_ready, 1)

            def selections(m):
                act.wait_ge(selT_ready, m + 1)
                if not (isinstance(m, int) and m == 0):
                    act.wait_ge(one_hot, m * NG)
                act.activation(selT[:], ps_sel, ACT.Copy).then_inc(selT_copied, 1)

            def step(m, p, turns=True):
                for g in range(HG):
                    gelu(m + 1, 1 - p, g)
                    if g == HG // 2 - 1:
                        similarities(m + 1, 0)
                similarities(m + 1, 1)
                if turns:
                    turned(m + 2, p)
                selections(m + 1)

            turned(0, 0)
            act.wait_ge(fit_ready, 1)
            act.activation(fold_hi[:].rearrange("p c n -> p (c n)"), fold, ACT.Copy, scale=fit[:, 1:2]).then_inc(hi_ready, 1)
            for c in range(DC):
                act.activation(down_hi[:, c].rearrange("p f r -> p (f r)"), raw[:, c], ACT.Copy,
                               scale=to_fit[:, c:c + 1]).then_inc(hi_ready, 1)
            for q in range(2):
                similarities(0, q)
            turned(1, 1)
            for g in range(HG):
                gelu(0, 0, g)
            selections(0)
            step(0, 0)
            step(1, 1)
            with act.Fori(1, PAIRS // 2 - 1) as mm:
                for p in range(2):
                    step(mm * 2 + p, p)
            step(PAIRS - 2, 0, turns=False)

        @block.vector
        def _(dve):
            dve.memset(one_row[:], 1.0).then_inc(limit, 1)
            dve.wait_ge(pk.down_loaded, 16)
            dve.tensor_reduce(peak[:], raw, AX.X, ALU.max, apply_absolute_value=True).then_inc(limit, 1)
            dve.wait_ge(limit, 2)
            dve.wait_ge(pk.keys_loaded, 48)
            dve.tensor_tensor(peak[:], peak[:], nw[:], ALU.mult).then_inc(fit_step, 1)
            dve.wait_ge(fit_step, 1)
            dve.tensor_reduce(peaks[:, 0:1], peak[:], AX.X, ALU.max, apply_absolute_value=True).then_inc(limit, 1)
            dve.wait_ge(fold_copied, DC)
            dve.tensor_reduce(peaks[:, 1:2], fold, AX.X, ALU.max, apply_absolute_value=True).then_inc(limit, 1)
            scale_dve(dve)
            dve.wait_ge(consts, 16 * 4)

            def norm(m):
                dve.wait_ge(x_loaded, m * 16 + 16)
                if not (isinstance(m, int) and m == 0):
                    dve.wait_ge(yT_ready, m)
                for q in range(2):
                    i = m * 2 + q
                    last = dve.tensor_scalar(y[:, q, :], x[:, q, :], mv[:, bass.ds(i, 1), 0], scale[:, bass.ds(i, 1)],
                                             ALU.subtract, ALU.mult)
                last.then_inc(y_ready, 1)

            def winners(m, p):
                n = [0]

                def settle(ins):
                    n[0] += 1
                    ins.then_inc(chain, 1)
                    dve.wait_ge(chain, m * STEPS + n[0])
                    dve.nop(nofuse=True)

                for q in range(2):
                    dve.wait_ge(sim_ready, m * 2 + q + 1)
                    dve.nop(nofuse=True)
                    for s in range(NS):
                        last = dve.max(top[:, q * NS + s, :], sim[:, q, s, :])
                    settle(last)
                    for s in range(NS):
                        last = dve.max_index(topi[:, q * NS + s, :], top[:, q * NS + s, :], sim[:, q, s, :])
                t2 = top[:].rearrange("p (h s) k -> p h s k", s=2)
                settle(dve.tensor_tensor(grid[:], t2[:, :, 0].unsqueeze(3).broadcast_to([P, HS, TOPK, TOPK]),
                                         t2[:, :, 1].unsqueeze(2).broadcast_to([P, HS, TOPK, TOPK]), ALU.add))
                for h in range(HS):
                    last = dve.max(best[:, h, :], grid[:, h].rearrange("p a b -> p (a b)"))
                settle(last)
                for h in range(HS):
                    last = dve.max_index(bi[:, h, :], best[:, h, :], grid[:, h].rearrange("p a b -> p (a b)"))
                dve.tensor_copy(topf[:], topi[:])
                settle(dve.tensor_reduce(w_max[:], best[:].rearrange("p (q h) k -> p q (h k)", q=2), AX.X, ALU.max))
                if not (isinstance(m, int) and m < 2):
                    dve.wait_ge(summed, m * 2 - 2)
                    dve.nop(nofuse=True)
                dve.tensor_scalar(w_unit[:, p], w_max[:], 1e-30, 1.0 / WS, ALU.max, ALU.mult)
                dve.tensor_scalar(ab[:, 0], bi[:], 3, None, ALU.logical_shift_right)
                settle(dve.tensor_scalar(ab[:, 1], bi[:], 7, None, ALU.bitwise_and))
                if not (isinstance(m, int) and m == 0):
                    dve.wait_ge(selT_ready, m)
                    dve.nop(nofuse=True)

                def kind(k):
                    return sel[:, k].rearrange("p q (h k) -> p (q h) k", h=PH)

                dve.reciprocal(w_inv[:], w_unit[:, p])
                settle(dve.tensor_copy(abf[:], ab[:]))
                for q in range(2):
                    dve.tensor_scalar(w[:, q * PH:(q + 1) * PH], best[:, q * PH:(q + 1) * PH], 0.0, w_inv[:, q:q + 1],
                                      ALU.max, ALU.mult)
                for s in range(2):
                    last = dve.tensor_tensor(hit[:, s], abf[:, s].unsqueeze(2).broadcast_to([P, HS, TOPK, TOPK]),
                                             iota8[:].unsqueeze(1).broadcast_to([P, HS, TOPK, TOPK]), ALU.is_equal)
                settle(last)
                tf = topf[:].rearrange("p (h s) k -> p s h k", s=2)
                dve.tensor_copy(kind(2), w[:])
                for s in range(2):
                    last = dve.tensor_tensor(hit[:, s], hit[:, s],
                                             tf[:, s].unsqueeze(3).broadcast_to([P, HS, TOPK, TOPK]), ALU.mult)
                settle(last)
                dve.tensor_tensor(kind(3), w[:], kind(2), ALU.subtract)
                for s in range(2):
                    last = dve.tensor_reduce(ij[:, s], hit[:, s].rearrange("p h c k -> p h k c"), AX.X, ALU.add)
                settle(last)
                settle(dve.tensor_scalar(far[:], ij[:, 1], float(NF), None, ALU.is_ge))
                dve.scalar_tensor_tensor(kind(0), ij[:, 0], 2.0, far[:], ALU.mult, ALU.add)
                settle(dve.scalar_tensor_tensor(col[:], far[:], -float(NF), ij[:, 1], ALU.mult, ALU.add))
                for q in range(2):
                    last = dve.tensor_scalar(kind(1)[:, q * PH:(q + 1) * PH], col[:, q * PH:(q + 1) * PH],
                                             float(NF * q), None, ALU.add)
                last.then_inc(sel_ready, 1)
                assert n[0] == STEPS, n[0]

            def expand(m, k):
                if k == 0:
                    dve.wait_ge(selT_copied, m + 1)
                buf = k % 2
                if not (isinstance(m, int) and m == 0 and k < 2):
                    dve.wait_ge(w_ready, m * NB + (k - 1) * BPG)
                    dve.wait_ge(one_hot, m * NG + k)
                elif k == 1:
                    dve.wait_ge(one_hot, 1)
                at = slice(k * TG, (k + 1) * TG)
                dve.tensor_tensor(eq[:], selT[:, 1, at].unsqueeze(1).broadcast_to([P, 2 * NF, TG]),
                                  iota[:, 0:2 * NF, :], ALU.is_equal).then_inc(eq_ready, 1)
                dve.tensor_tensor(rows[:, buf], selT[:, 0, at].unsqueeze(1).broadcast_to([P, P, TG]), iota[:],
                                  ALU.is_equal)
                dve.wait_ge(eq_ready, m * NG + k + 1)
                dve.tensor_tensor(cols[:, buf], eq[:].unsqueeze(1).broadcast_to([P, PARTS, 2 * NF, TG]),
                                  selT[:, 2:SEL, at].unsqueeze(2).broadcast_to([P, PARTS, 2 * NF, TG]),
                                  ALU.mult).then_inc(one_hot, 1)

            def weigh(m, p, k):
                if k == 0:
                    dve.wait_ge(hid_ready, m * HG + HG)
                for g in range(k * BPG, (k + 1) * BPG):
                    dve.wait_ge(w_ready, m * NB + g + 1)
                    v = hid[:, p].rearrange("p f (q t) -> p t q f", q=2)[:, g * TB:(g + 1) * TB]
                    dve.tensor_tensor(v, v, ps_w[:, g % 2], ALU.mult).then_inc(weighted, 1)

            def finish(m, p):
                dve.wait_ge(out_ready, m + 1)
                dve.wait_ge(xr_loaded, m * 16 + 16)
                if not (isinstance(m, int) and m == 0):
                    dve.wait_ge(stored, m * 16)
                for q in range(2):
                    dve.scalar_tensor_tensor(xo[:, q, :], ps_o[:, q, :], w_unit[:, p, q:q + 1], xr[:, q, :],
                                             ALU.mult, ALU.add).then_inc(summed, 1)
                dve.wait_ge(summed, m * 2 + 2)
                dve.bn_stats(st[:, 0, :], xo[:, 0, :])
                dve.bn_stats(st[:, 1, :], xo[:, 1, :]).then_inc(stats, 1)
                dve.wait_ge(stats, m * 2 + 1)
                dve.nop(nofuse=True)
                dve.bn_aggr(ag[:, 0, :], st[:, 0, :])
                dve.bn_aggr(ag[:, 1, :], st[:, 1, :]).then_inc(stats, 1)
                dve.wait_ge(stats, m * 2 + 2)
                dve.nop(nofuse=True)
                dve.tensor_copy(mv[:, bass.ds(m * 2, 2), :], ag[:])

            def step(m, p, before=True, turns=True, follows=True):
                if turns:
                    norm(m + 2)
                expand(m, 0)
                for k in range(NG):
                    if k < NG - 1:
                        expand(m, k + 1)
                    weigh(m, p, k)
                    if k == 6 and before:
                        finish(m - 1, 1 - p)
                if follows:
                    winners(m + 1, 1 - p)
                if turns:
                    split(m + 2, p)

            def split(m, p):
                dve.wait_ge(xT_ready, m + 1)
                dve.scalar_tensor_tensor(x_lo[:, p], xT[:, p], YS, x_hi[:, p], ALU.mult, ALU.subtract).then_inc(x_split, 1)

            norm(0)
            norm(1)
            dve.wait_ge(most_ready, 1)
            dve.tensor_reduce(most[:], ps_o[0:1, 0, 0:2 * P].rearrange("p (k n) -> p k n", k=2), AX.X, ALU.max).then_inc(limit, 1)
            dve.wait_ge(most_ready, 2)
            dve.tensor_scalar(unit[:], ps_o[:, 1, 0:2], 1e-30, 1.0 / DS, ALU.max, ALU.mult).then_inc(fit_step, 1)
            dve.wait_ge(fit_step, 2)
            dve.reciprocal(fit[:], unit[:]).then_inc(fit_step, 1)
            dve.tensor_scalar(back[:], unit[:], 1.0 / YS, None, ALU.mult)
            dve.wait_ge(fit_step, 3)
            dve.tensor_scalar(to_fit[:], nw[:], fit[:, 0:1], None, ALU.mult).then_inc(fit_ready, 1)
            dve.wait_ge(fit_ready, 1)
            dve.wait_ge(hi_ready, 1)
            dve.scalar_tensor_tensor(fold_lo[:].rearrange("p c n -> p (c n)"), fold, fit[:, 1:2],
                                     fold_hi[:].rearrange("p c n -> p (c n)"), ALU.mult, ALU.subtract).then_inc(fold_split, 1)
            split(0, 0)
            for c in range(DC):
                dve.wait_ge(hi_ready, c + 2)
                last = dve.scalar_tensor_tensor(down_lo[:, c].rearrange("p f r -> p (f r)"), raw[:, c], to_fit[:, c:c + 1],
                                                down_hi[:, c].rearrange("p f r -> p (f r)"), ALU.mult, ALU.subtract)
            last.then_inc(down_split, 1)
            winners(0, 0)
            split(1, 1)
            step(0, 0, before=False)
            step(1, 1)
            with dve.Fori(1, PAIRS // 2 - 1) as mm:
                for p in range(2):
                    step(mm * 2 + p, p)
            step(PAIRS - 2, 0, turns=False)
            step(PAIRS - 1, 1, turns=False, follows=False)
            finish(PAIRS - 1, 1)


ROW = D + 4
NOBODY = 4 * N
BATCH = 8


class Routed:

    def __init__(self, nc, ctx):
        def sb(name, shape):
            return ctx.enter_context(nc.sbuf_tensor("rd_" + name, shape, F32))

        self.rows = sb("rows", [P, TILES, ROW])
        self.w1, self.w2 = sb("w1", [P, E8, DC, D]), sb("w2", [P, E8, DC, D])
        self.b1, self.b2 = sb("b1", [P, E8, DC]), sb("b2", [P, E8, D])
        self.wr, self.br = sb("wr", [P, DC, E8]), sb("br", [P, E8])
        self.ident, self.upper = sb("ident", [P, P]), sb("upper", [P, P])
        self.iota = sb("iota", [P, E8])
        self.number = sb("number", [P, TILES])
        self.filled = ctx.enter_context(nc.semaphore("rd_filled"))
        self.loaded = ctx.enter_context(nc.semaphore("rd_loaded"))

    def loads(self, a, slots_d):
        blank = a["blank"].broadcast_to([E8 * CAP, ROW])
        names = ("wr", "br", "ident", "upper", "iota_e", "number", "w1", "b1", "w2", "b2")
        here = (self.wr, self.br, self.ident, self.upper, self.iota, self.number, self.w1, self.b1, self.w2, self.b2)
        self.count = len(names)
        return [(slots_d, blank, self.filled)] + [(t[:], a[n], self.loaded) for n, t in zip(names, here)]


def routed_experts(nc, out, mv, slots_d, rd):
    with ExitStack() as ctx:
        def sb(name, shape, dt=F32):
            return ctx.enter_context(nc.sbuf_tensor("re_" + name, shape, dt))

        def sem(name):
            return ctx.enter_context(nc.semaphore("re_" + name))

        def ps(name, shape, dt=F32):
            return ctx.enter_context(nc.psum_tensor("re_" + name, shape, dt))

        NBATCH, BP = TILES // BATCH, BATCH // 2
        BE, EB = [P, BATCH, E8], [P, E8, BATCH]
        ST = CAP // P
        MEAN, FACTOR, GATE, NUMBER = range(D, ROW)
        rows, number, iota, wr, br, ident, upper = rd.rows, rd.number, rd.iota, rd.wr, rd.br, rd.ident, rd.upper
        ones = sb("ones", [P, P])
        scale = sb("scale", [P, TILES])
        y, yT = sb("y", [P, 2, 2, D]), sb("yT", [P, 2, DC, 2, P])
        lg, d, ex, eq, oh = (sb(n, [P, NBATCH, BATCH, E8]) for n in ("lg", "d", "ex", "eq", "oh"))
        tot, inc, pos = (sb(n, [P, NBATCH, E8, BATCH]) for n in ("tot", "inc", "pos"))
        within = sb("within", EB)
        mx, se, gate, first, rank, keep, slot = (sb(n, [P, TILES]) for n in (
            "mx", "se", "gate", "first", "rank", "keep", "slot"))
        put = sb("put", [P, TILES], U32)
        b1, b2, w1, w2 = rd.b1, rd.b2, rd.w1, rd.w2
        taken = sb("taken", [P, E8, ST, ROW])
        back = sb("back", [P, E8, ST], U32)
        e_in, e_out = sb("e_in", [P, 2, ST, D]), sb("e_out", [P, 2, ST, D])
        eT, hT = sb("eT", [P, 2, DC, CAP]), sb("hT", [P, 2, DC, CAP])
        ps_t, ps_h, ps_e = ps("ps_t", [P, DC, CAP]), ps("ps_h", [P, DC, CAP]), ps("ps_e", [P, ST, D])
        ps_l = [ps_h[:, p, 0:BATCH * E8].rearrange("p (t e) -> p t e", e=E8) for p in range(2)]
        ps_c = [ps_e[:, p * 2, 0:2 * BATCH * E8].rearrange("p (a n) -> p a n", a=2) for p in range(2)]

        taken_loaded = [sem(f"taken_loaded{e}") for e in range(E8)]
        y_ready, yT_ready, yT_copied, l_ready, ones_ready = (sem(n) for n in (
            "y_ready", "yT_ready", "yT_copied", "l_ready", "ones_ready"))
        chain, d_ready, ex_ready, oh_ready, counted, put_ready, scattered = (sem(n) for n in (
            "chain", "d_ready", "ex_ready", "oh_ready", "counted", "put_ready", "scattered"))
        in_ready, t_ready, t_copied, h_ready, h_copied, e_ready, biased, e_done = (sem(n) for n in (
            "in_ready", "t_ready", "t_copied", "h_ready", "h_copied", "e_ready", "biased", "e_done"))
        returned = [sem(f"returned{p}") for p in range(2)]
        scale_dve, scale_act = row_scale(nc, ctx, mv, scale, False, "re_ln")
        block = ctx.enter_context(nc.Block())

        @block.sync
        def _(sp):
            sp.wait_ge(scattered, 16 * TILES)
            for e in range(E8):
                sp.dma_start(taken[:, e], slots_d[e * CAP:(e + 1) * CAP, :].rearrange("(s p) d -> p s d", p=P)
                             ).then_inc(taken_loaded[e], 16)

        @block.gpsimd
        def _(pool):
            pool.wait_ge(rd.filled, 16)
            for i in range(TILES):
                if i % BATCH == 0:
                    pool.wait_ge(put_ready, i // BATCH + 1)
                pool.indirect_dma_start(slots_d, bass.IndirectOffsetOnAxis(ap=put[:, i:i + 1], axis=0),
                                        rows[:, i, :], None, bounds_check=E8 * CAP - 1,
                                        oob_is_err=False).then_inc(scattered, 16)
            out_rows = out.rearrange("t p d -> (t p) d")
            pool.wait_ge(scattered, 16 * TILES)
            for e in range(E8):
                for s in range(ST):
                    pool.wait_ge(e_done, e * ST + s + 1)
                    pool.indirect_dma_start(out_rows, bass.IndirectOffsetOnAxis(ap=back[:, e, s:s + 1], axis=0),
                                            e_out[:, e % 2, s, :], None, bounds_check=N - 1,
                                            oob_is_err=False).then_inc(returned[e % 2], 16)
            for p in range(2):
                pool.wait_ge(returned[p], 16 * ST * E8 // 2)

        @block.tensor
        def _(pe):
            pe.wait_ge(rd.loaded, 16 * rd.count)

            def turn(j):
                pe.wait_ge(y_ready, j + 1)
                if j >= 2:
                    pe.wait_ge(yT_copied, j - 1)
                for c in range(DC):
                    for q in range(2):
                        last = pe.transpose(ps_t[:, j % 2, (c * 2 + q) * P:(c * 2 + q + 1) * P],
                                            y[:, j % 2, q, c * P:(c + 1) * P], ident[:])
                last.then_inc(yT_ready, 1)

            def logits(j):
                pe.wait_ge(yT_copied, j + 1)
                b, t = j // BP, (j % BP) * 2
                for q in range(2):
                    for c in range(DC):
                        last = pe.matmul(ps_l[b % 2][:, t + q, :], yT[:, j % 2, c, q, :], wr[:, c, :],
                                         start=(c == 0), stop=(c == DC - 1))
                if j % BP == BP - 1:
                    last.then_inc(l_ready, 1)

            def counts(b):
                pe.wait_ge(oh_ready, b + 1)
                if b >= 2:
                    pe.wait_ge(put_ready, b - 1)
                flat = oh[:, b].rearrange("p t e -> p (t e)")
                pe.matmul(ps_c[b % 2][:, 0], upper[:], flat, start=True, stop=True)
                pe.matmul(ps_c[b % 2][:, 1], ones[:], flat, start=True, stop=True).then_inc(counted, 1)

            turn(0)
            for j in range(1, TILES // 2):
                turn(j)
                logits(j - 1)
                if j % BP == 2 and j > BP:
                    if j == BP + 2:
                        pe.wait_ge(ones_ready, 1)
                    counts(j // BP - 1)
            logits(TILES // 2 - 1)
            counts(NBATCH - 1)

            def transposes(e):
                pe.wait_ge(in_ready, e + 1)
                if e == 0:
                    pe.wait_ge(yT_copied, TILES // 2)
                else:
                    pe.wait_ge(t_copied, e)
                for k in range(DC):
                    for s in range(ST):
                        last = pe.transpose(ps_t[:, k, s * P:(s + 1) * P], e_in[:, e % 2, s, k * P:(k + 1) * P], ident[:])
                last.then_inc(t_ready, 1)

            transposes(0)
            for e in range(E8):
                p = e % 2
                pe.wait_ge(t_copied, e + 1)
                for f in range(DC):
                    if e:
                        pe.wait_ge(h_copied, (e - 1) * DC + f + 1)
                    for k in range(DC):
                        last = pe.matmul(ps_h[:, f, :], w1[:, e, k, f * P:(f + 1) * P], eT[:, p, k, :],
                                         start=(k == 0), stop=(k == DC - 1))
                    last.then_inc(h_ready, 1)
                if e < E8 - 1:
                    transposes(e + 1)
                pe.wait_ge(h_copied, (e + 1) * DC)
                if e == 0:
                    pe.wait_ge(put_ready, NBATCH)
                else:
                    pe.wait_ge(biased, e)
                for s in range(ST):
                    for f in range(DC):
                        last = pe.matmul(ps_e[:, s, :], hT[:, p, f, s * P:(s + 1) * P], w2[:, e, f, :],
                                         start=(f == 0), stop=(f == DC - 1))
                last.then_inc(e_ready, 1)

        @block.scalar
        def _(act):
            scale_act(act)
            act.wait_ge(rd.loaded, 16 * rd.count)

            def exps(b):
                act.wait_ge(d_ready, b + 1)
                act.activation(ex[:, b], d[:, b], ACT.Exp).then_inc(ex_ready, 1)

            for j in range(TILES // 2):
                act.wait_ge(yT_ready, j + 1)
                if j >= 2 and j % BP == 1:
                    act.wait_ge(l_ready, j // BP)
                act.activation(yT[:, j % 2], ps_t[:, j % 2].rearrange("p (c q t) -> p c q t", c=DC, q=2),
                               ACT.Copy).then_inc(yT_copied, 1)
                if j % BP == 2 and j > BP:
                    exps(j // BP - 1)
            exps(NBATCH - 1)

            def turned(e):
                act.wait_ge(t_ready, e + 1)
                act.activation(eT[:, e % 2], ps_t[:], ACT.Copy).then_inc(t_copied, 1)

            turned(0)
            for e in range(E8):
                if e >= 2:
                    act.wait_ge(e_ready, e - 1)
                for f in range(DC):
                    act.wait_ge(h_ready, e * DC + f + 1)
                    act.activation(hT[:, e % 2, f, :], ps_h[:, f, :], ACT.Relu, bias=b1[:, e, f:f + 1]).then_inc(h_copied, 1)
                if e < E8 - 1:
                    turned(e + 1)

        @block.vector
        def _(dve):
            n = [0]

            def settle(ins):
                n[0] += 1
                ins.then_inc(chain, 1)
                dve.wait_ge(chain, n[0])

            scale_dve(dve)
            dve.memset(ones[:], 1.0).then_inc(ones_ready, 1)
            dve.memset(within[:], 1.0).then_inc(ones_ready, 1)
            dve.wait_ge(ones_ready, 2)
            settle(dve.memset(within[:, :, 0:1], 0.0))
            dve.wait_ge(rd.loaded, 16 * rd.count)
            dve.tensor_copy(rows[:, :, MEAN], mv[:, :, 0])
            dve.tensor_copy(rows[:, :, NUMBER], number[:])

            def normalise(j):
                if j >= 2:
                    dve.wait_ge(yT_ready, j - 1)
                for q in range(2):
                    i = 2 * j + q
                    last = dve.tensor_scalar(y[:, j % 2, q, :], rows[:, i, 0:D], mv[:, i, 0:1], scale[:, i:i + 1],
                                             ALU.subtract, ALU.mult)
                last.then_inc(y_ready, 1)

            def choose(b):
                at = slice(b * BATCH, (b + 1) * BATCH)
                iota_b = iota[:].unsqueeze(1).broadcast_to(BE)
                dve.wait_ge(l_ready, b + 1)
                settle(dve.tensor_tensor(lg[:, b], ps_l[b % 2], br[:].unsqueeze(1).broadcast_to(BE), ALU.add))
                settle(dve.tensor_reduce(mx[:, at], lg[:, b], AX.X, ALU.max))
                dve.tensor_tensor(d[:, b], lg[:, b], mx[:, at].unsqueeze(2).broadcast_to(BE), ALU.subtract).then_inc(d_ready, 1)
                dve.wait_ge(d_ready, b + 1)
                settle(dve.scalar_tensor_tensor(eq[:, b], d[:, b], 0.0, iota_b, ALU.is_equal, ALU.mult))
                settle(dve.tensor_reduce(first[:, at], eq[:, b], AX.X, ALU.min))
                dve.tensor_tensor(oh[:, b], first[:, at].unsqueeze(2).broadcast_to(BE), iota_b, ALU.is_equal).then_inc(oh_ready, 1)

            def place(b):
                at = slice(b * BATCH, (b + 1) * BATCH)
                dve.wait_ge(ex_ready, b + 1)
                dve.tensor_reduce(se[:, at], ex[:, b], AX.X, ALU.add)
                dve.wait_ge(counted, b + 1)
                settle(dve.tensor_copy(tot[:, b], ps_c[b % 2][:, 1].rearrange("p (t e) -> p e t", e=E8)))
                dve.reciprocal(gate[:, at], se[:, at])
                if b:
                    settle(dve.tensor_tensor(pos[:, b, :, 0], tot[:, b, :, 0], inc[:, b - 1, :, BATCH - 1], ALU.add))
                    settle(dve.tensor_copy(tot[:, b, :, 0], pos[:, b, :, 0]))
                settle(dve.tensor_tensor_scan(inc[:, b].rearrange("p e t -> p (e t)"), within[:].rearrange("p e t -> p (e t)"),
                                              tot[:, b].rearrange("p e t -> p (e t)"), 0.0, ALU.mult, ALU.add))
                settle(dve.tensor_tensor(pos[:, b], inc[:, b], ps_c[b % 2][:, 1].rearrange("p (t e) -> p e t", e=E8), ALU.subtract))
                settle(dve.tensor_tensor(pos[:, b], pos[:, b], ps_c[b % 2][:, 0].rearrange("p (t e) -> p e t", e=E8), ALU.add))
                settle(dve.tensor_tensor(pos[:, b], pos[:, b], oh[:, b].rearrange("p t e -> p e t"), ALU.mult))
                dve.tensor_tensor(rows[:, at, FACTOR], scale[:, at], gate[:, at], ALU.mult)
                dve.tensor_copy(rows[:, at, GATE], gate[:, at])
                settle(dve.tensor_reduce(rank[:, at], pos[:, b].rearrange("p e t -> p t e"), AX.X, ALU.add))
                settle(dve.tensor_scalar(keep[:, at], rank[:, at], float(CAP), float(NOBODY), ALU.is_ge, ALU.mult))
                settle(dve.tensor_tensor(rank[:, at], rank[:, at], keep[:, at], ALU.add))
                settle(dve.tensor_scalar(slot[:, at], first[:, at], float(E8), float(CAP), ALU.add, ALU.mult))
                settle(dve.tensor_tensor(slot[:, at], slot[:, at], rank[:, at], ALU.add))
                dve.tensor_copy(put[:, at], slot[:, at]).then_inc(put_ready, 1)

            for j in range(TILES // 2):
                normalise(j)
                if j >= BP and j % BP == 1:
                    choose(j // BP - 1)
                if j >= BP and j % BP == 3:
                    place(j // BP - 1)
            choose(NBATCH - 1)
            place(NBATCH - 1)

            def enter(e):
                dve.wait_ge(taken_loaded[e], 16)
                if e >= 2:
                    dve.wait_ge(t_ready, e - 1)
                for s in range(ST):
                    last = dve.tensor_scalar(e_in[:, e % 2, s, :], taken[:, e, s, 0:D], taken[:, e, s, MEAN:MEAN + 1],
                                             taken[:, e, s, FACTOR:FACTOR + 1], ALU.subtract, ALU.mult)
                last.then_inc(in_ready, 1)
                dve.tensor_copy(back[:, e], taken[:, e, :, NUMBER])

            enter(0)
            enter(1)
            for e in range(E8):
                p = e % 2
                dve.wait_ge(e_ready, e + 1)
                if e >= 2:
                    dve.wait_ge(returned[p], 16 * ST * (e // 2))
                dve.tensor_tensor(e_out[:, p], ps_e[:], b2[:, e].unsqueeze(1).broadcast_to([P, ST, D]), ALU.add).then_inc(biased, 1)
                dve.wait_ge(biased, e + 1)
                for s in range(ST):
                    dve.scalar_tensor_tensor(e_out[:, p, s, :], e_out[:, p, s, :], taken[:, e, s, GATE:GATE + 1],
                                             taken[:, e, s, 0:D], ALU.mult, ALU.add).then_inc(e_done, 1)
                if e + 2 < E8:
                    enter(e + 2)


def program(nc, x, ctxT, mask, a0, a1, pk, me, c, out):
    def rows(name):
        return nc.dram_tensor(name, [TILES, P, D], F32).ap()

    x1, x2 = rows("x1"), rows("x2")
    slots_d = nc.dram_tensor("slots_d", [E8 * CAP, ROW], F32).ap()
    with ExitStack() as ctx:
        mv = ctx.enter_context(nc.sbuf_tensor("mv", [P, TILES, 2], F32))
        with ExitStack() as first_half:
            pb = ProductKeys(nc, first_half)
            attention(nc, "a0", x, x1, mv[:], ctxT, *a0, c["bmask"], c["ident"], also=pb.loads(pk), fresh=True)
            product_key_experts(nc, x1, x2, mv[:], pb, pk["up"], c["ident"], c["identh"], c["iota8"], c["iota"])
        rd = Routed(nc, ctx)
        attention(nc, "a1", x2, out, mv[:], ctxT, *a1[:4], c["bmask"], c["ident"],
                  rope=(a1[4], c["cos_k"], c["sin_k"], c["cos_q"], c["sin_q"]), mask=mask, identb_d=c["identb"], keep=rd.rows,
                  also=rd.loads(me, slots_d))
        routed_experts(nc, out, mv[:], slots_d, rd)


def layouts(np, a):
    def rowchunks(w):
        return w.reshape(DC, P, -1).transpose(1, 0, 2)

    def halves_exchanged(w):
        return w.reshape(H, 2, DK // 2, D)[:, ::-1].reshape(D, D)

    L0, L1 = "L0_xattn_W_", "L1_xattn_W_"
    return {
        "x": a["x"].reshape(TILES, P, D),
        "ctxT": rowchunks(a["ctx_1024"].transpose(2, 0, 1).reshape(D, B * SK)),
        "mask": a["mask_Bx1xSxS2_ik0"].reshape(TILES, P, SK),
        **{f"a0_{n}": rowchunks(a[L0 + n].T) for n in "qkvo"},
        **{f"a1_{n}": rowchunks(a[L1 + n].T) for n in "qkvo"},
        "a1_kr": rowchunks(halves_exchanged(a[L1 + "k"]).T),
        "w_q": a["L0_ffn_w_q"].reshape(2 * PH, P, D).transpose(1, 0, 2),
        "keysT": a["L0_ffn_keys"].transpose(3, 0, 2, 1).reshape(P, 2 * PH, NKEYS),
        "norm_w": a["L0_ffn_norm_w"].reshape(DC, P).T,
        "down": a["L0_ffn_expert_down"].reshape(P, NF, DC, P).transpose(3, 2, 1, 0),
        "up": a["L0_ffn_expert_up"].reshape(P, NF, D),
        "wr": rowchunks(a["L1_ffn_Wr"]),
        "br": np.broadcast_to(a["L1_ffn_br"][None], (P, E8)),
        "w1": a["L1_ffn_W1"].reshape(E8, DC, P, D).transpose(2, 0, 1, 3),
        "b1": a["L1_ffn_b1"].reshape(E8, DC, P).transpose(2, 0, 1),
        "w2": a["L1_ffn_W2"].reshape(E8, DC, P, D).transpose(2, 0, 1, 3),
        "b2": np.broadcast_to(a["L1_ffn_b2"][None], (P, E8, D)),
    }


def constants(np, bf16):
    inv = (1.0 / 10000.0 ** (np.arange(0, DK, 2, dtype=np.float32) / DK)).astype(np.float32)
    angle = np.outer(inv, np.arange(S, dtype=np.float32)).astype(np.float32)
    cos, sin = np.cos(angle), np.sin(angle)
    eye = np.eye(P, dtype=np.float32)
    return {
        "bmask": np.repeat(np.eye(HU, dtype=np.float32), DK, axis=0),
        "ident": eye,
        "identb": eye.astype(bf16),
        "identh": eye.astype(np.float16),
        "iota8": np.broadcast_to(np.arange(TOPK, dtype=np.float32)[None, :, None], (P, TOPK, TOPK)).astype(bf16),
        "iota": np.broadcast_to(np.arange(P, dtype=np.float32)[None, :, None], (P, P, TG)).astype(np.float16),
        "iota_e": np.broadcast_to(np.arange(E8, dtype=np.float32)[None] - E8, (P, E8)),
        "number": np.arange(N, dtype=np.float32).reshape(TILES, P).T,
        "blank": np.array([[0.0] * (ROW - 1) + [NOBODY]], np.float32),
        "upper": np.triu(np.ones((P, P), np.float32)),
        "cos_k": np.tile(np.concatenate([cos, cos])[:, :SK], (HU, 1)),
        "sin_k": np.tile(np.concatenate([-sin, sin])[:, :SK], (HU, 1)),
        "cos_q": cos.reshape(DK // 2, TPB, P).transpose(2, 1, 0),
        "sin_q": np.stack([-sin, sin]).reshape(2, DK // 2, TPB, P).transpose(3, 2, 0, 1),
    }


def kernel(**inputs):
    import ml_dtypes
    import numpy as np
    import concourse.bacc as bacc
    from concourse.bass_utils import run_bass_kernel_spmd as run

    a = layouts(np, {k: np.asarray(v) for k, v in inputs.items()})
    c = constants(np, ml_dtypes.bfloat16)
    nc = bacc.Bacc("TRN2", target_bir_lowering=False, num_devices=1)
    arrays, aps = {}, {}
    for name, v in {**a, **c}.items():
        v = np.ascontiguousarray(v)
        arrays[f"in_{name}"] = v
        aps[name] = nc.dram_tensor(f"in_{name}", v.shape, mybir.dt.from_np(v.dtype), kind="ExternalInput").ap()
    out = nc.dram_tensor("out", [TILES, P, D], F32, kind="ExternalOutput").ap()
    program(nc, aps["x"], aps["ctxT"], aps["mask"],
            [aps[f"a0_{n}"] for n in "qkvo"],
            [aps[f"a1_{n}"] for n in "qkvo"] + [aps["a1_kr"]],
            aps, aps, aps, out)
    r = run(nc, [arrays], core_ids=[0])
    return r.results[0]["out"].reshape(B, S, D)
```
